# Optimizing a Trainium2 kernel written in Bass

```python
import numpy as np
import jax
import jax.numpy as jnp

def _softmax(x, axis=-1):
    return jax.nn.softmax(x, axis=axis)

def _gelu(x):
    return jax.nn.gelu(x, approximate=True)

def _silu(x):
    return jax.nn.silu(x)

def _sigmoid(x):
    return jax.nn.sigmoid(x)

def _layernorm(x, axis=-1, eps=1e-05):
    m = jnp.mean(x, axis=axis, keepdims=True)
    v = jnp.var(x, axis=axis, keepdims=True)
    return (x - m) / jnp.sqrt(v + eps)

def _scatter_add(tgt, idx, src, axis=0):
    return tgt.at[idx].add(src)

def _segment_sum(src, seg, n):
    return jax.ops.segment_sum(src, seg, n)
kernel_name = 'mk_perceiver_d2_seqx_r8_5c90c6'

def setup_inputs(seed: int=0):
    np.random.seed(seed)
    _w = jnp.asarray

    def _rec_inputs():
        import jax
        import jax.numpy as jnp
        _rk = jax.random.key(seed)
        x = -0.0002928 + 1 * jax.random.normal(jax.random.fold_in(_rk, 1), (64, 32, 128), jnp.float32)
        _lenS = 32 - jax.random.randint(jax.random.fold_in(_rk, 7), (64,), 0, max(1, 32 // 4) + 1, jnp.int32)
        _lenS2 = 257 - jax.random.randint(jax.random.fold_in(_rk, 8), (64,), 0, max(1, 257 // 4) + 1, jnp.int32)
        _ctx_1024P = jax.random.normal(jax.random.fold_in(_rk, 11), (64, 16, 128), jnp.float32)
        _ctx_1024c = jax.random.dirichlet(jax.random.fold_in(_rk, 511), 0.3 * jnp.ones((16,), jnp.float32), (64, 257))
        _ctx_1024t = jnp.einsum('bsk,bkd->bsd', _ctx_1024c, _ctx_1024P)
        _ctx_1024t = _ctx_1024t * jax.lax.rsqrt(jnp.mean(jnp.square(_ctx_1024t)) + 1e-12) * 0.953939
        ctx_1024 = -1.39393e-06 + 0.999914 * (_ctx_1024t + 0.3 * jax.random.normal(jax.random.fold_in(_rk, 611), (64, 257, 128), jnp.float32))
        _validS = jnp.arange(32)[None, :] < _lenS[:, None]
        _validS2 = jnp.arange(257)[None, :] < _lenS2[:, None]
        _causal = jnp.tril(jnp.ones((32, 32), dtype=bool))
        mask_Bx1x1xS2_ff0 = jnp.where(jnp.ones((64, 1, 1, 257), dtype=bool), 0.0, -1000000000.0).astype(jnp.float32)
        return (x, ctx_1024, mask_Bx1x1xS2_ff0)
    x, ctx_1024, mask_Bx1x1xS2_ff0 = _rec_inputs()

    def _L0_xattn_setup():
        import jax, jax.numpy as jnp
        import numpy as np
        import math
        D_MODEL = 128
        N_HEADS = 16
        D_HEAD = D_MODEL // N_HEADS
        key = jax.random.key(seed)
        ks = jax.random.split(key, 11)
        N, L, S = (2, 256, 256)
        inp = {'queries': jax.random.normal(ks[0], (N, L, D_MODEL), dtype=jnp.float32), 'keys': jax.random.normal(ks[1], (N, S, D_MODEL), dtype=jnp.float32), 'values': jax.random.normal(ks[2], (N, S, D_MODEL), dtype=jnp.float32), 'Wq': jax.random.normal(ks[3], (D_MODEL, N_HEADS * D_HEAD), dtype=jnp.float32) / math.sqrt(D_MODEL), 'bq': jnp.zeros((N_HEADS * D_HEAD,), dtype=jnp.float32), 'Wk': jax.random.normal(ks[4], (D_MODEL, N_HEADS * D_HEAD), dtype=jnp.float32) / math.sqrt(D_MODEL), 'bk': jnp.zeros((N_HEADS * D_HEAD,), dtype=jnp.float32), 'Wv': jax.random.normal(ks[5], (D_MODEL, N_HEADS * D_HEAD), dtype=jnp.float32) / math.sqrt(D_MODEL), 'bv': jnp.zeros((N_HEADS * D_HEAD,), dtype=jnp.float32), 'Wo': jax.random.normal(ks[6], (N_HEADS * D_HEAD, D_MODEL), dtype=jnp.float32) / math.sqrt(N_HEADS * D_HEAD), 'bo': jnp.zeros((D_MODEL,), dtype=jnp.float32)}
        return inp
    _L0_xattn_all = _L0_xattn_setup()
    _L0_xattn_in = {k: v for k, v in _L0_xattn_all.items() if k in ('Wq', 'bq', 'Wk', 'bk', 'Wv', 'bv', 'Wo', 'bo')}
    del _L0_xattn_all

    def _L0_attn_setup():
        import jax, jax.numpy as jnp
        import numpy as np
        key = jax.random.key(seed)
        k1, k2, k3, k4, k5 = jax.random.split(key, 5)
        B, L, D = (4, 512, 128)
        return {'x': jax.random.normal(k1, (B, L, D), dtype=jnp.float32), 'phazor': jax.random.normal(k2, (D, 2), dtype=jnp.float32), 'phazor_init': jax.random.normal(k3, (D, 2), dtype=jnp.float32), 'last_conv_re': jax.random.normal(k4, (D,), dtype=jnp.float32), 'last_conv_im': jax.random.normal(k5, (D,), dtype=jnp.float32)}
    _L0_attn_all = _L0_attn_setup()
    _L0_attn_in = {k: v for k, v in _L0_attn_all.items() if k in ('phazor', 'phazor_init', 'last_conv_re', 'last_conv_im')}
    del _L0_attn_all

    def _L0_ffn_setup():
        import jax, jax.numpy as jnp
        import numpy as np
        B, S, D, H, E = (8, 256, 128, 512, 16)
        key = jax.random.key(seed)
        ks = jax.random.split(key, 4)
        sd = 1.0 / np.sqrt(D).astype(np.float32)
        sh = 1.0 / np.sqrt(H).astype(np.float32)
        return {'x': jax.random.normal(ks[0], (B, S, D), jnp.float32), 'Wg': jax.random.normal(ks[1], (D, E), jnp.float32) * sd, 'bg': jnp.zeros((E,), jnp.float32), 'W1': jax.random.normal(ks[2], (E, D, H), jnp.float32) * sd, 'b1': jnp.zeros((E, H), jnp.float32), 'W2': jax.random.normal(ks[3], (E, H, D), jnp.float32) * sh, 'b2': jnp.zeros((E, D), jnp.float32)}
    _L0_ffn_all = _L0_ffn_setup()
    _L0_ffn_in = {k: v for k, v in _L0_ffn_all.items() if k in ('Wg', 'bg', 'W1', 'b1', 'W2', 'b2')}
    del _L0_ffn_all

    def _L1_xattn_setup():
        import jax, jax.numpy as jnp
        from jax import lax
        import numpy as np
        B, SQ, SK, H, NH, KS = (2, 256, 256, 128, 16, 3)
        D = H // NH

        def _conv1d_same(x, W, b):
            y = lax.conv_general_dilated(x, W, window_strides=(1,), padding='SAME', dimension_numbers=('NWC', 'WIO', 'NWC'))
            return y + b

        def _split_heads(x):
            b, s, _ = x.shape
            return x.reshape(b, s, NH, D).transpose(0, 2, 1, 3)
        key = jax.random.key(seed)
        ks = jax.random.split(key, 10)
        s = 0.02
        return {'query_input': jax.random.normal(ks[0], (B, SQ, H), jnp.float32), 'source_input': jax.random.normal(ks[1], (B, SK, H), jnp.float32), 'mask': jnp.zeros((B, 1, 1, SK), jnp.float32), 'Wq': jax.random.normal(ks[2], (KS, H, H), jnp.float32) * s, 'bq': jnp.zeros((H,), jnp.float32), 'Wk': jax.random.normal(ks[3], (KS, H, H), jnp.float32) * s, 'bk': jnp.zeros((H,), jnp.float32), 'Wv': jax.random.normal(ks[4], (KS, H, H), jnp.float32) * s, 'bv': jnp.zeros((H,), jnp.float32), 'Wo': jax.random.normal(ks[5], (H, H), jnp.float32) * s, 'bo': jnp.zeros((H,), jnp.float32)}
    _L1_xattn_all = _L1_xattn_setup()
    _L1_xattn_in = {k: v for k, v in _L1_xattn_all.items() if k in ('Wq', 'bq', 'Wk', 'bk', 'Wv', 'bv', 'Wo', 'bo')}
    del _L1_xattn_all

    def _L1_attn_setup():
        import jax, jax.numpy as jnp
        import numpy as np
        D_MODEL = 128
        NUM_HEADS = 16
        D_K = D_MODEL // NUM_HEADS
        ROPE_BASE = 10000.0

        def _rotate_half(x):
            x1 = x[..., ::2]
            x2 = x[..., 1::2]
            return jnp.stack((-x2, x1), axis=-1).reshape(x.shape)

        def _rope(q, k):
            seq_len = q.shape[-2]
            freqs = ROPE_BASE ** (jnp.arange(0, D_K, 2, dtype=q.dtype) / D_K)
            angles = jnp.arange(seq_len, dtype=q.dtype)[:, None] / freqs[None, :]
            sin = jnp.repeat(jnp.sin(angles), 2, axis=-1)[None, None]
            cos = jnp.repeat(jnp.cos(angles), 2, axis=-1)[None, None]
            return (q * cos + _rotate_half(q) * sin, k * cos + _rotate_half(k) * sin)
        key = jax.random.key(seed)
        ks = jax.random.split(key, 9)
        B, S, D = (2, 256, D_MODEL)
        s = 1.0 / np.sqrt(D)
        inp = {'x': jax.random.normal(ks[0], (B, S, D), dtype=jnp.float32), 'wq': jax.random.uniform(ks[1], (D, D), jnp.float32, -s, s), 'bq': jax.random.uniform(ks[2], (D,), jnp.float32, -s, s), 'wk': jax.random.uniform(ks[3], (D, D), jnp.float32, -s, s), 'bk': jax.random.uniform(ks[4], (D,), jnp.float32, -s, s), 'wv': jax.random.uniform(ks[5], (D, D), jnp.float32, -s, s), 'bv': jax.random.uniform(ks[6], (D,), jnp.float32, -s, s), 'wo': jax.random.uniform(ks[7], (D, D), jnp.float32, -s, s), 'bo': jax.random.uniform(ks[8], (D,), jnp.float32, -s, s)}
        return inp
    _L1_attn_all = _L1_attn_setup()
    _L1_attn_in = {k: v for k, v in _L1_attn_all.items() if k in ('wq', 'bq', 'wk', 'bk', 'wv', 'bv', 'wo', 'bo')}
    del _L1_attn_all

    def _L1_ffn_setup():
        import jax, jax.numpy as jnp
        import numpy as np
        B, S, D = (2, 256, 128)
        H, E, P, K = (8, 8, 128, 2)
        SCALE = 1.0 / np.sqrt(P)

        def _get_sel_gate(x, w, route_scale):
            logits = jnp.einsum('bsd,ed->bse', x, w).astype(jnp.float32)
            raw = logits.reshape(x.shape[0], x.shape[1], H, E)
            probs = jax.nn.sigmoid(raw)
            vals, idx = jax.lax.top_k(probs, K)
            vals = vals / jnp.clip(vals.sum(-1, keepdims=True), 1e-09)
            vals = vals * route_scale
            gate = (jax.nn.one_hot(idx, E, dtype=vals.dtype) * vals[..., None]).sum(-2)
            return gate
        key = jax.random.key(seed)
        ks = jax.random.split(key, 8)
        std = 1.0 / np.sqrt(D)
        return {'x': jax.random.normal(ks[0], (B, S, D), jnp.float32), 'q_w': jax.random.normal(ks[1], (H * P, D), jnp.float32) * std, 'k_w': jax.random.normal(ks[2], (H * P, D), jnp.float32) * std, 'v_w': jax.random.normal(ks[3], (H * E, D, P), jnp.float32) * std, 'o_w': jax.random.normal(ks[4], (H * E, P, D), jnp.float32) * (1.0 / np.sqrt(H * P)), 'sel_v_w': jax.random.normal(ks[5], (H * E, D), jnp.float32) * std, 'sel_o_w': jax.random.normal(ks[6], (H * E, D), jnp.float32) * std, 'route_scale': jnp.ones((1,), jnp.float32)}
    _L1_ffn_all = _L1_ffn_setup()
    _L1_ffn_in = {k: v for k, v in _L1_ffn_all.items() if k in ('q_w', 'k_w', 'v_w', 'o_w', 'sel_v_w', 'sel_o_w', 'route_scale')}
    del _L1_ffn_all
    return {'x': x, 'ctx_1024': ctx_1024, 'mask_Bx1x1xS2_ff0': mask_Bx1x1xS2_ff0, 'L0_xattn_Wq': _L0_xattn_in['Wq'], 'L0_xattn_bq': _L0_xattn_in['bq'], 'L0_xattn_Wk': _L0_xattn_in['Wk'], 'L0_xattn_bk': _L0_xattn_in['bk'], 'L0_xattn_Wv': _L0_xattn_in['Wv'], 'L0_xattn_bv': _L0_xattn_in['bv'], 'L0_xattn_Wo': _L0_xattn_in['Wo'], 'L0_xattn_bo': _L0_xattn_in['bo'], 'L0_attn_phazor': _L0_attn_in['phazor'], 'L0_attn_phazor_init': _L0_attn_in['phazor_init'], 'L0_attn_last_conv_re': _L0_attn_in['last_conv_re'], 'L0_attn_last_conv_im': _L0_attn_in['last_conv_im'], 'L0_ffn_Wg': _L0_ffn_in['Wg'], 'L0_ffn_bg': _L0_ffn_in['bg'], 'L0_ffn_W1': _L0_ffn_in['W1'], 'L0_ffn_b1': _L0_ffn_in['b1'], 'L0_ffn_W2': _L0_ffn_in['W2'], 'L0_ffn_b2': _L0_ffn_in['b2'], 'L1_xattn_Wq': _L1_xattn_in['Wq'], 'L1_xattn_bq': _L1_xattn_in['bq'], 'L1_xattn_Wk': _L1_xattn_in['Wk'], 'L1_xattn_bk': _L1_xattn_in['bk'], 'L1_xattn_Wv': _L1_xattn_in['Wv'], 'L1_xattn_bv': _L1_xattn_in['bv'], 'L1_xattn_Wo': _L1_xattn_in['Wo'], 'L1_xattn_bo': _L1_xattn_in['bo'], 'L1_attn_wq': _L1_attn_in['wq'], 'L1_attn_bq': _L1_attn_in['bq'], 'L1_attn_wk': _L1_attn_in['wk'], 'L1_attn_bk': _L1_attn_in['bk'], 'L1_attn_wv': _L1_attn_in['wv'], 'L1_attn_bv': _L1_attn_in['bv'], 'L1_attn_wo': _L1_attn_in['wo'], 'L1_attn_bo': _L1_attn_in['bo'], 'L1_ffn_q_w': _L1_ffn_in['q_w'], 'L1_ffn_k_w': _L1_ffn_in['k_w'], 'L1_ffn_v_w': _L1_ffn_in['v_w'], 'L1_ffn_o_w': _L1_ffn_in['o_w'], 'L1_ffn_sel_v_w': _L1_ffn_in['sel_v_w'], 'L1_ffn_sel_o_w': _L1_ffn_in['sel_o_w'], 'L1_ffn_route_scale': _L1_ffn_in['route_scale']}

def reference(x, ctx_1024, mask_Bx1x1xS2_ff0, L0_xattn_Wq, L0_xattn_bq, L0_xattn_Wk, L0_xattn_bk, L0_xattn_Wv, L0_xattn_bv, L0_xattn_Wo, L0_xattn_bo, L0_attn_phazor, L0_attn_phazor_init, L0_attn_last_conv_re, L0_attn_last_conv_im, L0_ffn_Wg, L0_ffn_bg, L0_ffn_W1, L0_ffn_b1, L0_ffn_W2, L0_ffn_b2, L1_xattn_Wq, L1_xattn_bq, L1_xattn_Wk, L1_xattn_bk, L1_xattn_Wv, L1_xattn_bv, L1_xattn_Wo, L1_xattn_bo, L1_attn_wq, L1_attn_bq, L1_attn_wk, L1_attn_bk, L1_attn_wv, L1_attn_bv, L1_attn_wo, L1_attn_bo, L1_ffn_q_w, L1_ffn_k_w, L1_ffn_v_w, L1_ffn_o_w, L1_ffn_sel_v_w, L1_ffn_sel_o_w, L1_ffn_route_scale):
    import jax
    import jax.numpy as jnp

    def _L0_xattn_ref(queries, keys, values, Wq, bq, Wk, bk, Wv, bv, Wo, bo):
        import jax, jax.numpy as jnp
        import numpy as np
        import math
        D_MODEL = 128
        N_HEADS = 16
        D_HEAD = D_MODEL // N_HEADS
        N, L, _ = queries.shape
        S = keys.shape[1]
        H, D = (N_HEADS, D_HEAD)
        q = (queries @ Wq + bq).reshape(N, L, H, D)
        k = (keys @ Wk + bk).reshape(N, S, H, D)
        v = (values @ Wv + bv).reshape(N, S, H, D)
        sm = jnp.einsum('nlhd,nshd->nlhs', q, k) / math.sqrt(D)
        sm = jax.nn.softmax(sm, axis=1)
        attn = jnp.einsum('nlhs,nshd->nlhd', sm, v).reshape(N, L, H * D)
        return attn @ Wo + bo

    def _L0_attn_ref(x, phazor, phazor_init, last_conv_re, last_conv_im):
        import jax, jax.numpy as jnp
        import numpy as np
        B, L, D = x.shape
        in_dtype = x.dtype
        x = x.astype(jnp.float32)
        ph = jax.lax.complex(phazor[:, 0], phazor[:, 1])
        ph_init = jax.lax.complex(phazor_init[:, 0], phazor_init[:, 1])
        last_conv = jax.lax.complex(last_conv_re, last_conv_im)
        mag = jnp.abs(ph)
        ph = ph / mag * jnp.exp(-mag)
        t = jnp.arange(L)[:, None]
        prog = ph[None, :] ** t
        filt = prog * ph_init[None, :]
        filt_fft = jnp.fft.fft(filt, n=2 * L, axis=0)
        x_fft = jnp.fft.fft(x, n=2 * L, axis=1)
        conv = jnp.fft.ifft(filt_fft[None, :, :] * x_fft, axis=1)[:, :L, :]
        conv_with_past = conv + last_conv[None, None, :] * prog[None, :, :] * ph[None, None, :]
        return conv_with_past.real.astype(in_dtype)

    def _L0_ffn_ref(x, Wg, bg, W1, b1, W2, b2):
        import jax, jax.numpy as jnp
        import numpy as np
        B, S, D, H, E = (8, 256, 128, 512, 16)
        d = x.shape[-1]
        xf = x.reshape(-1, d)
        n_tok = xf.shape[0]
        n_exp = Wg.shape[1]
        cap = -(-n_tok // n_exp)
        score = jax.nn.softmax(xf @ Wg + bg, axis=-1)
        gate = jnp.max(score, axis=-1)
        idx = jnp.argmax(score, axis=-1)
        onehot = jax.nn.one_hot(idx, n_exp, dtype=jnp.int32)
        pos = jnp.sum((jnp.cumsum(onehot, axis=0) - 1) * onehot, axis=-1)
        keep = pos < cap
        safe_pos = jnp.where(keep, pos, cap - 1)
        buf = jnp.zeros((n_exp, cap, d), x.dtype).at[idx, safe_pos].add(jnp.where(keep[:, None], xf, 0.0))
        h = jax.nn.relu(jnp.einsum('ecd,edh->ech', buf, W1) + b1[:, None, :])
        y = jnp.einsum('ech,ehd->ecd', h, W2) + b2[:, None, :]
        out = y[idx, safe_pos] * gate[:, None]
        out = jnp.where(keep[:, None], out, 0.0)
        return out.reshape(x.shape)

    def _L1_xattn_ref(query_input, source_input, mask, Wq, bq, Wk, bk, Wv, bv, Wo, bo):
        import jax, jax.numpy as jnp
        from jax import lax
        import numpy as np
        B, SQ, SK, H, NH, KS = (2, 256, 256, 128, 16, 3)
        D = H // NH

        def _conv1d_same(x, W, b):
            y = lax.conv_general_dilated(x, W, window_strides=(1,), padding='SAME', dimension_numbers=('NWC', 'WIO', 'NWC'))
            return y + b

        def _split_heads(x):
            b, s, _ = x.shape
            return x.reshape(b, s, NH, D).transpose(0, 2, 1, 3)
        q = _split_heads(_conv1d_same(query_input, Wq, bq)) * D ** (-0.5)
        k = _split_heads(_conv1d_same(source_input, Wk, bk))
        v = _split_heads(_conv1d_same(source_input, Wv, bv))
        logits = jnp.einsum('bhqd,bhkd->bhqk', q, k) + mask * -1000000000.0
        weights = jax.nn.softmax(logits, axis=-1)
        attn = jnp.einsum('bhqk,bhkd->bhqd', weights, v)
        attn = attn.transpose(0, 2, 1, 3).reshape(q.shape[0], -1, H)
        return attn @ Wo + bo

    def _L1_attn_ref(x, wq, bq, wk, bk, wv, bv, wo, bo):
        import jax, jax.numpy as jnp
        import numpy as np
        D_MODEL = 128
        NUM_HEADS = 16
        D_K = D_MODEL // NUM_HEADS
        ROPE_BASE = 10000.0

        def _rotate_half(x):
            x1 = x[..., ::2]
            x2 = x[..., 1::2]
            return jnp.stack((-x2, x1), axis=-1).reshape(x.shape)

        def _rope(q, k):
            seq_len = q.shape[-2]
            freqs = ROPE_BASE ** (jnp.arange(0, D_K, 2, dtype=q.dtype) / D_K)
            angles = jnp.arange(seq_len, dtype=q.dtype)[:, None] / freqs[None, :]
            sin = jnp.repeat(jnp.sin(angles), 2, axis=-1)[None, None]
            cos = jnp.repeat(jnp.cos(angles), 2, axis=-1)[None, None]
            return (q * cos + _rotate_half(q) * sin, k * cos + _rotate_half(k) * sin)
        B, S, D = x.shape
        H, dk = (NUM_HEADS, D_K)
        Q = (x @ wq.T + bq).reshape(B, S, H, dk).transpose(0, 2, 1, 3)
        K = (x @ wk.T + bk).reshape(B, S, H, dk).transpose(0, 2, 1, 3)
        V = (x @ wv.T + bv).reshape(B, S, H, dk).transpose(0, 2, 1, 3)
        Q, K = _rope(Q, K)
        score = jnp.einsum('bhqd,bhkd->bhqk', Q, K) / jnp.sqrt(jnp.asarray(dk, x.dtype))
        attn_w = jax.nn.softmax(score, axis=-1)
        out = jnp.einsum('bhqk,bhkd->bhqd', attn_w, V)
        out = out.transpose(0, 2, 1, 3).reshape(B, S, D)
        return out @ wo.T + bo

    def _L1_ffn_ref(x, q_w, k_w, v_w, o_w, sel_v_w, sel_o_w, route_scale):
        import jax, jax.numpy as jnp
        import numpy as np
        B, S, D = (2, 256, 128)
        H, E, P, K = (8, 8, 128, 2)
        SCALE = 1.0 / np.sqrt(P)

        def _get_sel_gate(x, w, route_scale):
            logits = jnp.einsum('bsd,ed->bse', x, w).astype(jnp.float32)
            raw = logits.reshape(x.shape[0], x.shape[1], H, E)
            probs = jax.nn.sigmoid(raw)
            vals, idx = jax.lax.top_k(probs, K)
            vals = vals / jnp.clip(vals.sum(-1, keepdims=True), 1e-09)
            vals = vals * route_scale
            gate = (jax.nn.one_hot(idx, E, dtype=vals.dtype) * vals[..., None]).sum(-2)
            return gate
        rs = route_scale[0]
        gate_v = _get_sel_gate(x, sel_v_w, rs)
        gate_o = _get_sel_gate(x, sel_o_w, rs)
        q = jnp.einsum('bsd,hpd->bhsp', x, q_w.reshape(H, P, D))
        k = jnp.einsum('bsd,hpd->bhsp', x, k_w.reshape(H, P, D))
        xv = jnp.einsum('bsd,hedp->bshep', x, v_w.reshape(H, E, D, P))
        v = jnp.einsum('bshep,bshe->bhsp', xv, gate_v)
        att = jax.nn.softmax(jnp.einsum('bhqp,bhkp->bhqk', q, k) * SCALE, axis=-1)
        ctx = jnp.einsum('bhqk,bhkp->bqhp', att, v)
        weighted = ctx[:, :, :, None, :] * gate_o[..., None]
        out = jnp.einsum('bshep,hepd->bsd', weighted, o_w.reshape(H, E, P, D))
        return out
    x = x + _L0_xattn_ref(_layernorm(x, axis=-1), ctx_1024, ctx_1024, L0_xattn_Wq, L0_xattn_bq, L0_xattn_Wk, L0_xattn_bk, L0_xattn_Wv, L0_xattn_bv, L0_xattn_Wo, L0_xattn_bo)
    x = x + _L0_attn_ref(_layernorm(x, axis=-1), L0_attn_phazor, L0_attn_phazor_init, L0_attn_last_conv_re, L0_attn_last_conv_im)
    x = x + _L0_ffn_ref(_layernorm(x, axis=-1), L0_ffn_Wg, L0_ffn_bg, L0_ffn_W1, L0_ffn_b1, L0_ffn_W2, L0_ffn_b2)
    x = x + _L1_xattn_ref(_layernorm(x, axis=-1), ctx_1024, mask_Bx1x1xS2_ff0, L1_xattn_Wq, L1_xattn_bq, L1_xattn_Wk, L1_xattn_bk, L1_xattn_Wv, L1_xattn_bv, L1_xattn_Wo, L1_xattn_bo)
    x = x + _L1_attn_ref(_layernorm(x, axis=-1), L1_attn_wq, L1_attn_bq, L1_attn_wk, L1_attn_bk, L1_attn_wv, L1_attn_bv, L1_attn_wo, L1_attn_bo)
    x = x + _L1_ffn_ref(_layernorm(x, axis=-1), L1_ffn_q_w, L1_ffn_k_w, L1_ffn_v_w, L1_ffn_o_w, L1_ffn_sel_v_w, L1_ffn_sel_o_w, L1_ffn_route_scale)
    return x

_drawn_inputs = setup_inputs


def setup_inputs(seed=0):
    import zlib

    import numpy as np

    out = dict(_drawn_inputs(seed))
    spreads = {'L0_xattn_bq': (0.0, 2.0),
     'L0_xattn_bk': (0.0, 0.1),
     'L0_xattn_bv': (0.0, 0.1),
     'L0_xattn_bo': (0.0, 0.356),
     'L0_ffn_bg': (0.0, 0.564),
     'L0_ffn_b1': (0.0, 0.8),
     'L0_ffn_b2': (0.0, 0.8),
     'L1_xattn_bq': (0.0, 0.8),
     'L1_xattn_bk': (0.0, 2.0),
     'L1_xattn_bv': (0.0, 0.8),
     'L1_xattn_bo': (0.0, 0.386)}
    factors = {'L0_attn_last_conv_re': 4.041,
     'L0_attn_last_conv_im': 4.201,
     'L1_xattn_Wq': 8.0,
     'L1_xattn_Wk': 8.0,
     'L1_xattn_Wv': 5.753,
     'L1_xattn_Wo': 5.258,
     'L1_attn_wq': 8.0,
     'L1_attn_bq': 35.305,
     'L1_attn_wk': 8.0,
     'L1_attn_bk': 45.584,
     'L1_attn_bv': 7.88,
     'L1_attn_bo': 4.981,
     'L1_ffn_q_w': 5.571,
     'L1_ffn_k_w': 5.5}
    for name, (base, spread) in spreads.items():
        noise = np.random.default_rng([zlib.crc32(name.encode()), seed]).standard_normal(out[name].shape)
        drawn = base * np.exp(spread * noise) if base else spread * noise
        out[name] = jnp.asarray(drawn.astype(out[name].dtype))
    for name, factor in factors.items():
        out[name] = (out[name] * factor).astype(out[name].dtype)
    return out
```

```python
from contextlib import ExitStack
import math

import numpy as np

import concourse.bass as bass
from concourse import mybir

ALU = mybir.AluOpType
ACT = mybir.ActivationFunctionType
F32 = mybir.dt.float32
BF16 = mybir.dt.bfloat16
U32 = mybir.dt.uint32
AX_X = mybir.AxisListType.X

B = 64
L = 32
D = 128
S = 257
NH = 16
DH = D // NH
PT = 128
TPB = PT // L
NT = B // TPB
TOK = B * L
HG = 4
SF = 2
EPS = 1e-5

CONV_AHEAD = (0, 16)
ROUTE_AHEAD = (16, 8)
EXPERT_AHEAD = (24, 32)
GATHER_AHEAD = (56, 8)

NE = 16
CAP = -(-TOK // NE)
HID = 512
HC = HID // PT
EB = 4

FH = 8
FE = 8
FP = 128

CONST_PARTS = [("ident", 128), ("head16", 16), ("head4", 4), ("upto", 128), ("ones", 128), ("spread16", 128),
               ("token_row", NT), ("rotate", 128), ("cos", L), ("sin", L), ("own_group", HG * D),
               ("rank16", NE), ("rank8", FE)]
CONST_AT = {}
_at = 0
for _name, _n in CONST_PARTS:
    CONST_AT[_name] = (_at, _at + _n)
    _at += _n
CONST_COLS = _at


def shape_constants():
    c = {}
    p = np.arange(PT)
    c["ident"] = np.eye(PT)
    c["head16"] = (p[:, None] // DH == np.arange(NH)[None, :])
    c["head4"] = ((p[:, None] // DH) % HG == np.arange(HG)[None, :])
    c["upto"] = (p[:, None] <= p[None, :])
    c["ones"] = np.ones((PT, PT))
    c["spread16"] = np.zeros((PT, PT))
    c["spread16"][:NH] = (np.arange(NH)[:, None] == p[None, :] // DH)
    c["token_row"] = NE * CAP + PT * np.arange(NT)[None, :] + p[:, None]
    rot = np.zeros((PT, PT))
    for i in range(PT // 2):
        rot[2 * i + 1, 2 * i] = -1.0
        rot[2 * i, 2 * i + 1] = 1.0
    c["rotate"] = rot
    freqs = np.float32(10000.0) ** (np.arange(0, DH, 2, dtype=np.float32) / np.float32(DH))
    angles = np.arange(L, dtype=np.float32)[:, None] / freqs[None, :]
    of_row = (p % DH) // 2
    c["cos"] = np.cos(angles)[:, of_row].T
    c["sin"] = np.sin(angles)[:, of_row].T
    c["own_group"] = np.broadcast_to(
        (np.arange(D)[None, :] // 32 == np.arange(HG)[:, None]).reshape(1, -1), (PT, HG * D))
    c["rank16"] = np.broadcast_to(NE - np.arange(NE)[None, :], (PT, NE))
    c["rank8"] = np.broadcast_to(FE - np.arange(FE)[None, :], (PT, FE))
    return np.concatenate([np.asarray(c[n], np.float32) for n, _ in CONST_PARTS], axis=1)


def wait_count(eng, sem, count):
    if isinstance(count, int) and count <= 0:
        return
    eng.wait_ge(sem, count)


def live(i, j, lag, total=B, per=TPB):
    return not isinstance(i, int) or 0 <= per * i + j - lag < total


def live_tile(i, lag):
    return not isinstance(i, int) or 0 <= i - lag < NT


def tile_steps(eng, step, first=2, tail=2, count=NT):
    for i in range(first):
        step(i)
    with eng.Fori(first, count) as i:
        step(i)
    for i in range(count, count + tail):
        step(i)


def clear_counts(nc, sems):
    nums = sorted(s.num for s in sems)
    runs = []
    for n in nums:
        if runs and runs[-1].stop == n:
            runs[-1] = range(runs[-1].start, n + 1)
        else:
            runs.append(range(n, n + 1))
    with nc.Block() as block:

        @block.gpsimd
        def _(pool):
            for run in runs:
                pool.sem_clear(run)


class State:
    weights_pending = True


def layer_norm(nc, st, tag, padded=False, products=()):
    st.xnT = st.xnT_pad[:, :, 1:L + 1] if padded else st.xnT_flat.rearrange("p (b l) -> p b l", l=L)
    with ExitStack() as ctx:
        stats = ctx.enter_context(nc.sbuf_tensor(f"stats_{tag}", [PT, NT, 6], F32))
        w = ctx.enter_context(nc.sbuf_tensor(f"moments_{tag}", [PT, 8, NT], F32))
        sems = []

        def sem(n):
            sems.append(ctx.enter_context(nc.semaphore(f"{n}_{tag}")))
            return sems[-1]

        stats_done, moment_done, std_done, xn_done, turned, xnT_done, made, kept, pad_done = map(
            sem, ("stats_done", "moment_done", "std_done", "xn_done", "turned", "xnT_done", "made", "kept",
                  "pad_done"))
        G = 4
        mean, var, std, rstd, dif, msum, vsum = (w[:, k, :] for k in range(7))
        x, xn, xnT = st.x, st.xn, st.xnT
        results = [(k, p) for k in range(NT // G) for p in range(len(products))]
        with nc.Block() as block:

            @block.gpsimd
            def _(pool):
                if padded:
                    nc.gpsimd.memset(st.xnT_pad[:, :, 0:1], 0.0).then_inc(pad_done, 1)
                    nc.gpsimd.memset(st.xnT_pad[:, :, L + 1:L + 2], 0.0).then_inc(pad_done, 1)

            @block.vector
            def _(dve):
                for t in range(NT):
                    ins = nc.vector.bn_stats(stats[:, t, :], x[:, t, :])
                ins.then_inc(stats_done, 1)
                dve.wait_ge(stats_done, 1)
                nc.vector.tensor_tensor(msum, stats[:, :, 1], stats[:, :, 4], ALU.add).then_inc(moment_done, 1)
                nc.vector.tensor_tensor(dif, stats[:, :, 1], stats[:, :, 4], ALU.subtract).then_inc(moment_done, 1)
                nc.vector.tensor_tensor(vsum, stats[:, :, 2], stats[:, :, 5], ALU.add).then_inc(moment_done, 1)
                dve.wait_ge(moment_done, 2)
                nc.vector.tensor_scalar(mean, msum, 0.5, None, ALU.mult).then_inc(moment_done, 1)
                nc.vector.scalar_tensor_tensor(var, dif, 0.25, dif, ALU.mult, ALU.mult).then_inc(moment_done, 1)
                dve.wait_ge(moment_done, 3)
                nc.vector.tensor_scalar(vsum, vsum, 1.0 / D, EPS, ALU.mult, ALU.add).then_inc(moment_done, 1)
                dve.wait_ge(moment_done, 6)
                nc.vector.tensor_tensor(var, var, vsum, ALU.add).then_inc(moment_done, 1)
                dve.wait_ge(std_done, 1)
                nc.vector.reciprocal(rstd, std).then_inc(moment_done, 1)
                dve.wait_ge(moment_done, 8)
                for t in range(NT):
                    nc.vector.tensor_scalar(xn[:, t, :], x[:, t, :], mean[:, t:t + 1], rstd[:, t:t + 1],
                                            ALU.subtract, ALU.mult).then_inc(xn_done, 1)
                for n, (k, p) in enumerate(results):
                    _, _, bias, scale, out = products[p]
                    dve.wait_ge(made, n + 1)
                    nc.vector.tensor_scalar(out[:, 512 * k:512 * (k + 1)], st.psum[:, 2 + n % 6, :], bias, scale,
                                            ALU.add, ALU.mult).then_inc(kept, 1)

            @block.scalar
            def _(act):
                nc.scalar.preload_act_table(ACT.Sqrt)
                act.wait_ge(moment_done, 7)
                nc.scalar.activation(std, var, ACT.Sqrt).then_inc(std_done, 1)
                for k in range(NT // G):
                    act.wait_ge(turned, k + 1)
                    nc.scalar.activation(xnT[:, 4 * G * k:4 * G * (k + 1), :],
                                         st.psum[:, k % 2, :].rearrange("p (b l) -> p b l", l=L),
                                         ACT.Copy).then_inc(xnT_done, 1)

            @block.tensor
            def _(pe):
                def turn(k):
                    pe.wait_ge(xn_done, G * (k + 1))
                    if k >= 2:
                        pe.wait_ge(xnT_done, k - 1)
                    for j in range(G):
                        mm = nc.tensor.transpose(st.psum[:, k % 2, PT * j:PT * (j + 1)], xn[:, G * k + j, :], st.ident)
                    mm.then_inc(turned, 1)

                def multiply(n):
                    k, p = results[n]
                    taps, weights = products[p][0:2]
                    pe.wait_ge(xnT_done, k + 1)
                    wait_count(pe, kept, n - 5)
                    for m, tap in enumerate(taps):
                        src = st.xnT if tap is None else st.xnT_pad[:, :, tap:tap + L]
                        mm = nc.tensor.matmul(st.psum[:, 2 + n % 6, :], weights[m], src[:, 16 * k:16 * (k + 1), :],
                                              start=(m == 0), stop=(m == len(taps) - 1))
                    mm.then_inc(made, 1)

                if padded and products:
                    pe.wait_ge(pad_done, 2)
                if st.weights_pending:
                    pe.wait_ge(st.weights_in, st.weights_count)
                for k in range(NT // G + 1):
                    if k < NT // G:
                        turn(k)
                    if k >= 1:
                        for p in range(len(products)):
                            multiply(len(products) * (k - 1) + p)
        st.weights_pending = False
        clear_counts(nc, sems)


def cross_attention_over_queries(nc, st):
    psum, cst, x = st.psum, st.cst, st.x
    qT = st.qT
    with ExitStack() as ctx:
        sb = lambda n, shape, dt=F32: ctx.enter_context(nc.sbuf_tensor("a_" + n, shape, dt))
        sems = []

        def sem(n):
            sems.append(ctx.enter_context(nc.semaphore("a_" + n)))
            return sems[-1]

        ctx_in = sb("ctx_in", [PT, 4, SF, D])
        ctxT = sb("ctxT", [PT, 4, S + 2])
        kT = sb("kT", [PT, 2, SF * PT])
        v = sb("v", [PT, 4, SF * D])
        vz = sb("vz", [PT, 2, SF * D])
        qbd = sb("qbd", [PT, 2, NH, L])
        prob = sb("prob", [PT, 4, SF * NH, L])
        top = sb("top", [PT, 2, SF * NH])
        total = sb("total", [PT, 2, SF * NH])
        inv = sb("inv", [PT, 2, SF * NH])
        attn = sb("attn", [PT, HG, TPB, L])
        left_in = sb("left_in", [B, D])
        leftT = sb("leftT", [PT, B])
        klT = sb("klT", [PT, B])
        vlT = sb("vlT", [PT, B])
        lprod = sb("lprod", [PT, B, L])
        lprob = sb("lprob", [NH, B, L])
        ltop = sb("ltop", [NH, B])
        linv = sb("linv", [NH, B])
        lattn = sb("lattn", [PT, TOK])
        lstage = sb("lstage", [PT, PT])
        womask = sb("womask", [PT, HG, D])
        bv_row = sb("bv_row", [1, D])

        wq, wk, wv, wo = (st.w[n] for n in ("L0_xattn_Wq", "L0_xattn_Wk", "L0_xattn_Wv", "L0_xattn_Wo"))
        bk, bvc = st.col["L0_xattn_bk"], st.col["L0_xattn_bv"]

        lload, lturn, lkept, lkv, lkv_kept, lprod_done, ls_done, lsm, lsp, latt = map(
            sem, ("lload", "lturn", "lkept", "lkv", "lkv_kept", "lprod_done", "ls_done", "lsm", "lsp", "latt"))
        lscore = psum[0:NH, 0:4, :].rearrange("p k (b l) -> p (k b) l", l=L)
        with nc.Block() as block:

            @block.sync
            def _(sp):
                sp.dma_start(left_in[:], st.ctx[:, S - 1, :]).then_inc(lload, 16)
                sp.dma_start(bv_row[:], st.dram["L0_xattn_bv"].rearrange("(o d) -> o d", o=1)).then_inc(lload, 16)
                sp.wait_ge(lload, 32)

            @block.gpsimd
            def _(pool):
                for c in (0, S + 1):
                    nc.gpsimd.memset(ctxT[:, :, c:c + 1], 0.0)
                pool.wait_ge(st.weights_in, st.weights_count)
                for h in range(HG):
                    nc.gpsimd.tensor_scalar(womask[:, h, :], wo, cst["head4"][:, h:h + 1], None, ALU.mult)

            @block.tensor
            def _(pe):
                pe.wait_ge(lload, 32)
                nc.tensor.transpose(psum[:, 4, 0:B], left_in[:], cst["ident"][0:B, 0:B]).then_inc(lturn, 1)
                pe.wait_ge(lkept, 1)
                nc.tensor.matmul(psum[:, 5, 0:B], wk, leftT[:], start=True, stop=True)
                nc.tensor.matmul(psum[:, 5, B:2 * B], wv, leftT[:], start=True, stop=True).then_inc(lkv, 1)
                pe.wait_ge(lprod_done, 1)
                for k in range(4):
                    mm = nc.tensor.matmul(psum[0:NH, k, :], cst["head16"], lprod[:, 16 * k:16 * (k + 1), :],
                                          start=True, stop=True)
                mm.then_inc(ls_done, 1)
                pe.wait_ge(lsp, 1)
                for k in range(4):
                    nc.tensor.matmul(psum[:, k, :], cst["spread16"][0:NH, :], lprob[:, 16 * k:16 * (k + 1), :],
                                     start=True, stop=True).then_inc(latt, 1)

            @block.vector
            def _(dve):
                dve.wait_ge(lturn, 1)
                nc.vector.tensor_copy(leftT[:], psum[:, 4, 0:B]).then_inc(lkept, 1)
                dve.wait_ge(lkv, 1)
                nc.vector.tensor_scalar(klT[:], psum[:, 5, 0:B], bk, None, ALU.add).then_inc(lkv_kept, 1)
                nc.vector.tensor_scalar(vlT[:], psum[:, 5, B:2 * B], bvc, None, ALU.add).then_inc(lkv_kept, 1)
                dve.wait_ge(lkv_kept, 2)
                nc.vector.tensor_tensor(lprod[:], qT[:].rearrange("p (b l) -> p b l", l=L),
                                        klT[:].unsqueeze(2).broadcast_to([PT, B, L]), ALU.mult).then_inc(lprod_done, 1)
                dve.wait_ge(ls_done, 1)
                nc.vector.tensor_reduce(ltop[:], lscore, AX_X, ALU.max).then_inc(lsm, 1)
                dve.wait_ge(lsm, 1)
                nc.vector.tensor_tensor(lprob[:], lscore, ltop[:].unsqueeze(2).broadcast_to([NH, B, L]),
                                        ALU.subtract).then_inc(lsm, 1)
                dve.wait_ge(lsm, 3)
                nc.vector.tensor_reduce(ltop[:], lprob[:], AX_X, ALU.add).then_inc(lsm, 1)
                dve.wait_ge(lsm, 4)
                nc.vector.reciprocal(linv[:], ltop[:]).then_inc(lsm, 1)
                dve.wait_ge(lsm, 5)
                nc.vector.tensor_tensor(lprob[:], lprob[:], linv[:].unsqueeze(2).broadcast_to([NH, B, L]),
                                        ALU.mult).then_inc(lsp, 1)
                for k in range(4):
                    dve.wait_ge(latt, k + 1)
                    nc.vector.tensor_tensor(
                        lattn[:, 512 * k:512 * (k + 1)].rearrange("p (b l) -> p b l", l=L),
                        psum[:, k, :].rearrange("p (b l) -> p b l", l=L),
                        vlT[:, 16 * k:16 * (k + 1)].unsqueeze(2).broadcast_to([PT, 16, L]), ALU.mult)

            @block.scalar
            def _(act):
                act.wait_ge(lsm, 2)
                nc.scalar.activation(lprob[:], lprob[:], ACT.Exp).then_inc(lsm, 1)

        load_done = [sem(f"load_done{k}") for k in range(4)]
        store_done = [sem(f"store_done{k}") for k in range(4)]
        (turned, left_put, ctxT_kept, kT_kept, v_done, v_kept, qbd_done, s_done, top_done, sub_done, exp_done,
         total_done, inv_done, vz_done, pv_done, attn_kept, lstage_done, o_done, x_done) = map(sem, (
             "turned", "left_put", "ctxT_kept", "kT_kept", "v_done", "v_kept", "qbd_done", "s_done",
             "top_done", "sub_done", "exp_done", "total_done", "inv_done", "vz_done", "pv_done", "attn_kept",
             "lstage_done", "o_done", "x_done"))
        scores = [psum[:, 0:2, :].rearrange("p t (h l) -> p (t h) l", l=L),
                  psum[:, 2:4, :].rearrange("p t (h l) -> p (t h) l", l=L)]
        T_BANK, KV_BANK, O_BANK, A_BANK = 4, 5, 6, 7
        V_AT = SF * PT
        KV, SC, PV, OUT = 1, 2, 4, 2

        with nc.Block() as block:

            @block.sync
            def _(sp):
                def step(i):
                    for j in range(TPB):
                        n = TPB * i + j
                        if live(i, j, 0):
                            wait_count(sp, turned, n - 3)
                            sp.dma_start(ctx_in[:, j, :, :], st.ctx[n, 0:SF * PT, :].rearrange(
                                "(t p) d -> p t d", p=PT)).then_inc(load_done[j], 16)
                tile_steps(sp, step, 1, 0)

            @block.gpsimd
            def _(pool):
                def step(i):
                    if live_tile(i, OUT):
                        wait_count(pool, o_done, i - OUT)
                        nc.gpsimd.tensor_copy(lstage[:], lattn[:, bass.ds((i - OUT) * PT, PT)]
                                              ).then_inc(lstage_done, 1)
                    for j in range(TPB):
                        if live(i, j, 0):
                            n = TPB * i + j
                            wait_count(pool, v_done, n - 3)
                            wait_count(pool, store_done[j], 16 * i)
                            nc.gpsimd.tensor_copy(ctxT[:, j, S:S + 1], leftT[:, bass.ds(n, 1)]).then_inc(left_put, 1)
                        if live(i, j, KV):
                            n = TPB * i + j - KV
                            wait_count(pool, s_done, n - 1)
                            nc.gpsimd.tensor_tensor(
                                qbd[:, (j - KV) % 2], qT[:, bass.ds(n * L, L)].unsqueeze(1).broadcast_to([PT, NH, L]),
                                cst["head16"].unsqueeze(2).broadcast_to([PT, NH, L]), ALU.mult).then_inc(qbd_done, 1)
                        if live(i, j, PV):
                            n = TPB * i + j - PV
                            pool.wait_ge(inv_done, n + 1)
                            pool.wait_ge(v_kept, n + 1)
                            wait_count(pool, pv_done, n - 1)
                            nc.gpsimd.tensor_tensor(
                                vz[:, (j - PV) % 2].rearrange("p (h d) -> p h d", d=DH),
                                v[:, (j - PV) % 4].rearrange("p (h d) -> p h d", d=DH),
                                inv[:, (j - PV) % 2].unsqueeze(2).broadcast_to([PT, SF * NH, DH]),
                                ALU.mult).then_inc(vz_done, 1)
                tile_steps(pool, step)

            @block.tensor
            def _(pe):
                def step(i):
                    for j in range(TPB):
                        n = TPB * i + j
                        if live(i, j, 0):
                            pe.wait_ge(load_done[j], 16 * (i + 1))
                            wait_count(pe, ctxT_kept, n)
                            for t in range(SF):
                                mm = nc.tensor.transpose(psum[:, T_BANK, PT * t:PT * (t + 1)], ctx_in[:, j, t, :],
                                                         st.ident)
                            mm.then_inc(turned, 1)
                        if live(i, j, SC):
                            m = n - SC
                            pe.wait_ge(kT_kept, m + 1)
                            pe.wait_ge(qbd_done, m + 1)
                            wait_count(pe, sub_done, m - 1)
                            for t in range(SF):
                                mm = nc.tensor.matmul(psum[:, 2 * ((j - SC) % 2) + t, :],
                                                      kT[:, (j - SC) % 2, PT * t:PT * (t + 1)],
                                                      qbd[:, (j - SC) % 2], start=True, stop=True)
                            mm.then_inc(s_done, 1)
                        if live(i, j, KV):
                            m = n - KV
                            c = (j - KV) % 4
                            pe.wait_ge(ctxT_kept, m + 1)
                            wait_count(pe, v_kept, m)
                            nc.tensor.matmul(psum[:, KV_BANK, 0:SF * PT], wk, ctxT[:, c, 1:SF * PT + 1],
                                             start=True, stop=True)
                            for t in range(SF):
                                to = psum[:, KV_BANK, V_AT + D * t:V_AT + D * (t + 1)]
                                nc.tensor.matmul(to, ctxT[:, c, 1 + PT * t:1 + PT * (t + 1)], wv,
                                                 start=True, stop=False)
                                mm = nc.tensor.matmul(to, cst["ones"][0:1, :], bv_row[:], start=False, stop=True)
                            mm.then_inc(v_done, 1)
                        if live(i, j, PV):
                            m = n - PV
                            c = (j - PV) % 4
                            pe.wait_ge(vz_done, m + 1)
                            if c == 0:
                                wait_count(pe, attn_kept, i - 1)
                            for t in range(SF):
                                for g in range(HG):
                                    mm = nc.tensor.matmul(
                                        psum[32 * g:32 * (g + 1), A_BANK, PT * c:PT * (c + 1)],
                                        vz[:, (j - PV) % 2, D * t + 32 * g:D * t + 32 * (g + 1)],
                                        prob[:, c, NH * t + HG * g:NH * t + HG * (g + 1), :],
                                        start=(t == 0), stop=(t == SF - 1), tile_position=(0, 32 * g))
                            mm.then_inc(pv_done, 1)
                        if j == 1 and live_tile(i, OUT):
                            t = i - OUT
                            pe.wait_ge(attn_kept, t + 1)
                            pe.wait_ge(lstage_done, t + 1)
                            wait_count(pe, x_done, t)
                            o = psum[:, O_BANK, 0:D]
                            for h in range(HG):
                                nc.tensor.matmul(o, attn[:, h], womask[:, h, :], start=(h == 0), stop=False)
                            nc.tensor.matmul(o, lstage[:], wo, start=False, stop=False)
                            nc.tensor.matmul(o, cst["ones"][0:1, :], st.row["L0_xattn_bo"], start=False, stop=True
                                             ).then_inc(o_done, 1)
                tile_steps(pe, step)

            @block.vector
            def _(dve):
                def step(i):
                    for j in range(TPB):
                        n = TPB * i + j
                        if j == 3 and live_tile(i, OUT):
                            dve.wait_ge(o_done, i - OUT + 1)
                            xt = x[:, bass.ds(i - OUT, 1), :].rearrange("p o d -> p (o d)")
                            nc.vector.tensor_tensor(xt, xt, psum[:, O_BANK, 0:D], ALU.add).then_inc(x_done, 1)
                        if live(i, j, SC):
                            m = n - SC
                            sc = scores[(j - SC) % 2]
                            dve.wait_ge(s_done, m + 1)
                            nc.vector.tensor_reduce(top[:, (j - SC) % 2], sc, AX_X, ALU.max).then_inc(top_done, 1)
                        if live(i, j, SC + 1):
                            m = n - SC - 1
                            c = (j - SC - 1) % 4
                            dve.wait_ge(exp_done, m + 1)
                            nc.vector.tensor_reduce(total[:, c % 2], prob[:, c], AX_X, ALU.add).then_inc(total_done, 1)
                        if live(i, j, SC):
                            m = n - SC
                            c = (j - SC) % 4
                            dve.wait_ge(top_done, m + 1)
                            wait_count(dve, pv_done, m - 3)
                            nc.vector.tensor_tensor(prob[:, c], scores[c % 2],
                                                    top[:, c % 2].unsqueeze(2).broadcast_to([PT, SF * NH, L]),
                                                    ALU.subtract).then_inc(sub_done, 1)
                        if live(i, j, SC + 1):
                            m = n - SC - 1
                            c = (j - SC - 1) % 2
                            dve.wait_ge(total_done, m + 1)
                            wait_count(dve, vz_done, m - 1)
                            nc.vector.reciprocal(inv[:, c], total[:, c]).then_inc(inv_done, 1)
                tile_steps(dve, step)

            @block.scalar
            def _(act):
                nc.scalar.preload_act_table(ACT.Exp)

                def step(i):
                    for j in range(TPB):
                        n = TPB * i + j
                        if j == 0 and live_tile(i, OUT):
                            t = i - OUT
                            act.wait_ge(pv_done, TPB * (t + 1))
                            wait_count(act, o_done, t)
                            nc.scalar.activation(attn[:].rearrange("p h b l -> p b h l"), psum[:, A_BANK, :].rearrange(
                                "p (b h l) -> p b h l", b=TPB, h=HG), ACT.Copy).then_inc(attn_kept, 1)
                        if live(i, j, 0):
                            act.wait_ge(turned, n + 1)
                            wait_count(act, v_done, n - 3)
                            wait_count(act, store_done[j], 16 * i)
                            nc.scalar.activation(ctxT[:, j, 1:SF * PT + 1], psum[:, T_BANK, 0:SF * PT], ACT.Copy
                                                 ).then_inc(ctxT_kept, 1)
                        if live(i, j, KV):
                            m = n - KV
                            act.wait_ge(left_put, m + 1)
                            act.wait_ge(ctxT_kept, m + 1)
                            act.dma_start(st.ctx_all[:, bass.ds(m, 1), :].rearrange("p o s -> p (o s)"),
                                          ctxT[:, (j - KV) % 4, :]).then_inc(store_done[(j - KV) % 4], 16)
                            act.wait_ge(v_done, m + 1)
                            wait_count(act, s_done, m - 1)
                            nc.scalar.activation(kT[:, (j - KV) % 2], psum[:, KV_BANK, 0:SF * PT], ACT.Identity,
                                                 bias=bk).then_inc(kT_kept, 1)
                            wait_count(act, vz_done, m - 3)
                            nc.scalar.activation(v[:, (j - KV) % 4], psum[:, KV_BANK, V_AT:V_AT + SF * D], ACT.Copy
                                                 ).then_inc(v_kept, 1)
                        if live(i, j, SC):
                            m = n - SC
                            act.wait_ge(sub_done, m + 1)
                            nc.scalar.activation(prob[:, (j - SC) % 4], prob[:, (j - SC) % 4], ACT.Exp
                                                 ).then_inc(exp_done, 1)
                tile_steps(act, step)
                for k in range(4):
                    act.wait_ge(store_done[k], 16 * NT)
        clear_counts(nc, sems)


class ContextProjection:
    BANKS = 4
    KEEP = 1

    def __init__(self, nc, st, tag, first, count, ctx, per=4):
        self.nc, self.st, self.first, self.count, self.per = nc, st, first, count, per
        sb = lambda n, shape: ctx.enter_context(nc.sbuf_tensor(f"p_{n}_{tag}", shape, F32))
        self.sems = []

        def sem(n):
            self.sems.append(ctx.enter_context(nc.semaphore(f"p_{n}_{tag}")))
            return self.sems[-1]

        self.ctxT = sb("ctxT", [PT, 4, S + 2])
        self.v = sb("v", [PT, 4, SF * D])
        self.load_done = [sem(f"load_done{k}") for k in range(4)]
        self.store_done = [sem(f"store_done{k}") for k in range(4)]
        self.v_done, self.k_done, self.v_kept, self.k_kept = map(sem, ("v_done", "k_done", "v_kept", "k_kept"))

    def is_live(self, i, j, lag=0):
        return live(i, j, lag, self.count, self.per)

    def uses(self, i, j):
        return self.per // 4 * i + j // 4

    def load(self, sp, i, j):
        if self.is_live(i, j):
            m, c = self.per * i + j, j % 4
            wait_count(sp, self.k_done, m - 3)
            sp.dma_start(self.ctxT[:, c, :], self.st.ctx_all[:, bass.ds(self.first + m, 1), :].rearrange(
                "p o s -> p (o s)")).then_inc(self.load_done[c], 16)

    def project(self, pe, i, j):
        if self.is_live(i, j):
            nc, st, m, c = self.nc, self.st, self.per * i + j, j % 4
            bank = self.BANKS + 2 * (j % 2)
            pe.wait_ge(self.load_done[c], 16 * (self.uses(i, j) + 1))
            wait_count(pe, self.v_kept, m - 1)
            for t in range(SF):
                for tap in range(3):
                    mm = nc.tensor.matmul(st.psum[:, bank, D * t:D * (t + 1)],
                                          self.ctxT[:, c, tap + PT * t:tap + PT * (t + 1)], st.convw[:, 2, tap, :],
                                          start=(tap == 0), stop=(tap == 2))
            mm.then_inc(self.v_done, 1)
            wait_count(pe, self.k_kept, m - 1)
            for tap in range(3):
                mm = nc.tensor.matmul(st.psum[:, bank + 1, 0:S], st.convw[:, 1, tap, :], self.ctxT[:, c, tap:tap + S],
                                      start=(tap == 0), stop=(tap == 2))
            mm.then_inc(self.k_done, 1)

    def keep(self, act, i, j):
        if self.is_live(i, j, self.KEEP):
            nc, st, m, c = self.nc, self.st, self.per * i + j - self.KEEP, (j - self.KEEP) % 4
            bank = self.BANKS + 2 * (c % 2)
            act.wait_ge(self.v_done, m + 1)
            wait_count(act, self.store_done[c], 16 * self.uses(i, j - self.KEEP))
            nc.scalar.activation(self.v[:, c, :], st.psum[:, bank, 0:SF * D], ACT.Copy).then_inc(self.v_kept, 1)
            act.wait_ge(self.k_done, m + 1)
            nc.scalar.activation(st.ctx_all[:, bass.ds(self.first + m, 1), 0:S].rearrange("p o s -> p (o s)"),
                                 st.psum[:, bank + 1, 0:S], ACT.Identity, bias=st.col["L1_xattn_bk"]
                                 ).then_inc(self.k_kept, 1)
            act.wait_ge(self.v_kept, m + 1)
            act.dma_start(st.v_dram[bass.ds(self.first + m, 1)].rearrange("o p d -> p (o d)"), self.v[:, c, :]
                          ).then_inc(self.store_done[c], 16)

    def run(self, eng, work):
        def step(i):
            for j in range(4):
                work(eng, i, j)
        tile_steps(eng, step, 1, 1, self.count // 4)

    def finish(self, sp):
        for k in range(4):
            sp.wait_ge(self.store_done[k], 16 * (self.count // 4))


def long_convolution(nc, st):
    x, psum = st.x, st.psum
    with ExitStack() as ctx:
        sb = lambda n, shape, dt=F32: ctx.enter_context(nc.sbuf_tensor("b_" + n, shape, dt))
        sems = []

        def sem(n):
            sems.append(ctx.enter_context(nc.semaphore("b_" + n)))
            return sems[-1]

        ph = sb("ph", [PT, 8])
        w = sb("w", [PT, 8])
        re = sb("re", [PT, L + 1])
        im = sb("im", [PT, L + 1])
        t1 = sb("t1", [PT, L])
        t2 = sb("t2", [PT, L])
        filt = sb("filt", [PT, L])
        past = sb("past", [PT, L])
        y = sb("y", [PT, B, L])
        ph_in, mag2_done, act_done, scale_done, power_done, tap_done, turned, x_done = map(sem, (
            "ph_in", "mag2_done", "act_done", "scale_done", "power_done", "tap_done", "turned", "x_done"))
        ahead = ContextProjection(nc, st, "b", CONV_AHEAD[0], CONV_AHEAD[1], ctx)
        with nc.Block() as block:

            @block.sync
            def _(sp):
                for k, n in enumerate(("phazor", "phazor_init")):
                    sp.dma_start(ph[:, 2 * k:2 * k + 2], st.dram["L0_attn_" + n]).then_inc(ph_in, 16)
                for k, n in enumerate(("last_conv_re", "last_conv_im")):
                    sp.dma_start(ph[:, 4 + k:5 + k], st.dram["L0_attn_" + n].rearrange("(p o) -> p o", o=1)
                                 ).then_inc(ph_in, 16)
                ahead.run(sp, ahead.load)
                ahead.finish(sp)

            @block.scalar
            def _(act):
                act.wait_ge(mag2_done, 4)
                nc.scalar.activation(w[:, 3:4], w[:, 2:3], ACT.Sqrt).then_inc(act_done, 1)
                act.wait_ge(act_done, 1)
                nc.scalar.activation(w[:, 4:5], w[:, 3:4], ACT.Exp, scale=-1.0).then_inc(act_done, 1)
                ahead.run(act, ahead.keep)

            @block.vector
            def _(dve):
                dve.wait_ge(ph_in, 64)
                nc.vector.tensor_tensor(w[:, 0:2], ph[:, 0:2], ph[:, 0:2], ALU.mult).then_inc(mag2_done, 1)
                nc.vector.memset(re[:, 0:1], 1.0).then_inc(mag2_done, 1)
                nc.vector.memset(im[:, 0:1], 0.0).then_inc(mag2_done, 1)
                dve.wait_ge(mag2_done, 3)
                nc.vector.tensor_tensor(w[:, 2:3], w[:, 0:1], w[:, 1:2], ALU.add).then_inc(mag2_done, 1)
                dve.wait_ge(act_done, 1)
                nc.vector.reciprocal(w[:, 5:6], w[:, 3:4]).then_inc(scale_done, 1)
                dve.wait_ge(act_done, 2)
                dve.wait_ge(scale_done, 1)
                nc.vector.tensor_tensor(w[:, 6:7], w[:, 4:5], w[:, 5:6], ALU.mult).then_inc(scale_done, 1)
                dve.wait_ge(scale_done, 2)
                nc.vector.tensor_scalar(re[:, 1:2], ph[:, 0:1], w[:, 6:7], None, ALU.mult).then_inc(power_done, 1)
                nc.vector.tensor_scalar(im[:, 1:2], ph[:, 1:2], w[:, 6:7], None, ALU.mult).then_inc(power_done, 1)
                done = 2
                m = 1
                while m < L:
                    a, b = re[:, m:m + 1], im[:, m:m + 1]
                    dve.wait_ge(power_done, done)
                    nc.vector.tensor_scalar(t1[:, 0:m], im[:, 1:m + 1], b, None, ALU.mult).then_inc(power_done, 1)
                    nc.vector.tensor_scalar(t2[:, 0:m], im[:, 1:m + 1], a, None, ALU.mult).then_inc(power_done, 1)
                    dve.wait_ge(power_done, done + 2)
                    nc.vector.scalar_tensor_tensor(re[:, m + 1:2 * m + 1], re[:, 1:m + 1], a, t1[:, 0:m],
                                                   ALU.mult, ALU.subtract).then_inc(power_done, 1)
                    nc.vector.scalar_tensor_tensor(im[:, m + 1:2 * m + 1], re[:, 1:m + 1], b, t2[:, 0:m],
                                                   ALU.mult, ALU.add).then_inc(power_done, 1)
                    done += 4
                    m *= 2
                dve.wait_ge(power_done, done)
                nc.vector.tensor_scalar(t1[:], im[:, 0:L], ph[:, 3:4], None, ALU.mult).then_inc(power_done, 1)
                nc.vector.tensor_scalar(t2[:], im[:, 1:L + 1], ph[:, 5:6], None, ALU.mult).then_inc(power_done, 1)
                dve.wait_ge(power_done, done + 2)
                nc.vector.scalar_tensor_tensor(filt[:], re[:, 0:L], ph[:, 2:3], t1[:], ALU.mult, ALU.subtract
                                               ).then_inc(power_done, 1)
                nc.vector.scalar_tensor_tensor(past[:], re[:, 1:L + 1], ph[:, 4:5], t2[:], ALU.mult, ALU.subtract
                                               ).then_inc(power_done, 1)
                dve.wait_ge(power_done, done + 4)
                nc.vector.scalar_tensor_tensor(y[:], st.xnT, filt[:, 0:1],
                                               past[:].unsqueeze(1).broadcast_to([PT, B, L]),
                                               ALU.mult, ALU.add).then_inc(tap_done, 1)
                for j in range(1, L):
                    dve.wait_ge(tap_done, j)
                    nc.vector.scalar_tensor_tensor(y[:, :, j:L], st.xnT[:, :, 0:L - j], filt[:, j:j + 1], y[:, :, j:L],
                                                   ALU.mult, ALU.add).then_inc(tap_done, 1)
                for k in range(4):
                    dve.wait_ge(turned, k + 1)
                    xk = x[:, 4 * k:4 * (k + 1), :].rearrange("p t d -> p (t d)")
                    nc.vector.tensor_tensor(xk, xk, psum[:, k, :], ALU.add)

            @block.tensor
            def _(pe):
                ahead.run(pe, ahead.project)
                pe.wait_ge(tap_done, L)
                for k in range(4):
                    for j in range(4):
                        t = 4 * k + j
                        mm = nc.tensor.transpose(psum[:, k, PT * j:PT * (j + 1)],
                                                 y[:, TPB * t:TPB * (t + 1), :].rearrange("p b l -> p (b l)"), st.ident)
                    mm.then_inc(turned, 1)
        clear_counts(nc, sems + ahead.sems)


def routed_ffn(nc, st):
    x, xn, psum, cst = st.x, st.xn, st.psum, st.cst
    with ExitStack() as ctx:
        sb = lambda n, shape, dt=F32: ctx.enter_context(nc.sbuf_tensor("c_" + n, shape, dt))
        sems = []

        def sem(n):
            sems.append(ctx.enter_context(nc.semaphore("c_" + n)))
            return sems[-1]

        scattered, gathered, y_stored = st.scattered, st.gathered, st.y_stored
        slots = nc.dram_tensor("slots_dram", (NE * CAP + TOK, D), F32).ap()
        answers = nc.dram_tensor("answers_dram", (NE * CAP, D), F32).ap()
        wg = sb("wg", [PT, NE])
        bg = sb("bg", [PT, NE])
        b1 = sb("b1", [NE * HC, PT])
        b1T = sb("b1T", [PT, NE * HC])
        logit = sb("logit", [PT, NT, NE])
        cand = sb("cand", [PT, NT, NE])
        onehot = sb("onehot", [PT, NT, NE])
        before = sb("before", [PT, 2, NT, NE])
        r = sb("r", [PT, 10, NT])
        dst = sb("dst", [PT, NT], U32)
        src = sb("src", [PT, NT], U32)
        back = sb("back", [PT, NT, D])
        w1 = sb("w1", [PT, EB, HID])
        w2 = sb("w2", [PT, EB, HC, D])
        b2 = sb("b2", [1, EB, D])
        rows = sb("rows", [PT, EB, D])
        rowsT = sb("rowsT", [PT, EB, CAP])
        hT = sb("hT", [PT, EB, HC, CAP])
        y = sb("y", [PT, EB, D])
        top, total, gate, first, count, keep, slot, gk, dstf, srcf = (r[:, k, :] for k in range(10))
        over_e = lambda a: a.unsqueeze(2).broadcast_to([PT, NT, NE])

        (route_in, zeroed, zero_stored, b1_turned, logits_done, route, exp_done, count_done, dst_done,
         prefix_done) = map(sem, ("route_in", "zeroed", "zero_stored", "b1_turned", "logits_done", "route", "exp_done",
                       "count_done", "dst_done", "prefix_done"))
        ahead = ContextProjection(nc, st, "c", ROUTE_AHEAD[0], ROUTE_AHEAD[1], ctx)
        with nc.Block() as block:

            @block.sync
            def _(sp):
                sp.dma_start(wg[:], st.dram["L0_ffn_Wg"]).then_inc(route_in, 16)
                sp.dma_start(bg[:], st.dram["L0_ffn_bg"].rearrange("(o e) -> o e", o=1).broadcast_to([PT, NE])
                             ).then_inc(route_in, 16)
                sp.dma_start(b1[:], st.dram["L0_ffn_b1"].rearrange("e (c p) -> (e c) p", p=PT)).then_inc(route_in, 16)
                sp.wait_ge(zeroed, 1)
                sp.dma_start(slots[0:NE * CAP, :].rearrange("(p r) d -> p r d", p=PT), back[:]
                             ).then_inc(zero_stored, 16)
                ahead.run(sp, ahead.load)
                ahead.finish(sp)
                sp.wait_ge(zero_stored, 16)

            @block.tensor
            def _(pe):
                pe.wait_ge(route_in, 48)
                nc.tensor.transpose(psum[:, 2, 0:NE * HC], b1[:], cst["ident"][0:NE * HC, 0:NE * HC]
                                    ).then_inc(b1_turned, 1)
                for t in range(NT):
                    mm = nc.tensor.matmul(psum[:, 0, NE * t:NE * (t + 1)], st.xnT_flat[:, PT * t:PT * (t + 1)], wg[:],
                                          start=True, stop=True)
                mm.then_inc(logits_done, 1)
                pe.wait_ge(route, 10)
                nc.tensor.matmul(psum[:, 1, 0:NT * NE], cst["upto"], onehot[:], start=True, stop=False)
                nc.tensor.matmul(psum[:, 1, 0:NT * NE], cst["ones"], before[:, 0], start=False, stop=True
                                 ).then_inc(count_done, 1)
                ahead.run(pe, ahead.project)

            @block.scalar
            def _(act):
                act.wait_ge(route, 4)
                nc.scalar.activation(logit[:], logit[:], ACT.Exp).then_inc(exp_done, 1)
                act.wait_ge(b1_turned, 1)
                nc.scalar.activation(b1T[:], psum[:, 2, 0:NE * HC], ACT.Copy)
                ahead.run(act, ahead.keep)

            @block.vector
            def _(dve):
                n = [0]

                def counted(instruction):
                    n[0] += 1
                    instruction.then_inc(route, 1)

                flat = lambda a: a.rearrange("p t e -> p (t e)")
                nc.vector.memset(back[:], 0.0).then_inc(zeroed, 1)
                dve.wait_ge(logits_done, 1)
                ps = psum[:, 0, 0:NT * NE].rearrange("p (t e) -> p t e", e=NE)
                counted(nc.vector.tensor_tensor(logit[:], ps, bg[:].unsqueeze(1).broadcast_to([PT, NT, NE]), ALU.add))
                dve.wait_ge(route, 1)
                counted(nc.vector.tensor_reduce(top, logit[:], AX_X, ALU.max))
                dve.wait_ge(route, 2)
                counted(nc.vector.tensor_tensor(logit[:], logit[:], over_e(top), ALU.subtract))
                dve.wait_ge(route, 3)
                counted(nc.vector.scalar_tensor_tensor(cand[:], logit[:], 0.0,
                                                       cst["rank16"].unsqueeze(1).broadcast_to([PT, NT, NE]),
                                                       ALU.is_ge, ALU.mult))
                dve.wait_ge(exp_done, 1)
                counted(nc.vector.tensor_reduce(total, logit[:], AX_X, ALU.add))
                dve.wait_ge(route, 5)
                counted(nc.vector.tensor_reduce(first, cand[:], AX_X, ALU.max))
                dve.wait_ge(route, 6)
                counted(nc.vector.tensor_tensor(onehot[:], cand[:], over_e(first), ALU.is_equal))
                dve.wait_ge(route, 7)
                counted(nc.vector.memset(before[:, 0, 0:1, :], 0.0))
                counted(nc.vector.tensor_copy(before[:, 0, 1:NT, :], onehot[:, 0:NT - 1, :]))
                a = 0
                for k in range(4):
                    m = 1 << k
                    dve.wait_ge(prefix_done, 2 * k) if k else dve.wait_ge(route, 9)
                    nc.vector.tensor_copy(before[:, 1 - a, 0:m, :], before[:, a, 0:m, :]).then_inc(prefix_done, 1)
                    nc.vector.tensor_tensor(before[:, 1 - a, m:NT, :], before[:, a, m:NT, :],
                                            before[:, a, 0:NT - m, :], ALU.add).then_inc(prefix_done, 1)
                    a = 1 - a
                dve.wait_ge(prefix_done, 8)
                counted(nc.vector.reciprocal(gate, total))
                dve.wait_ge(count_done, 1)
                ps = psum[:, 1, 0:NT * NE].rearrange("p (t e) -> p t e", e=NE)
                counted(nc.vector.tensor_tensor(cand[:], ps, onehot[:], ALU.mult))
                dve.wait_ge(route, 11)
                counted(nc.vector.tensor_reduce(count, cand[:], AX_X, ALU.add))
                dve.wait_ge(route, 12)
                counted(nc.vector.tensor_scalar(keep, count, float(CAP), None, ALU.is_le))
                counted(nc.vector.tensor_scalar(slot, first, -float(CAP), float(NE * CAP - 1), ALU.mult, ALU.add))
                dve.wait_ge(route, 14)
                counted(nc.vector.tensor_tensor(slot, slot, count, ALU.add))
                counted(nc.vector.tensor_tensor(gk, gate, keep, ALU.mult))
                dve.wait_ge(route, 16)
                counted(nc.vector.tensor_tensor(dstf, slot, cst["token_row"], ALU.subtract))
                counted(nc.vector.tensor_tensor(srcf, slot, keep, ALU.mult))
                dve.wait_ge(route, 18)
                counted(nc.vector.tensor_tensor(dstf, dstf, keep, ALU.mult))
                nc.vector.tensor_copy(src[:], srcf)
                dve.wait_ge(route, 19)
                counted(nc.vector.tensor_tensor(dstf, dstf, cst["token_row"], ALU.add))
                dve.wait_ge(route, 20)
                nc.vector.tensor_copy(dst[:], dstf).then_inc(dst_done, 1)

            @block.gpsimd
            def _(pool):
                pool.wait_ge(dst_done, 1)
                pool.wait_ge(zero_stored, 16)
                for t in range(NT):
                    nc.gpsimd.indirect_dma_start(
                        out=slots, out_offset=bass.IndirectOffsetOnAxis(ap=dst[:, t:t + 1], axis=0),
                        in_=xn[:, t, :], in_offset=None).then_inc(scattered, 16)
                pool.wait_ge(scattered, 16 * NT)

        clear_counts(nc, ahead.sems)
        ahead.first, ahead.count, ahead.per = *EXPERT_AHEAD, 2 * EB

        row_in = [sem(f"row_in{k}") for k in range(EB)]
        w_in = [sem(f"w_in{k}") for k in range(EB)]
        turned, rowsT_kept, h_done, hT_kept, y_done, y_kept, x_done = map(sem, (
            "turned", "rowsT_kept", "h_done", "hT_kept", "y_done", "y_kept", "x_done"))
        HL, YL = 1, 2
        is_live = lambda i, j, lag: live(i, j, lag, NE, EB)
        steps = lambda eng, step: tile_steps(eng, step, 1, 1, NE // EB)
        with nc.Block() as block:

            @block.sync
            def _(sp):
                def step(i):
                    for j in range(EB):
                        e = EB * i + j
                        if is_live(i, j, 0):
                            wait_count(sp, y_done, e - EB + 1)
                            sp.dma_start(w1[:, j, :], st.dram["L0_ffn_W1"][e]).then_inc(w_in[j], 16)
                            sp.dma_start(w2[:, j], st.dram["L0_ffn_W2"][e].rearrange("(c p) d -> p c d", p=PT)
                                         ).then_inc(w_in[j], 16)
                            sp.dma_start(b2[:, j, :], st.dram["L0_ffn_b2"][bass.ds(e, 1), :]).then_inc(w_in[j], 16)
                        for k in (2 * j, 2 * j + 1):
                            ahead.load(sp, i, k)
                steps(sp, step)
                ahead.finish(sp)

            @block.scalar
            def _(act):
                def step(i):
                    for j in range(EB):
                        e = EB * i + j
                        if is_live(i, j, 0):
                            wait_count(act, turned, e - EB + 1)
                            act.dma_start(rows[:, j, :], slots[bass.ds(e * CAP, CAP), :]).then_inc(row_in[j], 16)
                        if is_live(i, j, HL):
                            m, c = e - HL, (j - HL) % EB
                            act.wait_ge(h_done, m + 1)
                            wait_count(act, y_done, m - EB + 1)
                            for k in range(HC):
                                a = nc.scalar.activation(hT[:, c, k, :], psum[:, 1 + c % 2, CAP * k:CAP * (k + 1)],
                                                         ACT.Relu, bias=b1T[:, bass.ds(m * HC + k, 1)])
                            a.then_inc(hT_kept, 1)
                        for k in (2 * j, 2 * j + 1):
                            ahead.keep(act, i, k)
                steps(act, step)

            @block.tensor
            def _(pe):
                def step(i):
                    for j in range(EB):
                        e = EB * i + j
                        if is_live(i, j, 0):
                            pe.wait_ge(row_in[j], 16 * (i + 1))
                            wait_count(pe, rowsT_kept, e)
                            nc.tensor.transpose(psum[:, 0, 0:CAP], rows[:, j, :], st.ident).then_inc(turned, 1)
                        if is_live(i, j, HL):
                            m, c = e - HL, (j - HL) % EB
                            pe.wait_ge(rowsT_kept, m + 1)
                            pe.wait_ge(w_in[c], 48 * (i + (0 if j >= HL else -1) + 1))
                            wait_count(pe, hT_kept, m - 1)
                            for k in range(HC):
                                mm = nc.tensor.matmul(psum[:, 1 + c % 2, CAP * k:CAP * (k + 1)],
                                                      w1[:, c, PT * k:PT * (k + 1)], rowsT[:, c, :],
                                                      start=True, stop=True)
                            mm.then_inc(h_done, 1)
                        if is_live(i, j, YL):
                            m, c = e - YL, (j - YL) % EB
                            pe.wait_ge(hT_kept, m + 1)
                            wait_count(pe, y_kept, m)
                            for k in range(HC):
                                nc.tensor.matmul(psum[:, 3, 0:D], hT[:, c, k, :], w2[:, c, k, :],
                                                 start=(k == 0), stop=False)
                            nc.tensor.matmul(psum[:, 3, 0:D], cst["ones"][0:1, :], b2[:, c, :],
                                             start=False, stop=True).then_inc(y_done, 1)
                        for k in (2 * j, 2 * j + 1):
                            ahead.project(pe, i, k)
                steps(pe, step)

            @block.vector
            def _(dve):
                def step(i):
                    for j in range(EB):
                        e = EB * i + j
                        if is_live(i, j, 0):
                            dve.wait_ge(turned, e + 1)
                            wait_count(dve, h_done, e - EB + 1)
                            nc.vector.tensor_copy(rowsT[:, j, :], psum[:, 0, 0:CAP]).then_inc(rowsT_kept, 1)
                        if is_live(i, j, YL):
                            m, c = e - YL, (j - YL) % EB
                            dve.wait_ge(y_done, m + 1)
                            wait_count(dve, y_stored[c], 16 * (i + (0 if j >= YL else -1)))
                            nc.vector.tensor_copy(y[:, c, :], psum[:, 3, 0:D]).then_inc(y_kept, 1)
                steps(dve, step)

            @block.gpsimd
            def _(pool):
                def step(i):
                    for j in range(EB):
                        if is_live(i, j, YL):
                            m, c = EB * i + j - YL, (j - YL) % EB
                            pool.wait_ge(y_kept, m + 1)
                            pool.dma_start(answers[bass.ds(m * CAP, CAP), :], y[:, c, :]).then_inc(y_stored[c], 16)
                steps(pool, step)
                for c in range(2):
                    pool.wait_ge(y_stored[c], 16 * NE // EB)

        clear_counts(nc, ahead.sems)
        ahead.first, ahead.count, ahead.per = *GATHER_AHEAD, 4
        with nc.Block() as block:

            @block.sync
            def _(sp):
                ahead.run(sp, ahead.load)
                ahead.finish(sp)

            @block.scalar
            def _(act):
                ahead.run(act, ahead.keep)

            @block.tensor
            def _(pe):
                ahead.run(pe, ahead.project)

            @block.gpsimd
            def _(pool):
                for t in range(NT):
                    nc.gpsimd.indirect_dma_start(
                        out=back[:, t, :], out_offset=None, in_=answers,
                        in_offset=bass.IndirectOffsetOnAxis(ap=src[:, t:t + 1], axis=0)).then_inc(gathered, 16)
                pool.wait_ge(gathered, 16 * NT)

            @block.vector
            def _(dve):
                dve.wait_ge(gathered, 16 * NT)
                for t in range(NT):
                    nc.vector.scalar_tensor_tensor(x[:, t, :], back[:, t, :], r[:, 7, t:t + 1], x[:, t, :],
                                                   ALU.mult, ALU.add)
        clear_counts(nc, sems + ahead.sems)


def conv_cross_attention(nc, st):
    psum, cst, x, qT = st.psum, st.cst, st.x, st.qT
    with ExitStack() as ctx:
        sb = lambda n, shape, dt=F32: ctx.enter_context(nc.sbuf_tensor("d_" + n, shape, dt))
        sems = []

        def sem(n):
            sems.append(ctx.enter_context(nc.semaphore("d_" + n)))
            return sems[-1]

        mask_dram = nc.dram_tensor("mask_parts_dram", (B, 3, S), BF16).ap()
        vleft_dram = nc.dram_tensor("vleft_dram", (B, HG, D), F32).ap()
        wo = st.w["L1_xattn_Wo"]
        wv = [st.convw[:, 2, t, :] for t in range(3)]
        womask = sb("womask", [PT, HG, D])
        ones3 = sb("ones3", [3, PT], BF16)
        out_bias = sb("out_bias", [1, D])

        last_in = sb("last_in", [B, 2, D])
        lastT = sb("lastT", [PT, 2, B])
        vleft = sb("vleft", [B, HG, D])
        mask = sb("mask", [B, S])
        parts = sb("parts", [B, 3, S], BF16)
        pre_in, mask_step, mask_stored, last_turned, last_kept, vleft_done, vleft_kept, vleft_stored, ones_done = map(
            sem, ("pre_in", "mask_step", "mask_stored", "last_turned", "last_kept", "vleft_done", "vleft_kept",
                  "vleft_stored", "ones_done"))
        with nc.Block() as block:

            @block.sync
            def _(sp):
                sp.dma_start(last_in[:], st.ctx[:, S - 2:S, :]).then_inc(pre_in, 16)
                sp.dma_start(mask[:], st.dram["mask_Bx1x1xS2_ff0"].rearrange("b o u s -> (b o u) s")
                             ).then_inc(pre_in, 16)
                sp.wait_ge(mask_step, 6)
                sp.dma_start(mask_dram, parts[:]).then_inc(mask_stored, 16)
                sp.wait_ge(vleft_kept, 1)
                sp.dma_start(vleft_dram, vleft[:]).then_inc(vleft_stored, 16)
                sp.wait_ge(mask_stored, 16)
                sp.wait_ge(vleft_stored, 16)

            @block.gpsimd
            def _(pool):
                nc.gpsimd.memset(ones3[:], 1.0)
                for h in range(HG):
                    nc.gpsimd.tensor_scalar(womask[:, h, :], wo, cst["head4"][:, h:h + 1], None, ALU.mult)

            @block.tensor
            def _(pe):
                pe.wait_ge(pre_in, 32)
                for r in range(2):
                    mm = nc.tensor.transpose(psum[:, 0, B * r:B * (r + 1)], last_in[:, r, :], cst["ident"][0:B, 0:B])
                mm.then_inc(last_turned, 1)
                nc.tensor.matmul(psum[0:1, 2, 0:D], st.col["L1_xattn_bv"], wo, start=True, stop=True)
                pe.wait_ge(last_kept, 1)
                for r in range(2):
                    mm = nc.tensor.matmul(psum[0:B, 1, 0:D], lastT[:, r, :], wv[r], start=(r == 0), stop=(r == 1))
                mm.then_inc(vleft_done, 1)

            @block.vector
            def _(dve):
                dve.wait_ge(pre_in, 32)
                nc.vector.tensor_scalar(mask[:], mask[:], -1e9, None, ALU.mult).then_inc(mask_step, 1)
                for k in range(3):
                    dve.wait_ge(mask_step, 2 * k + 1)
                    nc.vector.tensor_copy(parts[:, k, :], mask[:]).then_inc(mask_step, 1)
                    if k < 2:
                        dve.wait_ge(mask_step, 2 * k + 2)
                        nc.vector.tensor_tensor(mask[:], mask[:], parts[:, k, :], ALU.subtract).then_inc(mask_step, 1)
                dve.wait_ge(last_turned, 1)
                nc.vector.tensor_copy(lastT[:], psum[:, 0, 0:2 * B].rearrange("p (r b) -> p r b", r=2)
                                      ).then_inc(last_kept, 1)
                dve.wait_ge(vleft_done, 1)
                nc.vector.tensor_tensor(vleft[:], psum[0:B, 1, 0:D].unsqueeze(1).broadcast_to([B, HG, D]),
                                        cst["own_group"][0:B, :].rearrange("p (g d) -> p g d", g=HG), ALU.mult
                                        ).then_inc(vleft_kept, 1)
                nc.vector.tensor_tensor(out_bias[:], psum[0:1, 2, 0:D], st.row["L1_xattn_bo"], ALU.add)

        HALF = HG // 2
        vl = sb("vl", [HG, 4, D])
        mp = sb("mp", [3, 4, S], BF16)
        v = sb("v", [PT, 4, SF * D])
        qbd = sb("qbd", [PT, 2, NH, L])
        prob = sb("prob", [PT, 2, HG, S])
        ntop = sb("ntop", [PT, 2, HG])
        total = sb("total", [PT, 2, HG])
        inv = sb("inv", [PT, 2, HG])
        invrep = sb("invrep", [PT, 2, HG, 32])
        pT = sb("pT", [PT, 2, 2, HALF, SF, PT])
        plT = sb("plT", [HG, 2, PT])
        scale = sb("scale", [PT, 2, PT])
        attn = sb("attn", [PT, HG, TPB, L])
        load_done = [sem(f"load_done{k}") for k in range(4)]
        (qbd_done, inv_done, invrep_done, turned_l, plT_kept, pv_done, scale_kept, attn_done, o_done, x_done
         ) = map(sem, ("qbd_done", "inv_done", "invrep_done", "turned_l", "plT_kept", "pv_done", "scale_kept",
                       "attn_done", "o_done", "x_done"))
        s_done, ntop_done, exp_done, turned, pT_kept = (
            [sem(f"{n}{a}") for a in range(2)] for n in ("s_done", "ntop_done", "exp_done", "turned", "pT_kept"))
        T_BANK, A_BANK, O_BANK = 4, 6, 7
        LEFT_AT = PT
        TL, PV, NORM = 1, 2, 3
        steps = lambda eng, step: tile_steps(eng, step, 2, 1)

        with nc.Block() as block:

            @block.sync
            def _(sp):
                def step(i):
                    for j in range(TPB):
                        n = TPB * i + j
                        if live(i, j, 0):
                            wait_count(sp, pv_done, n - 3)
                            sp.dma_start(v[:, j, :], st.v_dram[n]).then_inc(load_done[j], 16)
                            sp.dma_start(vl[:, j, :], vleft_dram[n]).then_inc(load_done[j], 16)
                            sp.dma_start(mp[:, j, :], mask_dram[n]).then_inc(load_done[j], 16)
                steps(sp, step)

            @block.gpsimd
            def _(pool):
                def step(i):
                    for j in range(TPB):
                        n = TPB * i + j
                        if live(i, j, 0):
                            wait_count(pool, s_done[1], n - 1)
                            nc.gpsimd.tensor_tensor(
                                qbd[:, j % 2], qT[:, bass.ds(n * L, L)].unsqueeze(1).broadcast_to([PT, NH, L]),
                                cst["head16"].unsqueeze(2).broadcast_to([PT, NH, L]), ALU.mult).then_inc(qbd_done, 1)
                        if live(i, j, TL):
                            m, c = n - TL, (j - TL) % 2
                            pool.wait_ge(inv_done, m + 1)
                            wait_count(pool, pv_done, m - 1)
                            nc.gpsimd.tensor_tensor(invrep[:, c], inv[:, c].unsqueeze(2).broadcast_to([PT, HG, 32]),
                                                    cst["ones"].rearrange("p (g r) -> p g r", g=HG), ALU.mult
                                                    ).then_inc(invrep_done, 1)
                steps(pool, step)

            @block.tensor
            def _(pe):
                def step(i):
                    for j in range(TPB):
                        n = TPB * i + j
                        if live(i, j, 0):
                            pe.wait_ge(load_done[j], 48 * (i + 1))
                            pe.wait_ge(qbd_done, n + 1)
                            keys = st.ctx_all[:, bass.ds(n, 1), 0:S].rearrange("p o s -> p (o s)")
                            for a in range(2):
                                wait_count(pe, exp_done[a], n)
                                for g in range(HALF * a, HALF * (a + 1)):
                                    nc.tensor.matmul(psum[:, g, 0:S], qbd[:, j % 2, HG * g:HG * (g + 1), :].rearrange(
                                        "p h l -> p (h l)"), keys, start=True, stop=False)
                                    mm = nc.tensor.matmul(psum[:, g, 0:S], ones3[:], mp[:, j, :],
                                                          start=False, stop=True)
                                mm.then_inc(s_done[a], 1)
                        if j == 3 and live_tile(i, 1):
                            t = i - 1
                            pe.wait_ge(attn_done, 2 * (t + 1))
                            wait_count(pe, plT_kept, n - TL if live(i, j, TL) else B)
                            o = psum[:, O_BANK, 0:D]
                            for h in range(HG):
                                nc.tensor.matmul(o, attn[:, h].rearrange("p b l -> p (b l)"), womask[:, h, :],
                                                 start=(h == 0), stop=False)
                            nc.tensor.matmul(o, cst["ones"][0:1, :], out_bias[:], start=False, stop=True
                                             ).then_inc(o_done, 1)
                        if live(i, j, PV):
                            m, c = n - PV, (j - PV) % 2
                            at = psum[:, A_BANK, 256 * c:256 * c + PT]
                            for a in range(2):
                                pe.wait_ge(pT_kept[a], m + 1)
                            pe.wait_ge(plT_kept, m + 1)
                            if c == 0:
                                wait_count(pe, attn_done, (TPB * i + j - PV) // 2 if isinstance(i, int)
                                           else 2 * i + (j - PV) // 2)
                            nc.tensor.matmul(at, vl[:, (j - PV) % 4, :], plT[:, c, :], start=True, stop=False)
                            for t in range(SF):
                                for g in range(HG):
                                    nc.tensor.matmul(
                                        at[32 * g:32 * (g + 1), :],
                                        v[:, (j - PV) % 4, D * t + 32 * g:D * t + 32 * (g + 1)],
                                        pT[:, c, g // HALF, g % HALF, t, :],
                                        start=False, stop=(t == SF - 1), tile_position=(0, 32 * g))
                            pe.wait_ge(invrep_done, m + 1)
                            nc.tensor.matmul(psum[:, A_BANK, 256 * c + PT:256 * (c + 1)],
                                             invrep[:, c].rearrange("p g r -> p (g r)"), st.ident,
                                             start=True, stop=True).then_inc(pv_done, 1)
                        if live(i, j, TL):
                            m, c = n - TL, (j - TL) % 2
                            for a in range(2):
                                pe.wait_ge(exp_done[a], m + 1)
                                wait_count(pe, pT_kept[a], m)
                                for g in range(HALF):
                                    for t in range(SF):
                                        at = PT * (SF * g + t)
                                        mm = nc.tensor.transpose(psum[:, T_BANK + a, at:at + PT],
                                                                 prob[:, c, HALF * a + g, PT * t:PT * (t + 1)],
                                                                 st.ident)
                                mm.then_inc(turned[a], 1)
                            wait_count(pe, plT_kept, m)
                            if j == 3:
                                wait_count(pe, x_done, i)
                            nc.tensor.transpose(psum[0:HG, O_BANK, LEFT_AT:LEFT_AT + PT], prob[:, c, :, S - 1],
                                                st.ident).then_inc(turned_l, 1)
                steps(pe, step)

            @block.vector
            def _(dve):
                def step(i):
                    for j in range(TPB):
                        n = TPB * i + j
                        if j % 2 == 0 and live(i, j, NORM):
                            m = n - NORM
                            pair = (j - NORM) // 2 % 2
                            count = m // 2 if isinstance(m, int) else 2 * i + (j - NORM) // 2
                            dve.wait_ge(scale_kept, count + 1)
                            if pair == 0:
                                wait_count(dve, o_done, i - 1 if j == 0 else i)
                            both = psum[:, A_BANK, :].rearrange("p (c w) -> p c w", c=2)[:, :, 0:PT]
                            nc.vector.tensor_tensor(
                                attn[:, :, 2 * pair:2 * pair + 2, :].rearrange("p h b l -> p b h l"),
                                both.rearrange("p b (h l) -> p b h l", h=HG),
                                scale[:].rearrange("p b (h l) -> p b h l", h=HG), ALU.mult).then_inc(attn_done, 1)
                        if live(i, j, 0):
                            for a in range(2):
                                dve.wait_ge(s_done[a], n + 1)
                                wait_count(dve, exp_done[a], n - 1)
                                nc.vector.tensor_reduce(ntop[:, j % 2, HALF * a:HALF * (a + 1)],
                                                        psum[:, HALF * a:HALF * (a + 1), 0:S], AX_X, ALU.max,
                                                        negate=True).then_inc(ntop_done[a], 1)
                        if j == 3 and live_tile(i, 1):
                            dve.wait_ge(o_done, i)
                            xt = x[:, bass.ds(i - 1, 1), :].rearrange("p o d -> p (o d)")
                            nc.vector.tensor_tensor(xt, xt, psum[:, O_BANK, 0:D], ALU.add).then_inc(x_done, 1)
                        if live(i, j, TL):
                            m, c = n - TL, (j - TL) % 2
                            for a in range(2):
                                dve.wait_ge(exp_done[a], m + 1)
                            wait_count(dve, invrep_done, m - 1)
                            nc.vector.reciprocal(inv[:, c], total[:, c]).then_inc(inv_done, 1)
                            dve.wait_ge(turned[1], m + 1)
                            wait_count(dve, pv_done, m - 1)
                            nc.vector.tensor_copy(pT[:, c, 1].rearrange("p g t k -> p (g t k)"),
                                                  psum[:, T_BANK + 1, :]).then_inc(pT_kept[1], 1)
                steps(dve, step)

            @block.scalar
            def _(act):
                nc.scalar.preload_act_table(ACT.Exp)

                def step(i):
                    for j in range(TPB):
                        n = TPB * i + j
                        if j % 2 == 0 and live(i, j, NORM):
                            m = n - NORM
                            count = m // 2 if isinstance(m, int) else 2 * i + (j - NORM) // 2
                            act.wait_ge(pv_done, m + 1)
                            wait_count(act, attn_done, count)
                            both = psum[:, A_BANK, :].rearrange("p (c w) -> p c w", c=2)[:, :, PT:2 * PT]
                            nc.scalar.activation(scale[:], both, ACT.Copy).then_inc(scale_kept, 1)
                        if live(i, j, 0):
                            wait_count(act, turned_l, n - 1)
                            wait_count(act, inv_done, n - 1)
                            for a in range(2):
                                act.wait_ge(ntop_done[a], n + 1)
                                for g in range(HALF * a, HALF * (a + 1)):
                                    ins = nc.scalar.activation(prob[:, j % 2, g, :], psum[:, g, 0:S], ACT.Exp,
                                                               bias=ntop[:, j % 2, g:g + 1],
                                                               accum_out=total[:, j % 2, g:g + 1])
                                ins.then_inc(exp_done[a], 1)
                        if live(i, j, TL):
                            m, c = n - TL, (j - TL) % 2
                            act.wait_ge(turned[0], m + 1)
                            wait_count(act, pv_done, m - 1)
                            nc.scalar.activation(pT[:, c, 0].rearrange("p g t k -> p (g t k)"), psum[:, T_BANK, :],
                                                 ACT.Copy).then_inc(pT_kept[0], 1)
                            act.wait_ge(turned_l, m + 1)
                            nc.scalar.activation(plT[:, c, :], psum[0:HG, O_BANK, LEFT_AT:LEFT_AT + PT], ACT.Copy
                                                 ).then_inc(plT_kept, 1)
                steps(act, step)
        clear_counts(nc, sems)


def rope_self_attention(nc, st):
    psum, cst, x = st.psum, st.cst, st.x
    q, rk = st.qT, st.xn_flat
    with ExitStack() as ctx:
        sb = lambda n, shape, dt=F32: ctx.enter_context(nc.sbuf_tensor("e_" + n, shape, dt))
        sems = []

        def sem(n):
            sems.append(ctx.enter_context(nc.semaphore("e_" + n)))
            return sems[-1]

        raw = sb("raw", [PT, 2, TOK])
        womask = sb("womask", [PT, HG, D])
        out_bias = sb("out_bias", [1, D])
        wq, wk, wv, wo = (st.w["L1_attn_" + n] for n in ("wqT", "wkT", "wvT", "woT"))
        layer_norm(nc, st, "n4", products=[([None], [wq], st.col["L1_attn_bq"], DH ** -0.5, raw[:, 0]),
                                           ([None], [wk], st.col["L1_attn_bk"], 1.0, raw[:, 1])])

        by_batch = lambda a: a.rearrange("p (b l) -> p b l", l=L)
        over_b = lambda a, n: a.unsqueeze(1).broadcast_to([PT, n, L])
        rotated, sin_done, cos_done, bias_done = map(sem, ("rotated", "sin_done", "cos_done", "bias_done"))
        sin_part = sb("sin_part", [PT, 2, 512])
        with nc.Block() as block:

            @block.tensor
            def _(pe):
                for k in range(8):
                    wait_count(pe, sin_done, k - 3)
                    nc.tensor.matmul(psum[:, k % 4, :], cst["rotate"], raw[:, k // 4, 512 * (k % 4):512 * (k % 4 + 1)],
                                     start=True, stop=True).then_inc(rotated, 1)
                nc.tensor.matmul(psum[0:1, 4, 0:D], st.col["L1_attn_bv"], wo, start=True, stop=True
                                 ).then_inc(bias_done, 1)

            @block.gpsimd
            def _(pool):
                for k, to in enumerate((q[:], rk)):
                    nc.gpsimd.tensor_tensor(by_batch(to), by_batch(raw[:, k]), over_b(cst["cos"], B), ALU.mult
                                            ).then_inc(cos_done, 1)
                for h in range(HG):
                    nc.gpsimd.tensor_scalar(womask[:, h, :], wo, cst["head4"][:, h:h + 1], None, ALU.mult)

            @block.vector
            def _(dve):
                for k in range(8):
                    to = (q[:], rk)[k // 4][:, 512 * (k % 4):512 * (k % 4 + 1)]
                    dve.wait_ge(rotated, k + 1)
                    nc.vector.tensor_tensor(by_batch(sin_part[:, k % 2]), by_batch(psum[:, k % 4, :]),
                                            over_b(cst["sin"], 16), ALU.mult).then_inc(sin_done, 1)
                    dve.wait_ge(sin_done, k + 1)
                    dve.wait_ge(cos_done, k // 4 + 1)
                    nc.vector.tensor_tensor(to, to, sin_part[:, k % 2], ALU.add)
                dve.wait_ge(bias_done, 1)
                nc.vector.tensor_tensor(out_bias[:], psum[0:1, 4, 0:D], st.row["L1_attn_bo"], ALU.add)

        xs = sb("xs", [PT, 2, PT])
        qs = sb("qs", [PT, 2, PT])
        kbd = sb("kbd", [PT, 2, TPB, NH, L])
        v = sb("v", [PT, 2, D])
        prob = sb("prob", [PT, 2, NH, L])
        pT = sb("pT", [PT, 2, NH * L])
        top = sb("top", [PT, NH])
        total = sb("total", [PT, NH])
        inv = sb("inv", [PT, NH])
        attn = sb("attn", [PT, HG, TPB, L])
        (xs_kept, qs_kept, kbd_done, v_done, v_kept, s_done, top_done, sub_done, exp_done, total_done, inv_done,
         norm_done, pT_done, pv_done, attn_kept, o_done, x_done) = map(sem, (
             "xs_kept", "qs_kept", "kbd_done", "v_done", "v_kept", "s_done", "top_done", "sub_done", "exp_done",
             "total_done", "inv_done", "norm_done", "pT_done", "pv_done", "attn_kept", "o_done", "x_done"))
        pv_open = sem("pv_open")
        V_BANK, A_BANK, O_BANK = 2, 3, 7
        SC, PV, OUT = 1, 2, 3
        is_live = lambda i, j, lag: live(i, j, lag, NT, 2)
        steps = lambda eng, step: tile_steps(eng, step, 2, 2, NT // 2)
        with nc.Block() as block:

            @block.gpsimd
            def _(pool):
                def step(i):
                    for j in range(2):
                        if is_live(i, j, 0):
                            n = 2 * i + j
                            wait_count(pool, s_done, n - 1)
                            for b in range(TPB):
                                ins = nc.gpsimd.tensor_tensor(
                                    kbd[:, j, b], rk[:, bass.ds(n * PT + b * L, L)].unsqueeze(1).broadcast_to(
                                        [PT, NH, L]),
                                    cst["head16"].unsqueeze(2).broadcast_to([PT, NH, L]), ALU.mult)
                            ins.then_inc(kbd_done, 1)
                steps(pool, step)

            @block.tensor
            def _(pe):
                def step(i):
                    for j in range(2):
                        n = 2 * i + j
                        if is_live(i, j, SC):
                            m, c = n - SC, (j - SC) % 2
                            pe.wait_ge(xs_kept, m + 1)
                            wait_count(pe, v_kept, m)
                            nc.tensor.matmul(psum[:, V_BANK, 0:D], xs[:, c], wv, start=True, stop=True
                                             ).then_inc(v_done, 1)
                            pe.wait_ge(kbd_done, m + 1)
                            pe.wait_ge(qs_kept, m + 1)
                            wait_count(pe, sub_done, m - 1)
                            for b in range(TPB):
                                mm = nc.tensor.matmul(psum[32 * b:32 * (b + 1), c, :], qs[:, c, L * b:L * (b + 1)],
                                                      kbd[:, c, b], start=True, stop=True, tile_position=(0, 32 * b))
                            mm.then_inc(s_done, 1)
                        if is_live(i, j, OUT):
                            m = n - OUT
                            pe.wait_ge(attn_kept, m + 1)
                            wait_count(pe, x_done, m)
                            o = psum[:, O_BANK, 0:D]
                            for h in range(HG):
                                nc.tensor.matmul(o, attn[:, h].rearrange("p b l -> p (b l)"), womask[:, h, :],
                                                 start=(h == 0), stop=False)
                            nc.tensor.matmul(o, cst["ones"][0:1, :], out_bias[:], start=False, stop=True
                                             ).then_inc(o_done, 1)
                        if is_live(i, j, PV):
                            m, c = n - PV, (j - PV) % 2
                            pe.wait_ge(pT_done, m + 1)
                            pe.wait_ge(v_kept, m + 1)
                            wait_count(pe, attn_kept, m)
                            pe.sem_inc(pv_open)
                            for g in range(HG):
                                for b in range(TPB):
                                    mm = nc.tensor.matmul(
                                        psum[32 * g:32 * (g + 1), A_BANK + b, 0:PT],
                                        v[32 * b:32 * (b + 1), c, 32 * g:32 * (g + 1)],
                                        pT[32 * b:32 * (b + 1), c, PT * g:PT * (g + 1)],
                                        start=True, stop=True, tile_position=(32 * b, 32 * g))
                            mm.then_inc(pv_done, 1)
                steps(pe, step)

            @block.vector
            def _(dve):
                over_k = lambda a: a.unsqueeze(2).broadcast_to([PT, NH, L])

                def step(i):
                    for j in range(2):
                        n = 2 * i + j
                        if is_live(i, j, SC):
                            m, c = n - SC, (j - SC) % 2
                            sc = psum[:, c, :].rearrange("p (h k) -> p h k", k=L)
                            dve.wait_ge(s_done, m + 1)
                            nc.vector.tensor_reduce(top[:], sc, AX_X, ALU.max).then_inc(top_done, 1)
                            dve.wait_ge(top_done, m + 1)
                            nc.vector.tensor_tensor(prob[:, c], sc, over_k(top[:]), ALU.subtract).then_inc(sub_done, 1)
                            dve.wait_ge(exp_done, m + 1)
                            nc.vector.tensor_reduce(total[:], prob[:, c], AX_X, ALU.add).then_inc(total_done, 1)
                            dve.wait_ge(total_done, m + 1)
                            nc.vector.reciprocal(inv[:], total[:]).then_inc(inv_done, 1)
                            dve.wait_ge(inv_done, m + 1)
                            nc.vector.tensor_tensor(prob[:, c], prob[:, c], over_k(inv[:]), ALU.mult
                                                    ).then_inc(norm_done, 1)
                            dve.wait_ge(norm_done, m + 1)
                            wait_count(dve, pv_done, m - 1)
                            nc.vector.transpose(pT[:, c], prob[:, c].rearrange("p h k -> p (h k)")
                                                ).then_inc(pT_done, 1)
                        if is_live(i, j, OUT):
                            m = n - OUT
                            dve.wait_ge(o_done, m + 1)
                            xt = x[:, bass.ds(m, 1), :].rearrange("p o d -> p (o d)")
                            nc.vector.tensor_tensor(xt, xt, psum[:, O_BANK, 0:D], ALU.add).then_inc(x_done, 1)
                steps(dve, step)

            @block.scalar
            def _(act):
                nc.scalar.preload_act_table(ACT.Exp)

                def step(i):
                    for j in range(2):
                        n = 2 * i + j
                        if is_live(i, j, SC):
                            m, c = n - SC, (j - SC) % 2
                            act.wait_ge(v_done, m + 1)
                            wait_count(act, pv_done, m - 1)
                            nc.scalar.activation(v[:, c], psum[:, V_BANK, 0:D], ACT.Copy).then_inc(v_kept, 1)
                        if is_live(i, j, 0):
                            wait_count(act, v_done, n - 1)
                            nc.scalar.activation(xs[:, j], st.xnT_flat[:, bass.ds(n * PT, PT)], ACT.Copy
                                                 ).then_inc(xs_kept, 1)
                            wait_count(act, s_done, n - 1)
                            nc.scalar.activation(qs[:, j], q[:, bass.ds(n * PT, PT)], ACT.Copy).then_inc(qs_kept, 1)
                        if is_live(i, j, SC):
                            m, c = n - SC, (j - SC) % 2
                            act.wait_ge(sub_done, m + 1)
                            nc.scalar.activation(prob[:, c], prob[:, c], ACT.Exp).then_inc(exp_done, 1)
                        if is_live(i, j, PV):
                            m = n - PV
                            act.wait_ge(pv_done, m + 1)
                            wait_count(act, o_done, m)
                            nc.scalar.activation(attn[:].rearrange("p h b l -> p b h l"),
                                                 psum[:, A_BANK:A_BANK + TPB, 0:PT].rearrange(
                                                     "p b (h l) -> p b h l", h=HG), ACT.Copy).then_inc(attn_kept, 1)
                steps(act, step)
        clear_counts(nc, sems)


def switch_head_ffn(nc, st):
    psum, cst, x = st.psum, st.cst, st.x
    with ExitStack() as ctx:
        sb = lambda n, shape, dt=F32: ctx.enter_context(nc.sbuf_tensor("f_" + n, shape, dt))
        sems = []

        def sem(n):
            sems.append(ctx.enter_context(nc.semaphore("f_" + n)))
            return sems[-1]

        HE = FH * FE
        SCALE = FP ** -0.5
        sel = sb("sel", [PT, 2 * HE])
        qw = sb("qw", [PT, FH * FP])
        kw = sb("kw", [PT, FH * FP])
        vw = sb("vw", [PT, HE, FP])
        ow = sb("ow", [PT, HE, D])
        rs = sb("rs", [PT, 1])
        gate = sb("gate", [PT, 2, 2 * HE])
        w_in = sem("w_in")
        vw_in = [sem(f"vw_in{h}") for h in range(FH)]
        ow_in = [sem(f"ow_in{h}") for h in range(FH)]

        sel_in, logits_done, prob_done = map(sem, ("sel_in", "logits_done", "prob_done"))
        routing = st.xn_flat
        with nc.Block() as block:

            @block.sync
            def _(sp):
                sp.dma_start(sel[:, 0:HE], st.dram["L1_ffn_sel_v_wT"]).then_inc(sel_in, 16)
                sp.dma_start(sel[:, HE:2 * HE], st.dram["L1_ffn_sel_o_wT"]).then_inc(sel_in, 16)
                sp.dma_start(rs[:], st.dram["L1_ffn_route_scale"].rearrange("(o n) -> o n", o=1)
                             .broadcast_to([PT, 1])).then_inc(sel_in, 16)
                sp.dma_start(qw[:], st.dram["L1_ffn_q_wT"]).then_inc(w_in, 16)
                sp.dma_start(kw[:], st.dram["L1_ffn_k_wT"]).then_inc(w_in, 16)
                for h in range(FH):
                    of_head = slice(FE * h, FE * (h + 1))
                    sp.dma_start(vw[:, of_head], st.dram["L1_ffn_v_w"][of_head].rearrange("e d p -> d e p")
                                 ).then_inc(vw_in[h], 16)
                for h in range(FH):
                    of_head = slice(FE * h, FE * (h + 1))
                    sp.dma_start(ow[:, of_head], st.dram["L1_ffn_o_w"][of_head].rearrange("e p d -> p e d")
                                 ).then_inc(ow_in[h], 16)

            @block.tensor
            def _(pe):
                pe.wait_ge(sel_in, 48)
                for t in range(NT):
                    mm = nc.tensor.matmul(psum[:, t // 4, PT * (t % 4):PT * (t % 4 + 1)],
                                          st.xnT_flat[:, PT * t:PT * (t + 1)], sel[:], start=True, stop=True)
                    if t % 4 == 3:
                        mm.then_inc(logits_done, 1)

            @block.scalar
            def _(act):
                nc.scalar.preload_act_table(ACT.Sigmoid)
                for k in range(4):
                    act.wait_ge(logits_done, k + 1)
                    nc.scalar.activation(routing[:, 512 * k:512 * (k + 1)], psum[:, k, :], ACT.Sigmoid
                                         ).then_inc(prob_done, 1)

        xs = sb("xs", [PT, PT])
        qk = sb("qk", [PT, 2, 2, PT])
        prob = sb("prob", [PT, FH, L])
        pT = sb("pT", [PT, FH, L])
        pbd = sb("pbd", [PT, 2, FH, PT])
        top = sb("top", [PT, FH])
        total = sb("total", [PT, FH])
        inv = sb("inv", [PT, FH])
        scaled = sb("scaled", [PT, 2, FE, FP])
        half = sb("half", [PT, 4, FP])
        v = sb("v", [PT, 4, FP])
        cT = sb("cT", [PT, PT])
        acc = sb("acc", [PT, 4, D])
        pair = sb("pair", [PT, 2, D])
        RH = 2 * FH
        prob_of = sb("prob_of", [PT, RH, FE])
        cand = sb("cand", [PT, RH, FE])
        picked = sb("picked", [PT, RH, FE])
        best = sb("best", [PT, 2, RH])
        first = sb("first", [PT, RH])
        weight = sb("weight", [PT, RH])
        GATE_STEPS = 19
        gate_step = sem("gate_step")
        (zeroed, xs_kept, qk_done, qk_kept, s_done, top_done, sub_done, exp_done, total_done,
         inv_done, norm_done, pT_done, pbd_done, v_done, v_scaled, v_half, v_quarter, v_kept, c_done, c_kept,
         o_done, o_weighed, pair_done, x_done) = map(sem, (
             "zeroed", "xs_kept", "qk_done", "qk_kept", "s_done", "top_done", "sub_done",
             "exp_done", "total_done", "inv_done", "norm_done", "pT_done", "pbd_done", "v_done", "v_scaled", "v_half",
             "v_quarter", "v_kept", "c_done", "c_kept", "o_done", "o_weighed", "pair_done", "x_done"))
        V_BANK, O_BANK, QK_BANK, C_BANK = 0, 2, 4, 6
        S_BANK = (5, 7)
        SC, VL, CL = 1, 8, 11
        PER = 2 * FH
        TOTAL = NT * FH
        is_live = lambda i, k, lag: live(i, k, lag, TOTAL, PER)
        steps = lambda eng, step: tile_steps(eng, step, 1, 1, NT // 2)

        with nc.Block() as block:

            @block.tensor
            def _(pe):
                def step(i):
                    for k in range(PER):
                        s = PER * i + k
                        if is_live(i, k, CL):
                            n, h = s - CL, (k - CL) % FH
                            par = (k - CL) // FH % 2
                            if h == 0:
                                pe.wait_ge(pbd_done, 4 * (2 * i + (k - CL) // FH + 1))
                            pe.wait_ge(v_kept, n + 1)
                            wait_count(pe, c_kept, n)
                            nc.tensor.matmul(psum[:, C_BANK, 0:PT], v[:, (k - CL) % 4], pbd[:, par, h],
                                             start=True, stop=True).then_inc(c_done, 1)
                        if is_live(i, k, VL):
                            n, h = s - VL, (k - VL) % FH
                            if h == 0:
                                pe.wait_ge(xs_kept, 2 * i + (k - VL) // FH + 1)
                            if isinstance(i, int) and i == 0:
                                pe.wait_ge(vw_in[h], 16)
                            for f in range(2):
                                wait_count(pe, v_scaled, 2 * n + f - 1)
                                nc.tensor.matmul(psum[:, V_BANK + f, :], xs[:],
                                                 vw[:, FE * h + 4 * f:FE * h + 4 * (f + 1), :],
                                                 start=True, stop=True).then_inc(v_done, 1)
                        if is_live(i, k, 0):
                            h = k % FH
                            wait_count(pe, qk_kept, s)
                            if isinstance(i, int) and i == 0 and k == 0:
                                pe.wait_ge(w_in, 32)
                            xt = st.xnT_flat[:, bass.ds((2 * i + k // FH) * PT, PT)]
                            nc.tensor.matmul(psum[:, QK_BANK, 0:PT], qw[:, FP * h:FP * (h + 1)], xt,
                                             start=True, stop=True)
                            nc.tensor.matmul(psum[:, QK_BANK, PT:2 * PT], kw[:, FP * h:FP * (h + 1)], xt,
                                             start=True, stop=True).then_inc(qk_done, 1)
                        if is_live(i, k, SC):
                            n, h = s - SC, (k - SC) % FH
                            c = (k - SC) % 2
                            par = (k - SC) // FH % 2
                            pe.wait_ge(qk_kept, n + 1)
                            if h == 0:
                                wait_count(pe, sub_done, 2 * i + (k - SC) // FH - 1)
                            for b in range(TPB):
                                mm = nc.tensor.matmul(psum[32 * b:32 * (b + 1), S_BANK[par], L * h:L * (h + 1)],
                                                      qk[:, c, 0, L * b:L * (b + 1)], qk[:, c, 1, L * b:L * (b + 1)],
                                                      start=True, stop=True, tile_position=(0, 32 * b))
                            mm.then_inc(s_done, 1)
                        if is_live(i, k, CL):
                            n, h = s - CL, (k - CL) % FH
                            if isinstance(n, int) and n < FH or not isinstance(n, int) and k < CL:
                                pe.wait_ge(ow_in[h], 16)
                            pe.wait_ge(c_kept, n + 1)
                            for f in range(2):
                                wait_count(pe, o_weighed, FE * (n - 1) + 4 * (f + 1))
                                nc.tensor.matmul(psum[:, O_BANK + f, :], cT[:],
                                                 ow[:, FE * h + 4 * f:FE * h + 4 * (f + 1), :],
                                                 start=True, stop=True).then_inc(o_done, 1)
                steps(pe, step)

            @block.scalar
            def _(act):
                nc.scalar.preload_act_table(ACT.Exp)

                def step(i):
                    for k in range(PER):
                        s = PER * i + k
                        if is_live(i, k, CL):
                            n = s - CL
                            act.wait_ge(c_done, n + 1)
                            wait_count(act, o_done, 2 * n)
                            nc.scalar.activation(cT[:], psum[:, C_BANK, 0:PT], ACT.Copy).then_inc(c_kept, 1)
                        if is_live(i, k, VL):
                            n, h = s - VL, (k - VL) % FH
                            t = 2 * i + (k - VL) // FH
                            if h == 0:
                                wait_count(act, v_done, 2 * n)
                                nc.scalar.activation(xs[:], st.xnT_flat[:, bass.ds(t * PT, PT)], ACT.Copy
                                                     ).then_inc(xs_kept, 1)
                                act.wait_ge(gate_step, GATE_STEPS * (t + 1))
                            wait_count(act, v_half, n - 1)
                            for f in range(2):
                                act.wait_ge(v_done, 2 * n + f + 1)
                                for e in range(4 * f, 4 * (f + 1)):
                                    a = nc.scalar.activation(scaled[:, (k - VL) % 2, e, :],
                                                             psum[:, V_BANK + f, FP * (e % 4):FP * (e % 4 + 1)],
                                                             ACT.Copy, scale=gate[:, (k - VL) // FH % 2, FE * h + e:FE * h + e + 1])
                                a.then_inc(v_scaled, 1)
                        if is_live(i, k, 0):
                            act.wait_ge(qk_done, s + 1)
                            wait_count(act, s_done, s - 1)
                            nc.scalar.activation(qk[:, k % 2].rearrange("p a t -> p (a t)"),
                                                 psum[:, QK_BANK, 0:2 * PT], ACT.Copy).then_inc(qk_kept, 1)
                        if k % FH == 1 and is_live(i, k, FH + 1):
                            t = 2 * i + (k - FH - 1) // FH
                            act.wait_ge(sub_done, t + 1)
                            nc.scalar.activation(prob[:], prob[:], ACT.Exp, scale=SCALE).then_inc(exp_done, 1)
                        if k % FH == 2 and is_live(i, k, FH + 2):
                            t = 2 * i + (k - FH - 2) // FH
                            par = (k - FH - 2) // FH % 2
                            act.wait_ge(pT_done, t + 1)
                            act.wait_ge(zeroed, 1)
                            wait_count(act, c_done, FH * (t - 1))
                            for b in range(TPB):
                                nc.scalar.activation(pbd[32 * b:32 * (b + 1), par, :, L * b:L * (b + 1)],
                                                     pT[32 * b:32 * (b + 1)], ACT.Copy).then_inc(pbd_done, 1)
                steps(act, step)

            @block.gpsimd
            def _(pool):
                nc.gpsimd.memset(pbd[:], 0.0).then_inc(zeroed, 1)

                def step(i):
                    for k in range(PER):
                        s = PER * i + k
                        if is_live(i, k, VL):
                            n = s - VL
                            c = (k - VL) % 2
                            pool.wait_ge(v_scaled, 2 * n + 2)
                            wait_count(pool, v_kept, n)
                            nc.gpsimd.tensor_tensor(half[:], scaled[:, c, 0:4, :], scaled[:, c, 4:8, :], ALU.add
                                                    ).then_inc(v_half, 1)
                            pool.wait_ge(v_half, n + 1)
                            nc.gpsimd.tensor_tensor(half[:, 0:2, :], half[:, 0:2, :], half[:, 2:4, :], ALU.add
                                                    ).then_inc(v_quarter, 1)
                            pool.wait_ge(v_quarter, n + 1)
                            wait_count(pool, c_done, n - 3)
                            nc.gpsimd.tensor_tensor(v[:, (k - VL) % 4], half[:, 0, :], half[:, 1, :], ALU.add
                                                    ).then_inc(v_kept, 1)
                steps(pool, step)

            @block.vector
            def _(dve):
                over_k = lambda a: a.unsqueeze(2).broadcast_to([PT, FH, L])
                over_e = lambda a: a.unsqueeze(2).broadcast_to([PT, RH, FE])
                rank = cst["rank8"].unsqueeze(1).broadcast_to([PT, RH, FE])

                def make_gates(t, par, part):
                    done = [GATE_STEPS * t + 3 * part + (1 if part else 0)]
                    choice = gate[:, par].rearrange("p (a e) -> p a e", e=FE)

                    def stepped(instruction):
                        done[0] += 1
                        instruction.then_inc(gate_step, 1)

                    def ready():
                        dve.wait_ge(gate_step, done[0])

                    if part == 0:
                        stepped(nc.vector.tensor_copy(prob_of[:].rearrange("p a e -> p (a e)"),
                                                      routing[:, bass.ds(t * 2 * HE, 2 * HE)]))
                        ready()
                        stepped(nc.vector.tensor_reduce(best[:, 0], prob_of[:], AX_X, ALU.max))
                        ready()
                        stepped(nc.vector.tensor_tensor(cand[:], prob_of[:], over_e(best[:, 0]), ALU.is_equal))
                        ready()
                        stepped(nc.vector.tensor_tensor(cand[:], cand[:], rank, ALU.mult))
                    elif part == 1:
                        ready()
                        stepped(nc.vector.tensor_reduce(first[:], cand[:], AX_X, ALU.max))
                        ready()
                        stepped(nc.vector.tensor_tensor(picked[:], cand[:], over_e(first[:]), ALU.is_equal))
                        ready()
                        wait_count(dve, v_scaled, 2 * FH * (t - 1))
                        wait_count(dve, o_weighed, FE * FH * (t - 1))
                        stepped(nc.vector.scalar_tensor_tensor(choice, picked[:], -2.0, prob_of[:],
                                                               ALU.mult, ALU.add))
                    elif part == 2:
                        ready()
                        stepped(nc.vector.tensor_reduce(best[:, 1], choice, AX_X, ALU.max))
                        ready()
                        stepped(nc.vector.tensor_tensor(cand[:], choice, over_e(best[:, 1]), ALU.is_equal))
                        ready()
                        stepped(nc.vector.tensor_tensor(cand[:], cand[:], rank, ALU.mult))
                    elif part == 3:
                        ready()
                        stepped(nc.vector.tensor_reduce(first[:], cand[:], AX_X, ALU.max))
                        ready()
                        stepped(nc.vector.tensor_tensor(cand[:], cand[:], over_e(first[:]), ALU.is_equal))
                        ready()
                        stepped(nc.vector.tensor_tensor(picked[:], picked[:], cand[:], ALU.add))
                    elif part == 4:
                        ready()
                        stepped(nc.vector.tensor_tensor(weight[:], best[:, 0], best[:, 1], ALU.add))
                        ready()
                        stepped(nc.vector.tensor_scalar(weight[:], weight[:], 1e-9, None, ALU.max))
                        ready()
                        stepped(nc.vector.reciprocal(weight[:], weight[:]))
                    else:
                        ready()
                        stepped(nc.vector.tensor_scalar(weight[:], weight[:], rs[:, 0:1], None, ALU.mult))
                        stepped(nc.vector.tensor_tensor(picked[:], picked[:], prob_of[:], ALU.mult))
                        ready()
                        stepped(nc.vector.tensor_tensor(choice, picked[:], over_e(weight[:]), ALU.mult))

                def step(i):
                    for k in range(PER):
                        s = PER * i + k
                        if k % FH == 1 and is_live(i, k, FH + 1):
                            t = 2 * i + (k - FH - 1) // FH
                            par = (k - FH - 1) // FH % 2
                            sc = psum[:, S_BANK[par], 0:FH * L].rearrange("p (h k) -> p h k", k=L)
                            dve.wait_ge(s_done, FH * (t + 1))
                            nc.vector.tensor_reduce(top[:], sc, AX_X, ALU.max).then_inc(top_done, 1)
                            dve.wait_ge(top_done, t + 1)
                            wait_count(dve, pT_done, t)
                            nc.vector.tensor_tensor(prob[:], sc, over_k(top[:]), ALU.subtract).then_inc(sub_done, 1)
                        if is_live(i, k, CL):
                            n, h = s - CL, (k - CL) % FH
                            t = 2 * i + (k - CL) // FH
                            for f in range(2):
                                dve.wait_ge(o_done, 2 * n + f + 1)
                                for e in range(4 * f, 4 * (f + 1)):
                                    part = psum[:, O_BANK + f, D * (e % 4):D * (e % 4 + 1)]
                                    g = gate[:, (k - CL) // FH % 2, HE + FE * h + e:HE + FE * h + e + 1]
                                    if h == 0 and f == 0:
                                        wait_count(dve, pair_done, 3 * t)
                                        ins = nc.vector.tensor_scalar(acc[:, e], part, g, None, ALU.mult)
                                    else:
                                        dve.wait_ge(o_weighed, FE * n + e - 3)
                                        ins = nc.vector.scalar_tensor_tensor(acc[:, e % 4], part, g, acc[:, e % 4],
                                                                             ALU.mult, ALU.add)
                                    ins.then_inc(o_weighed, 1)
                            if h == FH - 1:
                                dve.wait_ge(o_weighed, FE * (n + 1))
                                wait_count(dve, x_done, t)
                                nc.vector.tensor_tensor(pair[:], acc[:, 0:2], acc[:, 2:4], ALU.add
                                                        ).then_inc(pair_done, 1)
                                dve.wait_ge(pair_done, 3 * t + 1)
                                nc.vector.tensor_tensor(pair[:, 0], pair[:, 0], pair[:, 1], ALU.add
                                                        ).then_inc(pair_done, 2)
                                dve.wait_ge(pair_done, 3 * t + 3)
                                xt = x[:, bass.ds(t, 1), :].rearrange("p o d -> p (o d)")
                                nc.vector.tensor_tensor(xt, xt, pair[:, 0], ALU.add).then_inc(x_done, 1)
                        if k % FH == 1 and is_live(i, k, FH + 1):
                            t = 2 * i + (k - FH - 1) // FH
                            dve.wait_ge(exp_done, t + 1)
                            nc.vector.tensor_reduce(total[:], prob[:], AX_X, ALU.add).then_inc(total_done, 1)
                            dve.wait_ge(total_done, t + 1)
                            nc.vector.reciprocal(inv[:], total[:]).then_inc(inv_done, 1)
                            dve.wait_ge(inv_done, t + 1)
                            nc.vector.tensor_tensor(prob[:], prob[:], over_k(inv[:]), ALU.mult).then_inc(norm_done, 1)
                            dve.wait_ge(norm_done, t + 1)
                            wait_count(dve, pbd_done, 4 * t)
                            nc.vector.transpose(pT[:].rearrange("p h k -> p (h k)"),
                                                prob[:].rearrange("p h k -> p (h k)")).then_inc(pT_done, 1)
                        if k % FH >= 2 and is_live(i, k, 0):
                            make_gates(2 * i + k // FH, k // FH, k % FH - 2)
                steps(dve, step)
        clear_counts(nc, sems)


WEIGHTS = ["L0_xattn_Wq", "L0_xattn_Wk", "L0_xattn_Wv", "L0_xattn_Wo", "L1_xattn_Wo",
           "L1_attn_wqT", "L1_attn_wkT", "L1_attn_wvT", "L1_attn_woT"]
COLUMNS = ["L0_xattn_bq", "L0_xattn_bk", "L0_xattn_bv", "L1_xattn_bq", "L1_xattn_bk", "L1_xattn_bv",
           "L1_attn_bq", "L1_attn_bk", "L1_attn_bv"]
ROWS = ["L0_xattn_bo", "L1_xattn_bo", "L1_attn_bo"]


def perceiver(nc, ins, out, stop_after=6):
    with ExitStack() as ctx:
        sb = lambda n, shape, dt=F32: ctx.enter_context(nc.sbuf_tensor(n, shape, dt))
        st = State()
        st.dram = ins
        st.ctx = ins["ctx_1024"]
        st.v_dram = nc.dram_tensor("v_dram", (B, PT, SF * D), F32).ap()
        st.x = sb("x", [PT, NT, D])
        st.xn = sb("xn", [PT, NT, D])
        st.xn_flat = st.xn[:].rearrange("p t d -> p (t d)")
        st.xnT_pad = sb("xnT", [PT, B, L + 2])
        st.xnT_flat = st.xnT_pad[:].rearrange("p b l -> p (b l)")[:, 0:TOK]
        st.qT = sb("qT", [PT, TOK])
        st.psum = ctx.enter_context(nc.psum_tensor("psum", [PT, 8, 512], F32))
        consts = sb("consts", [PT, CONST_COLS])
        st.cst = {n: consts[:, a:b] for n, (a, b) in CONST_AT.items()}
        st.ident = st.cst["ident"]
        wall = sb("wall", [PT, len(WEIGHTS), D])
        st.w = {n: wall[:, k, :] for k, n in enumerate(WEIGHTS)}
        cols = sb("cols", [PT, len(COLUMNS)])
        st.col = {n: cols[:, k:k + 1] for k, n in enumerate(COLUMNS)}
        rows = sb("rows", [1, len(ROWS), D])
        st.row = {n: rows[:, k, :] for k, n in enumerate(ROWS)}
        st.convw = sb("convw", [PT, 3, 3, D])
        st.scattered, st.gathered = (ctx.enter_context(nc.semaphore(n)) for n in ("scattered", "gathered"))
        st.y_stored = [ctx.enter_context(nc.semaphore(f"y_stored{k}")) for k in range(EB)]
        st.weights_in = ctx.enter_context(nc.semaphore("weights_in"))
        x_in = ctx.enter_context(nc.semaphore("x_in"))
        pad_done = ctx.enter_context(nc.semaphore("pad_done"))
        stored = ctx.enter_context(nc.semaphore("stored"))
        st.weights_count = 16 * (len(WEIGHTS) + len(COLUMNS) + len(ROWS) + 1 + 3)

        with nc.Block() as block:

            @block.sync
            def _(sp):
                sp.dma_start(st.x[:], ins["x"].rearrange("(t b) l d -> (b l) t d", b=TPB)).then_inc(x_in, 16)
                for k, n in enumerate(WEIGHTS):
                    sp.dma_start(wall[:, k, :], ins[n]).then_inc(st.weights_in, 16)
                for k, n in enumerate(("L1_xattn_Wq", "L1_xattn_Wk", "L1_xattn_Wv")):
                    sp.dma_start(st.convw[:, k], ins[n].rearrange("t i o -> i t o")).then_inc(st.weights_in, 16)
                sp.wait_ge(x_in, 16)

            @block.scalar
            def _(act):
                act.dma_start(consts[:], ins["consts"]).then_inc(st.weights_in, 16)
                for k, n in enumerate(COLUMNS):
                    act.dma_start(cols[:, k:k + 1], ins[n].rearrange("(p o) -> p o", o=1)).then_inc(st.weights_in, 16)
                for k, n in enumerate(ROWS):
                    act.dma_start(rows[:, k, :], ins[n].rearrange("(o d) -> o d", o=1)).then_inc(st.weights_in, 16)

        with ExitStack() as inner:
            st.ctx_all = inner.enter_context(nc.sbuf_tensor("ctx_all", [PT, B, S + 2], F32))
            if stop_after >= 1:
                layer_norm(nc, st, "n0", products=[([None], [st.w["L0_xattn_Wq"]], st.col["L0_xattn_bq"],
                                                    DH ** -0.5, st.qT[:])])
                cross_attention_over_queries(nc, st)
            if stop_after >= 2:
                layer_norm(nc, st, "n1")
                long_convolution(nc, st)
            if stop_after >= 3:
                layer_norm(nc, st, "n2")
                routed_ffn(nc, st)
            if stop_after >= 4:
                layer_norm(nc, st, "n3", padded=True, products=[
                    ([0, 1, 2], [st.convw[:, 0, t, :] for t in range(3)], st.col["L1_xattn_bq"], DH ** -0.5,
                     st.qT[:])])
                conv_cross_attention(nc, st)
        if stop_after >= 5:
            rope_self_attention(nc, st)
        if stop_after >= 6:
            layer_norm(nc, st, "n5")
            switch_head_ffn(nc, st)

        with nc.Block() as block:

            @block.sync
            def _(sp):
                sp.dma_start(out.rearrange("(t b) l d -> (b l) t d", b=TPB), st.x[:]).then_inc(stored, 16)
                sp.wait_ge(stored, 16)


_TURNED = {"L1_attn_wqT": "L1_attn_wq", "L1_attn_wkT": "L1_attn_wk", "L1_attn_wvT": "L1_attn_wv",
           "L1_attn_woT": "L1_attn_wo", "L1_ffn_q_wT": "L1_ffn_q_w", "L1_ffn_k_wT": "L1_ffn_k_w",
           "L1_ffn_sel_v_wT": "L1_ffn_sel_v_w", "L1_ffn_sel_o_wT": "L1_ffn_sel_o_w"}


def build(nc, inputs, stop_after=6):
    arrays, aps = {}, {}
    laid = {n: a for n, a in inputs.items() if n not in _TURNED.values()}
    laid.update({new: np.transpose(np.asarray(inputs[old])) for new, old in _TURNED.items()})
    laid["consts"] = shape_constants()
    for name, a in laid.items():
        a = np.ascontiguousarray(a)
        arrays[f"in_{name}"] = a
        aps[name] = nc.dram_tensor(f"in_{name}", a.shape, mybir.dt.from_np(a.dtype), kind="ExternalInput").ap()
    out = nc.dram_tensor("out_0", (B, L, D), F32, kind="ExternalOutput").ap()
    perceiver(nc, aps, out, stop_after)
    return arrays


def kernel(**inputs):
    import concourse.bacc as _bacc
    from concourse.bass_utils import run_bass_kernel_spmd as _run

    nc = _bacc.Bacc("TRN2", target_bir_lowering=False, num_devices=1)
    arrays = build(nc, inputs)
    return _run(nc, [arrays], core_ids=[0]).results[0]["out_0"]
```

```python
from contextlib import ExitStack
import math

import numpy as np

import concourse.bass as bass
from concourse import mybir

ALU = mybir.AluOpType
ACT = mybir.ActivationFunctionType
F32 = mybir.dt.float32
BF16 = mybir.dt.bfloat16
F32R = mybir.dt.float32r
U32 = mybir.dt.uint32
AX_X = mybir.AxisListType.X

B = 64
L = 32
D = 128
S = 257
NH = 16
DH = D // NH
PT = 128
TPB = PT // L
NT = B // TPB
TOK = B * L
HG = 4
SF = 2
EPS = 1e-5

CONV_AHEAD = (0, 12)
ROUTE_AHEAD = (12, 12)
EXPERT_AHEAD = (24, 32)
GATHER_AHEAD = (56, 8)

NE = 16
CAP = -(-TOK // NE)
HID = 512
HC = HID // PT
EB = 4

FH = 8
FE = 8
FP = 128

CONST_PARTS = [("ident", 128), ("head16", 16), ("head4", 4), ("upto", 128), ("ones", 128), ("head32", 32), ("spread", 4 * 128),
               ("token_row", NT), ("rotate", 128), ("cos", L), ("sin", L), ("own_group", HG * D),
               ("rank16", NE), ("rank8", FE)]
CONST_AT = {}
_at = 0
for _name, _n in CONST_PARTS:
    CONST_AT[_name] = (_at, _at + _n)
    _at += _n
CONST_COLS = _at


def shape_constants():
    c = {}
    p = np.arange(PT)
    c["ident"] = np.eye(PT)
    c["head16"] = (p[:, None] // DH == np.arange(NH)[None, :])
    c["head4"] = ((p[:, None] // DH) % HG == np.arange(HG)[None, :])
    c["upto"] = (p[:, None] <= p[None, :])
    c["ones"] = np.ones((PT, PT))
    c["head32"] = (p[:, None] // DH == np.arange(32)[None, :])
    c["spread"] = np.zeros((4, 32, 4, PT))
    for k in range(4):
        c["spread"][k, :NH, k] = (np.arange(NH)[:, None] == p[None, :] // DH)
    c["spread"] = c["spread"].reshape(PT, 4 * PT)
    c["token_row"] = NE * CAP + PT * np.arange(NT)[None, :] + p[:, None]
    rot = np.zeros((PT, PT))
    for i in range(PT // 2):
        rot[2 * i + 1, 2 * i] = -1.0
        rot[2 * i, 2 * i + 1] = 1.0
    c["rotate"] = rot
    freqs = np.float32(10000.0) ** (np.arange(0, DH, 2, dtype=np.float32) / np.float32(DH))
    angles = np.arange(L, dtype=np.float32)[:, None] / freqs[None, :]
    of_row = (p % DH) // 2
    c["cos"] = np.cos(angles)[:, of_row].T
    c["sin"] = np.sin(angles)[:, of_row].T
    c["own_group"] = np.broadcast_to(
        (np.arange(D)[None, :] // 32 == np.arange(HG)[:, None]).reshape(1, -1), (PT, HG * D))
    c["rank16"] = np.broadcast_to(NE - np.arange(NE)[None, :], (PT, NE))
    c["rank8"] = np.broadcast_to(FE - np.arange(FE)[None, :], (PT, FE))
    return np.concatenate([np.asarray(c[n], np.float32) for n, _ in CONST_PARTS], axis=1)


def wait_count(eng, sem, count):
    if isinstance(count, int) and count <= 0:
        return
    eng.wait_ge(sem, count)


def live(i, j, lag, total=B, per=TPB):
    return not isinstance(i, int) or 0 <= per * i + j - lag < total


def live_tile(i, lag):
    return not isinstance(i, int) or 0 <= i - lag < NT


def tile_steps(eng, step, first=2, tail=2, count=NT):
    for i in range(first):
        step(i)
    with eng.Fori(first, count) as i:
        step(i)
    for i in range(count, count + tail):
        step(i)


def clear_counts(nc, sems):
    nums = sorted(s.num for s in sems)
    runs = []
    for n in nums:
        if runs and runs[-1].stop == n:
            runs[-1] = range(runs[-1].start, n + 1)
        else:
            runs.append(range(n, n + 1))
    with nc.Block() as block:

        @block.gpsimd
        def _(pool):
            for run in runs:
                pool.sem_clear(run)


class State:
    pass


def layer_norm(nc, st, tag, padded=False, products=(), first=False, loads=None, on_group=None, on_scalar=None):
    st.xnT = st.xnT_pad[:, :, 1:L + 1] if padded else st.xnT_flat.rearrange("p (b l) -> p b l", l=L)
    with ExitStack() as ctx:
        stats = ctx.enter_context(nc.sbuf_tensor(f"stats_{tag}", [PT, NT, 6], F32))
        w = ctx.enter_context(nc.sbuf_tensor(f"moments_{tag}", [PT, 8, NT], F32))
        sem = lambda n: st.norm_sem(f"{n}_{tag}")
        stats_done, moment_done, std_done, xn_done, turned, xnT_done, made, kept, pad_done = map(
            sem, ("stats_done", "moment_done", "std_done", "xn_done", "turned", "xnT_done", "made", "kept",
                  "pad_done"))
        G = 4
        mean, var, std, rstd, dif, msum, vsum = (w[:, k, :] for k in range(7))
        x, xn, xnT = st.x, st.xn, st.xnT
        results = [(k, p) for k in range(NT // G) for p in range(len(products))]
        with nc.Block() as block:

            @block.gpsimd
            def _(pool):
                if padded:
                    nc.gpsimd.memset(st.xnT_pad[:, :, 0:1], 0.0).then_inc(pad_done, 1)
                    nc.gpsimd.memset(st.xnT_pad[:, :, L + 1:L + 2], 0.0).then_inc(pad_done, 1)

            @block.sync
            def _(sp):
                if loads:
                    loads(sp)

            @block.vector
            def _(dve):
                for t in range(NT):
                    if first and t % (NT // 2) == 0:
                        dve.wait_ge(st.x_in[2 * t // NT], 16)
                    ins = nc.vector.bn_stats(stats[:, t, :], x[:, t, :])
                ins.then_inc(stats_done, 1)
                dve.wait_ge(stats_done, 1)
                nc.vector.tensor_tensor(msum, stats[:, :, 1], stats[:, :, 4], ALU.add).then_inc(moment_done, 1)
                nc.vector.tensor_tensor(dif, stats[:, :, 1], stats[:, :, 4], ALU.subtract).then_inc(moment_done, 1)
                nc.vector.tensor_tensor(vsum, stats[:, :, 2], stats[:, :, 5], ALU.add).then_inc(moment_done, 1)
                dve.wait_ge(moment_done, 2)
                nc.vector.tensor_scalar(mean, msum, 0.5, None, ALU.mult).then_inc(moment_done, 1)
                nc.vector.scalar_tensor_tensor(var, dif, 0.25, dif, ALU.mult, ALU.mult).then_inc(moment_done, 1)
                dve.wait_ge(moment_done, 3)
                nc.vector.tensor_scalar(vsum, vsum, 1.0 / D, EPS, ALU.mult, ALU.add).then_inc(moment_done, 1)
                dve.wait_ge(moment_done, 6)
                nc.vector.tensor_tensor(var, var, vsum, ALU.add).then_inc(moment_done, 1)
                dve.wait_ge(std_done, 1)
                nc.vector.reciprocal(rstd, std).then_inc(moment_done, 1)
                dve.wait_ge(moment_done, 8)
                for t in range(NT):
                    nc.vector.tensor_scalar(xn[:, t, :], x[:, t, :], mean[:, t:t + 1], rstd[:, t:t + 1],
                                            ALU.subtract, ALU.mult).then_inc(xn_done, 1)
                for n, (k, p) in enumerate(results):
                    _, _, bias, scale, out = products[p]
                    dve.wait_ge(made, n + 1)
                    nc.vector.tensor_scalar(out[:, 512 * k:512 * (k + 1)], st.psum[:, 2 + n % 6, :], bias, scale,
                                            ALU.add, ALU.mult).then_inc(kept, 1)

            @block.scalar
            def _(act):
                if first:
                    st.load_on_scalar(act)
                nc.scalar.preload_act_table(ACT.Sqrt)
                act.wait_ge(moment_done, 7)
                nc.scalar.activation(std, var, ACT.Sqrt).then_inc(std_done, 1)
                for k in range(NT // G):
                    act.wait_ge(turned, k + 1)
                    nc.scalar.activation(xnT[:, 4 * G * k:4 * G * (k + 1), :],
                                         st.psum[:, k % 2, :].rearrange("p (b l) -> p b l", l=L),
                                         ACT.Copy).then_inc(xnT_done, 1)
                if on_scalar:
                    on_scalar(act)

            @block.tensor
            def _(pe):
                def turn(k):
                    pe.wait_ge(xn_done, G * (k + 1))
                    if k >= 2:
                        pe.wait_ge(xnT_done, k - 1)
                    for j in range(G):
                        mm = nc.tensor.transpose(st.psum[:, k % 2, PT * j:PT * (j + 1)], xn[:, G * k + j, :], st.ident)
                    mm.then_inc(turned, 1)

                def multiply(n):
                    k, p = results[n]
                    taps, weights = products[p][0:2]
                    pe.wait_ge(xnT_done, k + 1)
                    wait_count(pe, kept, n - 5)
                    for m, tap in enumerate(taps):
                        src = st.xnT if tap is None else st.xnT_pad[:, :, tap:tap + L]
                        mm = nc.tensor.matmul(st.psum[:, 2 + n % 6, :], weights[m], src[:, 16 * k:16 * (k + 1), :],
                                              start=(m == 0), stop=(m == len(taps) - 1))
                    mm.then_inc(made, 1)

                if padded and products:
                    pe.wait_ge(pad_done, 2)
                if first:
                    pe.wait_ge(st.weights_in, st.weights_count)
                for k in range(NT // G + 1):
                    if k < NT // G:
                        turn(k)
                    if k >= 1:
                        for p in range(len(products)):
                            multiply(len(products) * (k - 1) + p)
                        if on_group:
                            pe.wait_ge(xnT_done, k)
                            on_group(pe, k - 1)


def cross_attention_over_queries(nc, st):
    psum, cst, x = st.psum, st.cst, st.x
    qT = st.qT
    with ExitStack() as ctx:
        sb = lambda n, shape, dt=F32: ctx.enter_context(nc.sbuf_tensor("a_" + n, shape, dt))
        sems = []

        def sem(n):
            sems.append(ctx.enter_context(nc.semaphore("a_" + n)))
            return sems[-1]

        LB = B // 4
        ctx_in = sb("ctx_in", [PT, 4, SF, D])
        ctxT = sb("ctxT", [PT, 4, S + 2])
        kT = sb("kT", [PT, 2, SF * PT])
        v = sb("v", [PT, 4, SF * D])
        vz = sb("vz", [PT, 2, SF * D])
        qbd = sb("qbd", [PT, 2, NH, L])
        prob = sb("prob", [PT, 4, SF * NH, L])
        top = sb("top", [PT, 2, SF * NH])
        total = sb("total", [PT, 2, SF * NH])
        inv = sb("inv", [PT, 2, SF * NH])
        attn = sb("attn", [PT, HG, TPB, L])
        left_in = sb("left_in", [B, D])
        leftT = sb("leftT", [PT, B])
        klT = sb("klT", [PT, B])
        vlT = sb("vlT", [PT, B])
        lprod = sb("lprod", [PT, B, L])
        lprob = sb("lprob", [PT, LB, L])
        ltop = sb("ltop", [PT, LB])
        linv = sb("linv", [PT, LB])
        lattn = sb("lattn", [PT, TOK])
        lstage = sb("lstage", [PT, PT])
        womask = sb("womask", [PT, HG, D])
        bv_rest = sb("bv_rest", [3, D])
        bv_parts = sb("bv_parts", [3, 3, D], BF16)
        bv_sum = sb("bv_sum", [3, 2, D])
        bv3 = sb("bv3", [3, SF, D], BF16)
        ones3 = sb("ones3", [3, PT], BF16)

        wq, wk, wv, wo = (st.w[n] for n in ("L0_xattn_Wq", "L0_xattn_Wk", "L0_xattn_Wv", "L0_xattn_Wo"))
        bk, bvc = st.col["L0_xattn_bk"], st.col["L0_xattn_bv"]

        ph = sb("ph", [PT, 6])
        w = sb("w", [PT, 8])
        re = sb("re", [PT, L + 1])
        im = sb("im", [PT, L + 1])
        t1 = sb("t1", [PT, L])
        t2 = sb("t2", [PT, L])
        filt, past = st.filt, st.past
        ph_in, mag2_done, act_done, scale_done, power_done = map(sem, (
            "ph_in", "mag2_done", "act_done", "scale_done", "power_done"))

        lload, lturn, lkept, lkv, lkv_kept, lprod_done, ls_done, lsm, lsp, latt, bv_step, bias_in = map(
            sem, ("lload", "lturn", "lkept", "lkv", "lkv_kept", "lprod_done", "ls_done", "lsm", "lsp", "latt",
                  "bv_step", "bias_in"))
        lscore = psum[:, 0, :].rearrange("p (b l) -> p b l", l=L)
        with nc.Block() as block:

            @block.sync
            def _(sp):
                sp.dma_start(left_in[:], st.ctx[:, S - 1, :]).then_inc(lload, 16)
                for k, n in enumerate(("phazor", "phazor_init")):
                    sp.dma_start(ph[:, 2 * k:2 * k + 2], st.dram["L0_attn_" + n]).then_inc(ph_in, 16)
                for k, n in enumerate(("last_conv_re", "last_conv_im")):
                    sp.dma_start(ph[:, 4 + k:5 + k], st.dram["L0_attn_" + n].rearrange("(p o) -> p o", o=1)
                                 ).then_inc(ph_in, 16)
                sp.dma_start(bv_rest[:], st.dram["L0_xattn_bv"].rearrange("(o d) -> o d", o=1).broadcast_to([3, D])
                             ).then_inc(bias_in, 16)

            @block.gpsimd
            def _(pool):
                nc.gpsimd.memset(ones3[:], 1.0)
                for c in (0, S + 1):
                    nc.gpsimd.memset(ctxT[:, :, c:c + 1], 0.0)
                pool.wait_ge(st.weights_in, st.weights_count)
                for h in range(HG):
                    nc.gpsimd.tensor_scalar(womask[:, h, :], wo, cst["head4"][:, h:h + 1], None, ALU.mult)

            @block.tensor
            def _(pe):
                pe.wait_ge(lload, 16)
                nc.tensor.transpose(psum[:, 4, 0:B], left_in[:], cst["ident"][0:B, 0:B]).then_inc(lturn, 1)
                pe.wait_ge(lkept, 1)
                nc.tensor.matmul(psum[:, 5, 0:B], wk, leftT[:], start=True, stop=True)
                nc.tensor.matmul(psum[:, 5, B:2 * B], wv, leftT[:], start=True, stop=True).then_inc(lkv, 1)
                pe.wait_ge(lprod_done, 1)
                for k in range(4):
                    mm = nc.tensor.matmul(psum[32 * k:32 * (k + 1), 0, :], cst["head32"],
                                          lprod[:, LB * k:LB * (k + 1), :], start=True, stop=True,
                                          tile_position=(0, 32 * k))
                mm.then_inc(ls_done, 1)
                pe.wait_ge(lsp, 1)
                for k in range(4):
                    nc.tensor.matmul(psum[:, k, :], cst["spread"][:, PT * k:PT * (k + 1)], lprob[:],
                                     start=True, stop=True).then_inc(latt, 1)

            @block.vector
            def _(dve):
                dve.wait_ge(lturn, 1)
                nc.vector.tensor_copy(leftT[:], psum[:, 4, 0:B]).then_inc(lkept, 1)
                dve.wait_ge(lkv, 1)
                nc.vector.tensor_scalar(klT[:], psum[:, 5, 0:B], bk, None, ALU.add).then_inc(lkv_kept, 1)
                nc.vector.tensor_scalar(vlT[:], psum[:, 5, B:2 * B], bvc, None, ALU.add).then_inc(lkv_kept, 1)
                dve.wait_ge(lkv_kept, 2)
                nc.vector.tensor_tensor(lprod[:], qT[:].rearrange("p (b l) -> p b l", l=L),
                                        klT[:].unsqueeze(2).broadcast_to([PT, B, L]), ALU.mult).then_inc(lprod_done, 1)
                dve.wait_ge(ph_in, 64)
                nc.vector.tensor_tensor(w[:, 0:2], ph[:, 0:2], ph[:, 0:2], ALU.mult).then_inc(mag2_done, 1)
                nc.vector.memset(re[:, 0:1], 1.0).then_inc(mag2_done, 1)
                nc.vector.memset(im[:, 0:1], 0.0).then_inc(mag2_done, 1)
                dve.wait_ge(mag2_done, 3)
                nc.vector.tensor_tensor(w[:, 2:3], w[:, 0:1], w[:, 1:2], ALU.add).then_inc(mag2_done, 1)
                dve.wait_ge(bias_in, 16)
                for k in range(3):
                    wait_count(dve, bv_step, 2 * k)
                    nc.vector.tensor_copy(bv_parts[:, k], bv_rest[:]).then_inc(bv_step, 1)
                    dve.wait_ge(bv_step, 2 * k + 1)
                    nc.vector.tensor_tensor(bv_rest[:], bv_rest[:], bv_parts[:, k], ALU.subtract).then_inc(bv_step, 1)
                nc.vector.tensor_scalar(bv_sum[:, 0], bv_parts[:, 0], cst["ident"][0:3, 0:1], None, ALU.mult
                                        ).then_inc(bv_step, 1)
                dve.wait_ge(bv_step, 7)
                nc.vector.scalar_tensor_tensor(bv_sum[:, 1], bv_parts[:, 1], cst["ident"][0:3, 1:2], bv_sum[:, 0],
                                               ALU.mult, ALU.add).then_inc(bv_step, 1)
                dve.wait_ge(bv_step, 8)
                nc.vector.scalar_tensor_tensor(bv_sum[:, 0], bv_parts[:, 2], cst["ident"][0:3, 2:3], bv_sum[:, 1],
                                               ALU.mult, ALU.add).then_inc(bv_step, 1)
                dve.wait_ge(bv_step, 9)
                for t in range(SF):
                    nc.vector.tensor_copy(bv3[:, t], bv_sum[:, 0])
                dve.wait_ge(act_done, 1)
                nc.vector.reciprocal(w[:, 5:6], w[:, 3:4]).then_inc(scale_done, 1)
                dve.wait_ge(act_done, 2)
                dve.wait_ge(scale_done, 1)
                nc.vector.tensor_tensor(w[:, 6:7], w[:, 4:5], w[:, 5:6], ALU.mult).then_inc(scale_done, 1)
                dve.wait_ge(scale_done, 2)
                nc.vector.tensor_scalar(re[:, 1:2], ph[:, 0:1], w[:, 6:7], None, ALU.mult).then_inc(power_done, 1)
                nc.vector.tensor_scalar(im[:, 1:2], ph[:, 1:2], w[:, 6:7], None, ALU.mult).then_inc(power_done, 1)
                done = 2
                m = 1
                while m < L:
                    a, b = re[:, m:m + 1], im[:, m:m + 1]
                    dve.wait_ge(power_done, done)
                    nc.vector.tensor_scalar(t1[:, 0:m], im[:, 1:m + 1], b, None, ALU.mult).then_inc(power_done, 1)
                    nc.vector.tensor_scalar(t2[:, 0:m], im[:, 1:m + 1], a, None, ALU.mult).then_inc(power_done, 1)
                    dve.wait_ge(power_done, done + 2)
                    nc.vector.scalar_tensor_tensor(re[:, m + 1:2 * m + 1], re[:, 1:m + 1], a, t1[:, 0:m],
                                                   ALU.mult, ALU.subtract).then_inc(power_done, 1)
                    nc.vector.scalar_tensor_tensor(im[:, m + 1:2 * m + 1], re[:, 1:m + 1], b, t2[:, 0:m],
                                                   ALU.mult, ALU.add).then_inc(power_done, 1)
                    done += 4
                    m *= 2
                dve.wait_ge(power_done, done)
                nc.vector.tensor_scalar(t1[:], im[:, 0:L], ph[:, 3:4], None, ALU.mult).then_inc(power_done, 1)
                nc.vector.tensor_scalar(t2[:], im[:, 1:L + 1], ph[:, 5:6], None, ALU.mult).then_inc(power_done, 1)
                dve.wait_ge(power_done, done + 2)
                nc.vector.scalar_tensor_tensor(filt[:], re[:, 0:L], ph[:, 2:3], t1[:], ALU.mult, ALU.subtract
                                               ).then_inc(power_done, 1)
                nc.vector.scalar_tensor_tensor(past[:], re[:, 1:L + 1], ph[:, 4:5], t2[:], ALU.mult, ALU.subtract
                                               ).then_inc(power_done, 1)
                dve.wait_ge(power_done, done + 4)
                dve.wait_ge(ls_done, 1)
                nc.vector.tensor_reduce(ltop[:], lscore, AX_X, ALU.max).then_inc(lsm, 1)
                dve.wait_ge(lsm, 1)
                nc.vector.tensor_tensor(lprob[:], lscore, ltop[:].unsqueeze(2).broadcast_to([PT, LB, L]),
                                        ALU.subtract).then_inc(lsm, 1)
                dve.wait_ge(lsm, 3)
                nc.vector.tensor_reduce(ltop[:], lprob[:], AX_X, ALU.add).then_inc(lsm, 1)
                dve.wait_ge(lsm, 4)
                nc.vector.reciprocal(linv[:], ltop[:]).then_inc(lsm, 1)
                dve.wait_ge(lsm, 5)
                nc.vector.tensor_tensor(lprob[:], lprob[:], linv[:].unsqueeze(2).broadcast_to([PT, LB, L]),
                                        ALU.mult).then_inc(lsp, 1)
                for k in range(4):
                    dve.wait_ge(latt, k + 1)
                    nc.vector.tensor_tensor(
                        lattn[:, 512 * k:512 * (k + 1)].rearrange("p (b l) -> p b l", l=L),
                        psum[:, k, :].rearrange("p (b l) -> p b l", l=L),
                        vlT[:, 16 * k:16 * (k + 1)].unsqueeze(2).broadcast_to([PT, 16, L]), ALU.mult)

            @block.scalar
            def _(act):
                act.wait_ge(mag2_done, 4)
                nc.scalar.activation(w[:, 3:4], w[:, 2:3], ACT.Sqrt).then_inc(act_done, 1)
                act.wait_ge(act_done, 1)
                nc.scalar.activation(w[:, 4:5], w[:, 3:4], ACT.Exp, scale=-1.0).then_inc(act_done, 1)
                act.wait_ge(lsm, 2)
                nc.scalar.activation(lprob[:], lprob[:], ACT.Exp).then_inc(lsm, 1)

        load_done = [sem(f"load_done{k}") for k in range(4)]
        store_done = [sem(f"store_done{k}") for k in range(4)]
        (turned, left_put, ctxT_kept, kT_kept, v_done, v_kept, qbd_done, s_done, top_done, sub_done, exp_done,
         total_done, inv_done, vz_done, pv_done, attn_kept, lstage_done, o_done, x_done) = map(sem, (
             "turned", "left_put", "ctxT_kept", "kT_kept", "v_done", "v_kept", "qbd_done", "s_done",
             "top_done", "sub_done", "exp_done", "total_done", "inv_done", "vz_done", "pv_done", "attn_kept",
             "lstage_done", "o_done", "x_done"))
        scores = [psum[:, 0:2, :].rearrange("p t (h l) -> p (t h) l", l=L),
                  psum[:, 2:4, :].rearrange("p t (h l) -> p (t h) l", l=L)]
        T_BANK, KV_BANK, O_BANK, A_BANK = 4, 5, 6, 7
        V_AT = SF * PT
        KV, SC, PV, OUT = 1, 2, 4, 2

        with nc.Block() as block:

            @block.sync
            def _(sp):
                def step(i):
                    for j in range(TPB):
                        n = TPB * i + j
                        if live(i, j, 0):
                            wait_count(sp, turned, n - 3)
                            sp.dma_start(ctx_in[:, j, :, :], st.ctx[n, 0:SF * PT, :].rearrange(
                                "(t p) d -> p t d", p=PT)).then_inc(load_done[j], 16)
                tile_steps(sp, step, 1, 0)

            @block.gpsimd
            def _(pool):
                def step(i):
                    if live_tile(i, OUT):
                        wait_count(pool, o_done, i - OUT)
                        nc.gpsimd.tensor_copy(lstage[:], lattn[:, bass.ds((i - OUT) * PT, PT)]
                                              ).then_inc(lstage_done, 1)
                    for j in range(TPB):
                        if live(i, j, 0):
                            n = TPB * i + j
                            wait_count(pool, v_done, n - 3)
                            wait_count(pool, store_done[j], 16 * i)
                            nc.gpsimd.tensor_copy(ctxT[:, j, S:S + 1], leftT[:, bass.ds(n, 1)]).then_inc(left_put, 1)
                        if live(i, j, KV):
                            n = TPB * i + j - KV
                            wait_count(pool, s_done, n - 1)
                            nc.gpsimd.tensor_tensor(
                                qbd[:, (j - KV) % 2], qT[:, bass.ds(n * L, L)].unsqueeze(1).broadcast_to([PT, NH, L]),
                                cst["head16"].unsqueeze(2).broadcast_to([PT, NH, L]), ALU.mult).then_inc(qbd_done, 1)
                        if live(i, j, PV):
                            n = TPB * i + j - PV
                            pool.wait_ge(inv_done, n + 1)
                            pool.wait_ge(v_kept, n + 1)
                            wait_count(pool, pv_done, n - 1)
                            nc.gpsimd.tensor_tensor(
                                vz[:, (j - PV) % 2].rearrange("p (h d) -> p h d", d=DH),
                                v[:, (j - PV) % 4].rearrange("p (h d) -> p h d", d=DH),
                                inv[:, (j - PV) % 2].unsqueeze(2).broadcast_to([PT, SF * NH, DH]),
                                ALU.mult).then_inc(vz_done, 1)
                tile_steps(pool, step)

            @block.tensor
            def _(pe):
                def step(i):
                    for j in range(TPB):
                        n = TPB * i + j
                        if live(i, j, 0):
                            pe.wait_ge(load_done[j], 16 * (i + 1))
                            wait_count(pe, ctxT_kept, n)
                            for t in range(SF):
                                mm = nc.tensor.transpose(psum[:, T_BANK, PT * t:PT * (t + 1)], ctx_in[:, j, t, :],
                                                         st.ident)
                            mm.then_inc(turned, 1)
                        if live(i, j, SC):
                            m = n - SC
                            pe.wait_ge(kT_kept, m + 1)
                            pe.wait_ge(qbd_done, m + 1)
                            wait_count(pe, sub_done, m - 1)
                            for t in range(SF):
                                mm = nc.tensor.matmul(psum[:, 2 * ((j - SC) % 2) + t, :],
                                                      kT[:, (j - SC) % 2, PT * t:PT * (t + 1)],
                                                      qbd[:, (j - SC) % 2], start=True, stop=True)
                            mm.then_inc(s_done, 1)
                        if live(i, j, KV):
                            m = n - KV
                            c = (j - KV) % 4
                            pe.wait_ge(ctxT_kept, m + 1)
                            wait_count(pe, v_kept, m)
                            nc.tensor.matmul(psum[:, KV_BANK, 0:SF * PT], wk, ctxT[:, c, 1:SF * PT + 1],
                                             start=True, stop=True)
                            nc.tensor.matmul(psum[:, KV_BANK, V_AT:V_AT + SF * D], ones3[:],
                                             bv3[:].rearrange("p t d -> p (t d)"), start=True, stop=False)
                            for t in range(SF):
                                mm = nc.tensor.matmul(psum[:, KV_BANK, V_AT + D * t:V_AT + D * (t + 1)],
                                                      ctxT[:, c, 1 + PT * t:1 + PT * (t + 1)], wv,
                                                      start=False, stop=(t == SF - 1))
                            mm.then_inc(v_done, 1)
                        if live(i, j, PV):
                            m = n - PV
                            c = (j - PV) % 4
                            pe.wait_ge(vz_done, m + 1)
                            if c == 0:
                                wait_count(pe, attn_kept, i - 1)
                            for t in range(SF):
                                for g in range(HG):
                                    mm = nc.tensor.matmul(
                                        psum[32 * g:32 * (g + 1), A_BANK, PT * c:PT * (c + 1)],
                                        vz[:, (j - PV) % 2, D * t + 32 * g:D * t + 32 * (g + 1)],
                                        prob[:, c, NH * t + HG * g:NH * t + HG * (g + 1), :],
                                        start=(t == 0), stop=(t == SF - 1), tile_position=(0, 32 * g))
                            mm.then_inc(pv_done, 1)
                        if j == 1 and live_tile(i, OUT):
                            t = i - OUT
                            pe.wait_ge(attn_kept, t + 1)
                            pe.wait_ge(lstage_done, t + 1)
                            wait_count(pe, x_done, t)
                            o = psum[:, O_BANK, 0:D]
                            for h in range(HG):
                                nc.tensor.matmul(o, attn[:, h], womask[:, h, :], start=(h == 0), stop=False)
                            nc.tensor.matmul(o, lstage[:], wo, start=False, stop=False)
                            nc.tensor.matmul(o, cst["ones"][0:1, :], st.row["L0_xattn_bo"], start=False, stop=True
                                             ).then_inc(o_done, 1)
                tile_steps(pe, step)

            @block.vector
            def _(dve):
                def step(i):
                    for j in range(TPB):
                        n = TPB * i + j
                        if j == 3 and live_tile(i, OUT):
                            dve.wait_ge(o_done, i - OUT + 1)
                            xt = x[:, bass.ds(i - OUT, 1), :].rearrange("p o d -> p (o d)")
                            nc.vector.tensor_tensor(xt, xt, psum[:, O_BANK, 0:D], ALU.add).then_inc(x_done, 1)
                        if live(i, j, SC):
                            m = n - SC
                            sc = scores[(j - SC) % 2]
                            dve.wait_ge(s_done, m + 1)
                            nc.vector.tensor_reduce(top[:, (j - SC) % 2], sc, AX_X, ALU.max).then_inc(top_done, 1)
                        if live(i, j, SC + 1):
                            m = n - SC - 1
                            c = (j - SC - 1) % 4
                            dve.wait_ge(exp_done, m + 1)
                            nc.vector.tensor_reduce(total[:, c % 2], prob[:, c], AX_X, ALU.add).then_inc(total_done, 1)
                        if live(i, j, SC):
                            m = n - SC
                            c = (j - SC) % 4
                            dve.wait_ge(top_done, m + 1)
                            wait_count(dve, pv_done, m - 3)
                            nc.vector.tensor_tensor(prob[:, c], scores[c % 2],
                                                    top[:, c % 2].unsqueeze(2).broadcast_to([PT, SF * NH, L]),
                                                    ALU.subtract).then_inc(sub_done, 1)
                        if live(i, j, SC + 1):
                            m = n - SC - 1
                            c = (j - SC - 1) % 2
                            dve.wait_ge(total_done, m + 1)
                            wait_count(dve, vz_done, m - 1)
                            nc.vector.reciprocal(inv[:, c], total[:, c]).then_inc(inv_done, 1)
                tile_steps(dve, step)

            @block.scalar
            def _(act):
                nc.scalar.preload_act_table(ACT.Exp)

                def step(i):
                    for j in range(TPB):
                        n = TPB * i + j
                        if j == 0 and live_tile(i, OUT):
                            t = i - OUT
                            act.wait_ge(pv_done, TPB * (t + 1))
                            wait_count(act, o_done, t)
                            nc.scalar.activation(attn[:].rearrange("p h b l -> p b h l"), psum[:, A_BANK, :].rearrange(
                                "p (b h l) -> p b h l", b=TPB, h=HG), ACT.Copy).then_inc(attn_kept, 1)
                        if live(i, j, 0):
                            act.wait_ge(turned, n + 1)
                            wait_count(act, v_done, n - 3)
                            wait_count(act, store_done[j], 16 * i)
                            nc.scalar.activation(ctxT[:, j, 1:SF * PT + 1], psum[:, T_BANK, 0:SF * PT], ACT.Copy
                                                 ).then_inc(ctxT_kept, 1)
                        if live(i, j, KV):
                            m = n - KV
                            act.wait_ge(left_put, m + 1)
                            act.wait_ge(ctxT_kept, m + 1)
                            act.dma_start(st.ctx_all[:, bass.ds(m, 1), :].rearrange("p o s -> p (o s)"),
                                          ctxT[:, (j - KV) % 4, :]).then_inc(store_done[(j - KV) % 4], 16)
                            act.wait_ge(v_done, m + 1)
                            wait_count(act, s_done, m - 1)
                            nc.scalar.activation(kT[:, (j - KV) % 2], psum[:, KV_BANK, 0:SF * PT], ACT.Identity,
                                                 bias=bk).then_inc(kT_kept, 1)
                            wait_count(act, vz_done, m - 3)
                            nc.scalar.activation(v[:, (j - KV) % 4], psum[:, KV_BANK, V_AT:V_AT + SF * D], ACT.Copy
                                                 ).then_inc(v_kept, 1)
                        if live(i, j, SC):
                            m = n - SC
                            act.wait_ge(sub_done, m + 1)
                            nc.scalar.activation(prob[:, (j - SC) % 4], prob[:, (j - SC) % 4], ACT.Exp
                                                 ).then_inc(exp_done, 1)
                tile_steps(act, step)
                for k in range(4):
                    act.wait_ge(store_done[k], 16 * NT)
        clear_counts(nc, sems)


class ContextProjection:
    BANKS = 4
    KEEP = 1

    def __init__(self, nc, st, tag, first, count, ctx, per=4):
        self.nc, self.st, self.first, self.count, self.per = nc, st, first, count, per
        sb = lambda n, shape: ctx.enter_context(nc.sbuf_tensor(f"p_{n}_{tag}", shape, F32))
        self.sems = []

        def sem(n):
            self.sems.append(ctx.enter_context(nc.semaphore(f"p_{n}_{tag}")))
            return self.sems[-1]

        self.ctxT = sb("ctxT", [PT, 4, S + 2])
        self.v = sb("v", [PT, 4, SF * D])
        self.load_done = [sem(f"load_done{k}") for k in range(4)]
        self.store_done = [sem(f"store_done{k}") for k in range(4)]
        self.v_done, self.k_done, self.v_kept, self.k_kept = map(sem, ("v_done", "k_done", "v_kept", "k_kept"))

    def is_live(self, i, j, lag=0):
        return live(i, j, lag, self.count, self.per)

    def uses(self, i, j):
        return self.per // 4 * i + j // 4

    def load(self, sp, i, j):
        if self.is_live(i, j):
            m, c = self.per * i + j, j % 4
            wait_count(sp, self.k_done, m - 3)
            sp.dma_start(self.ctxT[:, c, :], self.st.ctx_all[:, bass.ds(self.first + m, 1), :].rearrange(
                "p o s -> p (o s)")).then_inc(self.load_done[c], 16)

    def project(self, pe, i, j):
        if self.is_live(i, j):
            nc, st, m, c = self.nc, self.st, self.per * i + j, j % 4
            bank = self.BANKS + 2 * (j % 2)
            pe.wait_ge(self.load_done[c], 16 * (self.uses(i, j) + 1))
            wait_count(pe, self.v_kept, m - 1)
            for t in range(SF):
                for tap in range(3):
                    mm = nc.tensor.matmul(st.psum[:, bank, D * t:D * (t + 1)],
                                          self.ctxT[:, c, tap + PT * t:tap + PT * (t + 1)], st.convw[:, 2, tap, :],
                                          start=(tap == 0), stop=(tap == 2))
            mm.then_inc(self.v_done, 1)
            wait_count(pe, self.k_kept, m - 1)
            for tap in range(3):
                mm = nc.tensor.matmul(st.psum[:, bank + 1, 0:S], st.convw[:, 1, tap, :], self.ctxT[:, c, tap:tap + S],
                                      start=(tap == 0), stop=(tap == 2))
            mm.then_inc(self.k_done, 1)

    def keep(self, act, i, j):
        if self.is_live(i, j, self.KEEP):
            nc, st, m, c = self.nc, self.st, self.per * i + j - self.KEEP, (j - self.KEEP) % 4
            bank = self.BANKS + 2 * (c % 2)
            act.wait_ge(self.v_done, m + 1)
            wait_count(act, self.store_done[c], 16 * self.uses(i, j - self.KEEP))
            nc.scalar.activation(self.v[:, c, :], st.psum[:, bank, 0:SF * D], ACT.Copy).then_inc(self.v_kept, 1)
            act.wait_ge(self.k_done, m + 1)
            nc.scalar.activation(st.ctx_all[:, bass.ds(self.first + m, 1), 0:S].rearrange("p o s -> p (o s)"),
                                 st.psum[:, bank + 1, 0:S], ACT.Identity, bias=st.col["L1_xattn_bk"]
                                 ).then_inc(self.k_kept, 1)
            act.wait_ge(self.v_kept, m + 1)
            act.dma_start(st.v_dram[bass.ds(self.first + m, 1)].rearrange("o p d -> p (o d)"), self.v[:, c, :]
                          ).then_inc(self.store_done[c], 16)

    def run(self, eng, work):
        def step(i):
            for j in range(4):
                work(eng, i, j)
        tile_steps(eng, step, 1, 1, self.count // 4)

    def finish(self, sp):
        for k in range(4):
            sp.wait_ge(self.store_done[k], 16 * (self.count // 4))


def long_convolution(nc, st):
    x, psum = st.x, st.psum
    with ExitStack() as ctx:
        sb = lambda n, shape, dt=F32: ctx.enter_context(nc.sbuf_tensor("b_" + n, shape, dt))
        sems = []

        def sem(n):
            sems.append(ctx.enter_context(nc.semaphore("b_" + n)))
            return sems[-1]

        filt, past = st.filt, st.past
        y = sb("y", [PT, B, L])
        tap_done, turned, x_done = map(sem, ("tap_done", "turned", "x_done"))
        ahead = ContextProjection(nc, st, "b", CONV_AHEAD[0], CONV_AHEAD[1], ctx)
        with nc.Block() as block:

            @block.sync
            def _(sp):
                ahead.run(sp, ahead.load)
                ahead.finish(sp)

            @block.scalar
            def _(act):
                ahead.run(act, ahead.keep)

            @block.vector
            def _(dve):
                nc.vector.scalar_tensor_tensor(y[:], st.xnT, filt[:, 0:1],
                                               past[:].unsqueeze(1).broadcast_to([PT, B, L]),
                                               ALU.mult, ALU.add).then_inc(tap_done, 1)
                for j in range(1, L):
                    dve.wait_ge(tap_done, j)
                    nc.vector.scalar_tensor_tensor(y[:, :, j:L], st.xnT[:, :, 0:L - j], filt[:, j:j + 1], y[:, :, j:L],
                                                   ALU.mult, ALU.add).then_inc(tap_done, 1)
                for k in range(4):
                    dve.wait_ge(turned, k + 1)
                    xk = x[:, 4 * k:4 * (k + 1), :].rearrange("p t d -> p (t d)")
                    nc.vector.tensor_tensor(xk, xk, psum[:, k, :], ALU.add)

            @block.tensor
            def _(pe):
                ahead.run(pe, ahead.project)
                pe.wait_ge(tap_done, L)
                for k in range(4):
                    for j in range(4):
                        t = 4 * k + j
                        mm = nc.tensor.transpose(psum[:, k, PT * j:PT * (j + 1)],
                                                 y[:, TPB * t:TPB * (t + 1), :].rearrange("p b l -> p (b l)"), st.ident)
                    mm.then_inc(turned, 1)
        clear_counts(nc, sems + ahead.sems)


def routed_ffn(nc, st):
    x, xn, psum, cst = st.x, st.xn, st.psum, st.cst
    with ExitStack() as ctx:
        sb = lambda n, shape, dt=F32: ctx.enter_context(nc.sbuf_tensor("c_" + n, shape, dt))
        sems = []

        def sem(n):
            sems.append(ctx.enter_context(nc.semaphore("c_" + n)))
            return sems[-1]

        scattered, gathered, y_stored = st.scattered, st.gathered, st.y_stored
        slots = nc.dram_tensor("slots_dram", (NE * CAP + TOK, D), F32).ap()
        answers = nc.dram_tensor("answers_dram", (NE * CAP, D), F32).ap()
        wg, bg, b1 = st.wg, st.bg, st.b1
        b1T = sb("b1T", [PT, NE * HC])
        logit = sb("logit", [PT, NT, NE])
        cand = sb("cand", [PT, NT, NE])
        onehot = sb("onehot", [PT, NT, NE])
        before = sb("before", [PT, 2, NT, NE])
        r = sb("r", [PT, 10, NT])
        dst = sb("dst", [PT, NT], U32)
        src = sb("src", [PT, NT], U32)
        back = sb("back", [PT, NT, D])
        w1 = sb("w1", [PT, EB, HID])
        w2 = sb("w2", [PT, EB, HC, D])
        b2 = sb("b2", [1, EB, D])
        rows = sb("rows", [PT, EB, D])
        rowsT = sb("rowsT", [PT, EB, CAP])
        hT = sb("hT", [PT, EB, HC, CAP])
        y = sb("y", [PT, EB, D])
        top, total, gate, first, count, keep, slot, gk, dstf, srcf = (r[:, k, :] for k in range(10))
        over_e = lambda a: a.unsqueeze(2).broadcast_to([PT, NT, NE])

        LOGIT_BANK = 7

        def logits(pe, k):
            for t in range(4 * k, 4 * (k + 1)):
                nc.tensor.matmul(psum[:, LOGIT_BANK, NE * t:NE * (t + 1)], st.xnT_flat[:, PT * t:PT * (t + 1)], wg[:],
                                 start=True, stop=True)

        layer_norm(nc, st, "n2", on_group=logits)
        (zeroed, zero_stored, b1_turned, route, exp_done, count_done, dst_done,
         prefix_done) = map(sem, ("zeroed", "zero_stored", "b1_turned", "route", "exp_done",
                       "count_done", "dst_done", "prefix_done"))
        ahead = ContextProjection(nc, st, "c", ROUTE_AHEAD[0], ROUTE_AHEAD[1], ctx)
        with nc.Block() as block:

            @block.sync
            def _(sp):
                sp.wait_ge(zeroed, 1)
                sp.dma_start(slots[0:NE * CAP, :].rearrange("(p r) d -> p r d", p=PT), back[:]
                             ).then_inc(zero_stored, 16)
                ahead.run(sp, ahead.load)
                ahead.finish(sp)
                sp.wait_ge(zero_stored, 16)

            @block.tensor
            def _(pe):
                nc.tensor.transpose(psum[:, 2, 0:NE * HC], b1[:], cst["ident"][0:NE * HC, 0:NE * HC]
                                    ).then_inc(b1_turned, 1)
                for j in (0, 1):
                    ahead.project(pe, 0, j)
                pe.wait_ge(route, 10)
                nc.tensor.matmul(psum[:, 1, 0:NT * NE], cst["upto"], onehot[:], start=True, stop=False)
                nc.tensor.matmul(psum[:, 1, 0:NT * NE], cst["ones"], before[:, 0], start=False, stop=True
                                 ).then_inc(count_done, 1)
                for j in (2, 3):
                    ahead.project(pe, 0, j)
                with pe.Fori(1, ahead.count // 4) as i:
                    for j in range(4):
                        ahead.project(pe, i, j)

            @block.scalar
            def _(act):
                act.wait_ge(route, 4)
                nc.scalar.activation(logit[:], logit[:], ACT.Exp).then_inc(exp_done, 1)
                act.wait_ge(b1_turned, 1)
                nc.scalar.activation(b1T[:], psum[:, 2, 0:NE * HC], ACT.Copy)
                ahead.run(act, ahead.keep)

            @block.vector
            def _(dve):
                n = [0]

                def counted(instruction):
                    n[0] += 1
                    instruction.then_inc(route, 1)

                flat = lambda a: a.rearrange("p t e -> p (t e)")
                ps = psum[:, LOGIT_BANK, 0:NT * NE].rearrange("p (t e) -> p t e", e=NE)
                counted(nc.vector.tensor_tensor(logit[:], ps, bg[:].unsqueeze(1).broadcast_to([PT, NT, NE]), ALU.add))
                nc.vector.memset(back[:], 0.0).then_inc(zeroed, 1)
                dve.wait_ge(route, 1)
                counted(nc.vector.tensor_reduce(top, logit[:], AX_X, ALU.max))
                dve.wait_ge(route, 2)
                counted(nc.vector.tensor_tensor(logit[:], logit[:], over_e(top), ALU.subtract))
                dve.wait_ge(route, 3)
                counted(nc.vector.scalar_tensor_tensor(cand[:], logit[:], 0.0,
                                                       cst["rank16"].unsqueeze(1).broadcast_to([PT, NT, NE]),
                                                       ALU.is_ge, ALU.mult))
                dve.wait_ge(exp_done, 1)
                counted(nc.vector.tensor_reduce(total, logit[:], AX_X, ALU.add))
                dve.wait_ge(route, 5)
                counted(nc.vector.tensor_reduce(first, cand[:], AX_X, ALU.max))
                dve.wait_ge(route, 6)
                counted(nc.vector.tensor_tensor(onehot[:], cand[:], over_e(first), ALU.is_equal))
                dve.wait_ge(route, 7)
                counted(nc.vector.memset(before[:, 0, 0:1, :], 0.0))
                counted(nc.vector.tensor_copy(before[:, 0, 1:NT, :], onehot[:, 0:NT - 1, :]))
                a = 0
                for k in range(4):
                    m = 1 << k
                    dve.wait_ge(prefix_done, 2 * k) if k else dve.wait_ge(route, 9)
                    nc.vector.tensor_copy(before[:, 1 - a, 0:m, :], before[:, a, 0:m, :]).then_inc(prefix_done, 1)
                    nc.vector.tensor_tensor(before[:, 1 - a, m:NT, :], before[:, a, m:NT, :],
                                            before[:, a, 0:NT - m, :], ALU.add).then_inc(prefix_done, 1)
                    a = 1 - a
                dve.wait_ge(prefix_done, 8)
                counted(nc.vector.reciprocal(gate, total))
                dve.wait_ge(count_done, 1)
                ps = psum[:, 1, 0:NT * NE].rearrange("p (t e) -> p t e", e=NE)
                counted(nc.vector.tensor_tensor(cand[:], ps, onehot[:], ALU.mult))
                dve.wait_ge(route, 11)
                counted(nc.vector.tensor_reduce(count, cand[:], AX_X, ALU.add))
                dve.wait_ge(route, 12)
                counted(nc.vector.tensor_scalar(keep, count, float(CAP), None, ALU.is_le))
                counted(nc.vector.tensor_scalar(slot, first, -float(CAP), float(NE * CAP - 1), ALU.mult, ALU.add))
                dve.wait_ge(route, 14)
                counted(nc.vector.tensor_tensor(slot, slot, count, ALU.add))
                counted(nc.vector.tensor_tensor(gk, gate, keep, ALU.mult))
                dve.wait_ge(route, 16)
                counted(nc.vector.tensor_tensor(dstf, slot, cst["token_row"], ALU.subtract))
                counted(nc.vector.tensor_tensor(srcf, slot, keep, ALU.mult))
                dve.wait_ge(route, 18)
                counted(nc.vector.tensor_tensor(dstf, dstf, keep, ALU.mult))
                nc.vector.tensor_copy(src[:], srcf)
                dve.wait_ge(route, 19)
                counted(nc.vector.tensor_tensor(dstf, dstf, cst["token_row"], ALU.add))
                dve.wait_ge(route, 20)
                nc.vector.tensor_copy(dst[:], dstf).then_inc(dst_done, 1)

            @block.gpsimd
            def _(pool):
                pool.wait_ge(dst_done, 1)
                pool.wait_ge(zero_stored, 16)
                for t in range(NT):
                    nc.gpsimd.indirect_dma_start(
                        out=slots, out_offset=bass.IndirectOffsetOnAxis(ap=dst[:, t:t + 1], axis=0),
                        in_=xn[:, t, :], in_offset=None).then_inc(scattered, 16)
                pool.wait_ge(scattered, 16 * NT)

        clear_counts(nc, ahead.sems)
        ahead.first, ahead.count, ahead.per = *EXPERT_AHEAD, 2 * EB

        row_in = [sem(f"row_in{k}") for k in range(EB)]
        w_in = [sem(f"w_in{k}") for k in range(EB)]
        turned, rowsT_kept, h_done, hT_kept, y_done, y_kept, x_done = map(sem, (
            "turned", "rowsT_kept", "h_done", "hT_kept", "y_done", "y_kept", "x_done"))
        HL, YL = 1, 2
        is_live = lambda i, j, lag: live(i, j, lag, NE, EB)
        steps = lambda eng, step: tile_steps(eng, step, 1, 1, NE // EB)
        with nc.Block() as block:

            @block.sync
            def _(sp):
                def step(i):
                    for j in range(EB):
                        e = EB * i + j
                        if is_live(i, j, 0):
                            wait_count(sp, turned, e - EB + 1)
                            sp.dma_start(rows[:, j, :], slots[bass.ds(e * CAP, CAP), :]).then_inc(row_in[j], 16)
                            wait_count(sp, y_done, e - EB + 1)
                            sp.dma_start(w1[:, j, :], st.dram["L0_ffn_W1"][e]).then_inc(w_in[j], 16)
                            sp.dma_start(w2[:, j], st.dram["L0_ffn_W2"][e].rearrange("(c p) d -> p c d", p=PT)
                                         ).then_inc(w_in[j], 16)
                            sp.dma_start(b2[:, j, :], st.dram["L0_ffn_b2"][bass.ds(e, 1), :]).then_inc(w_in[j], 16)
                        for k in (2 * j, 2 * j + 1):
                            ahead.load(sp, i, k)
                steps(sp, step)
                ahead.finish(sp)

            @block.scalar
            def _(act):
                def step(i):
                    for j in range(EB):
                        e = EB * i + j
                        if is_live(i, j, HL):
                            m, c = e - HL, (j - HL) % EB
                            act.wait_ge(h_done, m + 1)
                            wait_count(act, y_done, m - EB + 1)
                            for k in range(HC):
                                a = nc.scalar.activation(hT[:, c, k, :], psum[:, 1 + c % 2, CAP * k:CAP * (k + 1)],
                                                         ACT.Relu, bias=b1T[:, bass.ds(m * HC + k, 1)])
                            a.then_inc(hT_kept, 1)
                        for k in (2 * j, 2 * j + 1):
                            ahead.keep(act, i, k)
                steps(act, step)

            @block.tensor
            def _(pe):
                def step(i):
                    for j in range(EB):
                        e = EB * i + j
                        if is_live(i, j, 0):
                            pe.wait_ge(row_in[j], 16 * (i + 1))
                            wait_count(pe, rowsT_kept, e)
                            nc.tensor.transpose(psum[:, 0, 0:CAP], rows[:, j, :], st.ident).then_inc(turned, 1)
                        if is_live(i, j, HL):
                            m, c = e - HL, (j - HL) % EB
                            pe.wait_ge(rowsT_kept, m + 1)
                            pe.wait_ge(w_in[c], 48 * (i + (0 if j >= HL else -1) + 1))
                            wait_count(pe, hT_kept, m - 1)
                            for k in range(HC):
                                mm = nc.tensor.matmul(psum[:, 1 + c % 2, CAP * k:CAP * (k + 1)],
                                                      w1[:, c, PT * k:PT * (k + 1)], rowsT[:, c, :],
                                                      start=True, stop=True)
                            mm.then_inc(h_done, 1)
                        if is_live(i, j, YL):
                            m, c = e - YL, (j - YL) % EB
                            pe.wait_ge(hT_kept, m + 1)
                            wait_count(pe, y_kept, m)
                            for k in range(HC):
                                nc.tensor.matmul(psum[:, 3, 0:D], hT[:, c, k, :], w2[:, c, k, :],
                                                 start=(k == 0), stop=False)
                            nc.tensor.matmul(psum[:, 3, 0:D], cst["ones"][0:1, :], b2[:, c, :],
                                             start=False, stop=True).then_inc(y_done, 1)
                        for k in (2 * j, 2 * j + 1):
                            ahead.project(pe, i, k)
                steps(pe, step)

            @block.vector
            def _(dve):
                def step(i):
                    for j in range(EB):
                        e = EB * i + j
                        if is_live(i, j, 0):
                            dve.wait_ge(turned, e + 1)
                            wait_count(dve, h_done, e - EB + 1)
                            nc.vector.tensor_copy(rowsT[:, j, :], psum[:, 0, 0:CAP]).then_inc(rowsT_kept, 1)
                        if is_live(i, j, YL):
                            m, c = e - YL, (j - YL) % EB
                            dve.wait_ge(y_done, m + 1)
                            wait_count(dve, y_stored[c], 16 * (i + (0 if j >= YL else -1)))
                            nc.vector.tensor_copy(y[:, c, :], psum[:, 3, 0:D]).then_inc(y_kept, 1)
                steps(dve, step)

            @block.gpsimd
            def _(pool):
                def step(i):
                    for j in range(EB):
                        if is_live(i, j, YL):
                            m, c = EB * i + j - YL, (j - YL) % EB
                            pool.wait_ge(y_kept, m + 1)
                            pool.dma_start(answers[bass.ds(m * CAP, CAP), :], y[:, c, :]).then_inc(y_stored[c], 16)
                steps(pool, step)
                for c in range(2):
                    pool.wait_ge(y_stored[c], 16 * NE // EB)

        clear_counts(nc, ahead.sems)
        ahead.first, ahead.count, ahead.per = *GATHER_AHEAD, 4
        with nc.Block() as block:

            @block.sync
            def _(sp):
                ahead.run(sp, ahead.load)
                ahead.finish(sp)

            @block.scalar
            def _(act):
                ahead.run(act, ahead.keep)

            @block.tensor
            def _(pe):
                ahead.run(pe, ahead.project)

            @block.gpsimd
            def _(pool):
                for t in range(NT):
                    nc.gpsimd.indirect_dma_start(
                        out=back[:, t, :], out_offset=None, in_=answers,
                        in_offset=bass.IndirectOffsetOnAxis(ap=src[:, t:t + 1], axis=0)).then_inc(gathered, 16)
                pool.wait_ge(gathered, 16 * NT)

            @block.vector
            def _(dve):
                dve.wait_ge(gathered, 16 * NT)
                for t in range(NT):
                    nc.vector.scalar_tensor_tensor(x[:, t, :], back[:, t, :], r[:, 7, t:t + 1], x[:, t, :],
                                                   ALU.mult, ALU.add)
        clear_counts(nc, sems + ahead.sems)


def conv_cross_attention(nc, st):
    psum, cst, x, qT = st.psum, st.cst, st.x, st.qT
    with ExitStack() as ctx:
        sb = lambda n, shape, dt=F32: ctx.enter_context(nc.sbuf_tensor("d_" + n, shape, dt))
        sems = []

        def sem(n):
            sems.append(ctx.enter_context(nc.semaphore("d_" + n)))
            return sems[-1]

        mask_dram = nc.dram_tensor("mask_parts_dram", (B, 3, S), BF16).ap()
        vleft_dram = nc.dram_tensor("vleft_dram", (B, HG, D), F32).ap()
        wo = st.w["L1_xattn_Wo"]
        wv = [st.convw[:, 2, t, :] for t in range(3)]
        womask = sb("womask", [PT, HG, D])
        ones3 = sb("ones3", [3, PT], BF16)
        out_bias = sb("out_bias", [1, D])

        last_in = sb("last_in", [B, 2, D])
        lastT = sb("lastT", [PT, 2, B])
        vleft = sb("vleft", [B, HG, D])
        mask = sb("mask", [B, S])
        parts = sb("parts", [B, 3, S], BF16)
        pre_in, mask_step, mask_stored, last_turned, last_kept, vleft_done, vleft_kept, vleft_stored, ones_done = map(
            sem, ("pre_in", "mask_step", "mask_stored", "last_turned", "last_kept", "vleft_done", "vleft_kept",
                  "vleft_stored", "ones_done"))
        with nc.Block() as block:

            @block.sync
            def _(sp):
                sp.dma_start(last_in[:], st.ctx[:, S - 2:S, :]).then_inc(pre_in, 16)
                sp.dma_start(mask[:], st.dram["mask_Bx1x1xS2_ff0"].rearrange("b o u s -> (b o u) s")
                             ).then_inc(pre_in, 16)
                sp.wait_ge(mask_step, 6)
                sp.dma_start(mask_dram, parts[:]).then_inc(mask_stored, 16)
                sp.wait_ge(vleft_kept, 1)
                sp.dma_start(vleft_dram, vleft[:]).then_inc(vleft_stored, 16)
                sp.wait_ge(mask_stored, 16)
                sp.wait_ge(vleft_stored, 16)

            @block.gpsimd
            def _(pool):
                nc.gpsimd.memset(ones3[:], 1.0)
                for h in range(HG):
                    nc.gpsimd.tensor_scalar(womask[:, h, :], wo, cst["head4"][:, h:h + 1], None, ALU.mult)

            @block.tensor
            def _(pe):
                pe.wait_ge(pre_in, 32)
                for r in range(2):
                    mm = nc.tensor.transpose(psum[:, 0, B * r:B * (r + 1)], last_in[:, r, :], cst["ident"][0:B, 0:B])
                mm.then_inc(last_turned, 1)
                nc.tensor.matmul(psum[0:1, 2, 0:D], st.col["L1_xattn_bv"], wo, start=True, stop=True)
                pe.wait_ge(last_kept, 1)
                for r in range(2):
                    mm = nc.tensor.matmul(psum[0:B, 1, 0:D], lastT[:, r, :], wv[r], start=(r == 0), stop=(r == 1))
                mm.then_inc(vleft_done, 1)

            @block.vector
            def _(dve):
                dve.wait_ge(pre_in, 32)
                nc.vector.tensor_scalar(mask[:], mask[:], -1e9, None, ALU.mult).then_inc(mask_step, 1)
                for k in range(3):
                    dve.wait_ge(mask_step, 2 * k + 1)
                    nc.vector.tensor_copy(parts[:, k, :], mask[:]).then_inc(mask_step, 1)
                    if k < 2:
                        dve.wait_ge(mask_step, 2 * k + 2)
                        nc.vector.tensor_tensor(mask[:], mask[:], parts[:, k, :], ALU.subtract).then_inc(mask_step, 1)
                dve.wait_ge(last_turned, 1)
                nc.vector.tensor_copy(lastT[:], psum[:, 0, 0:2 * B].rearrange("p (r b) -> p r b", r=2)
                                      ).then_inc(last_kept, 1)
                dve.wait_ge(vleft_done, 1)
                nc.vector.tensor_tensor(vleft[:], psum[0:B, 1, 0:D].unsqueeze(1).broadcast_to([B, HG, D]),
                                        cst["own_group"][0:B, :].rearrange("p (g d) -> p g d", g=HG), ALU.mult
                                        ).then_inc(vleft_kept, 1)
                nc.vector.tensor_tensor(out_bias[:], psum[0:1, 2, 0:D], st.row["L1_xattn_bo"], ALU.add)

        HALF = HG // 2
        vl = sb("vl", [HG, 4, D])
        mp = sb("mp", [3, 4, S], BF16)
        v = sb("v", [PT, 4, SF * D])
        qbd = sb("qbd", [PT, 2, NH, L])
        prob = sb("prob", [PT, 2, HG, S])
        ntop = sb("ntop", [PT, 2, HG])
        total = sb("total", [PT, 2, HG])
        inv = sb("inv", [PT, 2, HG])
        invrep = sb("invrep", [PT, 2, HG, 32])
        pT = sb("pT", [PT, 2, 2, HALF, SF, PT])
        plT = sb("plT", [HG, 2, PT])
        scale = sb("scale", [PT, 2, PT])
        attn = sb("attn", [PT, HG, TPB, L])
        load_done = [sem(f"load_done{k}") for k in range(4)]
        (qbd_done, inv_done, invrep_done, turned_l, plT_kept, pv_done, scale_kept, attn_done, o_done, x_done
         ) = map(sem, ("qbd_done", "inv_done", "invrep_done", "turned_l", "plT_kept", "pv_done", "scale_kept",
                       "attn_done", "o_done", "x_done"))
        s_done, ntop_done, exp_done, turned, pT_kept = (
            [sem(f"{n}{a}") for a in range(2)] for n in ("s_done", "ntop_done", "exp_done", "turned", "pT_kept"))
        T_BANK, A_BANK, O_BANK = 4, 6, 7
        LEFT_AT = PT
        TL, PV, NORM = 1, 2, 3
        steps = lambda eng, step: tile_steps(eng, step, 2, 1)

        with nc.Block() as block:

            @block.sync
            def _(sp):
                def step(i):
                    for j in range(TPB):
                        n = TPB * i + j
                        if live(i, j, 0):
                            wait_count(sp, pv_done, n - 3)
                            sp.dma_start(v[:, j, :], st.v_dram[n]).then_inc(load_done[j], 16)
                            sp.dma_start(vl[:, j, :], vleft_dram[n]).then_inc(load_done[j], 16)
                            sp.dma_start(mp[:, j, :], mask_dram[n]).then_inc(load_done[j], 16)
                steps(sp, step)

            @block.gpsimd
            def _(pool):
                def step(i):
                    for j in range(TPB):
                        n = TPB * i + j
                        if live(i, j, 0):
                            wait_count(pool, s_done[1], n - 1)
                            nc.gpsimd.tensor_tensor(
                                qbd[:, j % 2], qT[:, bass.ds(n * L, L)].unsqueeze(1).broadcast_to([PT, NH, L]),
                                cst["head16"].unsqueeze(2).broadcast_to([PT, NH, L]), ALU.mult).then_inc(qbd_done, 1)
                        if live(i, j, PV):
                            m, c = n - PV, (j - PV) % 2
                            pool.wait_ge(inv_done, m + 1)
                            wait_count(pool, pv_done, m - 1)
                            nc.gpsimd.tensor_tensor(invrep[:, c], inv[:, c].unsqueeze(2).broadcast_to([PT, HG, 32]),
                                                    cst["ones"].rearrange("p (g r) -> p g r", g=HG), ALU.mult
                                                    ).then_inc(invrep_done, 1)
                steps(pool, step)

            @block.tensor
            def _(pe):
                def step(i):
                    for j in range(TPB):
                        n = TPB * i + j
                        if live(i, j, 0):
                            pe.wait_ge(load_done[j], 48 * (i + 1))
                            pe.wait_ge(qbd_done, n + 1)
                            keys = st.ctx_all[:, bass.ds(n, 1), 0:S].rearrange("p o s -> p (o s)")
                            for a in range(2):
                                wait_count(pe, exp_done[a], n)
                                for g in range(HALF * a, HALF * (a + 1)):
                                    nc.tensor.matmul(psum[:, g, 0:S], qbd[:, j % 2, HG * g:HG * (g + 1), :].rearrange(
                                        "p h l -> p (h l)"), keys, start=True, stop=False)
                                    mm = nc.tensor.matmul(psum[:, g, 0:S], ones3[:], mp[:, j, :],
                                                          start=False, stop=True)
                                mm.then_inc(s_done[a], 1)
                        if j == 3 and live_tile(i, 1):
                            t = i - 1
                            pe.wait_ge(attn_done, 2 * (t + 1))
                            wait_count(pe, plT_kept, n - TL if live(i, j, TL) else B)
                            o = psum[:, O_BANK, 0:D]
                            for h in range(HG):
                                nc.tensor.matmul(o, attn[:, h].rearrange("p b l -> p (b l)"), womask[:, h, :],
                                                 start=(h == 0), stop=False)
                            nc.tensor.matmul(o, cst["ones"][0:1, :], out_bias[:], start=False, stop=True
                                             ).then_inc(o_done, 1)
                        if live(i, j, PV):
                            m, c = n - PV, (j - PV) % 2
                            at = psum[:, A_BANK, 256 * c:256 * c + PT]
                            for a in range(2):
                                pe.wait_ge(pT_kept[a], m + 1)
                            pe.wait_ge(plT_kept, m + 1)
                            if c == 0:
                                wait_count(pe, attn_done, (TPB * i + j - PV) // 2 if isinstance(i, int)
                                           else 2 * i + (j - PV) // 2)
                            nc.tensor.matmul(at, vl[:, (j - PV) % 4, :], plT[:, c, :], start=True, stop=False)
                            for t in range(SF):
                                for g in range(HG):
                                    nc.tensor.matmul(
                                        at[32 * g:32 * (g + 1), :],
                                        v[:, (j - PV) % 4, D * t + 32 * g:D * t + 32 * (g + 1)],
                                        pT[:, c, g // HALF, g % HALF, t, :],
                                        start=False, stop=(t == SF - 1), tile_position=(0, 32 * g))
                            pe.wait_ge(invrep_done, m + 1)
                            nc.tensor.matmul(psum[:, A_BANK, 256 * c + PT:256 * (c + 1)],
                                             invrep[:, c].rearrange("p g r -> p (g r)"), st.ident,
                                             start=True, stop=True).then_inc(pv_done, 1)
                        if live(i, j, TL):
                            m, c = n - TL, (j - TL) % 2
                            for a in range(2):
                                pe.wait_ge(exp_done[a], m + 1)
                                wait_count(pe, pT_kept[a], m)
                                for g in range(HALF):
                                    for t in range(SF):
                                        at = PT * (SF * g + t)
                                        mm = nc.tensor.transpose(psum[:, T_BANK + a, at:at + PT],
                                                                 prob[:, c, HALF * a + g, PT * t:PT * (t + 1)],
                                                                 st.ident)
                                mm.then_inc(turned[a], 1)
                            wait_count(pe, plT_kept, m)
                            if j == 3:
                                wait_count(pe, x_done, i)
                            nc.tensor.transpose(psum[0:HG, O_BANK, LEFT_AT:LEFT_AT + PT], prob[:, c, :, S - 1],
                                                st.ident).then_inc(turned_l, 1)
                steps(pe, step)

            @block.vector
            def _(dve):
                def step(i):
                    for j in range(TPB):
                        n = TPB * i + j
                        if j % 2 == 0 and live(i, j, NORM):
                            m = n - NORM
                            pair = (j - NORM) // 2 % 2
                            count = m // 2 if isinstance(m, int) else 2 * i + (j - NORM) // 2
                            dve.wait_ge(scale_kept, count + 1)
                            if pair == 0:
                                wait_count(dve, o_done, i - 1 if j == 0 else i)
                            both = psum[:, A_BANK, :].rearrange("p (c w) -> p c w", c=2)[:, :, 0:PT]
                            nc.vector.tensor_tensor(
                                attn[:, :, 2 * pair:2 * pair + 2, :].rearrange("p h b l -> p b h l"),
                                both.rearrange("p b (h l) -> p b h l", h=HG),
                                scale[:].rearrange("p b (h l) -> p b h l", h=HG), ALU.mult).then_inc(attn_done, 1)
                        if live(i, j, 0):
                            for a in range(2):
                                dve.wait_ge(s_done[a], n + 1)
                                wait_count(dve, exp_done[a], n - 1)
                                nc.vector.tensor_reduce(ntop[:, j % 2, HALF * a:HALF * (a + 1)],
                                                        psum[:, HALF * a:HALF * (a + 1), 0:S], AX_X, ALU.max,
                                                        negate=True).then_inc(ntop_done[a], 1)
                        if j == 3 and live_tile(i, 1):
                            dve.wait_ge(o_done, i)
                            xt = x[:, bass.ds(i - 1, 1), :].rearrange("p o d -> p (o d)")
                            nc.vector.tensor_tensor(xt, xt, psum[:, O_BANK, 0:D], ALU.add).then_inc(x_done, 1)
                        if live(i, j, TL):
                            m, c = n - TL, (j - TL) % 2
                            for a in range(2):
                                dve.wait_ge(exp_done[a], m + 1)
                            wait_count(dve, invrep_done, m - 1)
                            nc.vector.reciprocal(inv[:, c], total[:, c]).then_inc(inv_done, 1)
                            dve.wait_ge(turned[1], m + 1)
                            wait_count(dve, pv_done, m - 1)
                            nc.vector.tensor_copy(pT[:, c, 1].rearrange("p g t k -> p (g t k)"),
                                                  psum[:, T_BANK + 1, :]).then_inc(pT_kept[1], 1)
                steps(dve, step)

            @block.scalar
            def _(act):
                nc.scalar.preload_act_table(ACT.Exp)

                def step(i):
                    for j in range(TPB):
                        n = TPB * i + j
                        if j % 2 == 0 and live(i, j, NORM):
                            m = n - NORM
                            count = m // 2 if isinstance(m, int) else 2 * i + (j - NORM) // 2
                            act.wait_ge(pv_done, m + 1)
                            wait_count(act, attn_done, count)
                            both = psum[:, A_BANK, :].rearrange("p (c w) -> p c w", c=2)[:, :, PT:2 * PT]
                            nc.scalar.activation(scale[:], both, ACT.Copy).then_inc(scale_kept, 1)
                        if live(i, j, 0):
                            wait_count(act, turned_l, n - 1)
                            wait_count(act, inv_done, n - 1)
                            for a in range(2):
                                act.wait_ge(ntop_done[a], n + 1)
                                for g in range(HALF * a, HALF * (a + 1)):
                                    ins = nc.scalar.activation(prob[:, j % 2, g, :], psum[:, g, 0:S], ACT.Exp,
                                                               bias=ntop[:, j % 2, g:g + 1],
                                                               accum_out=total[:, j % 2, g:g + 1])
                                ins.then_inc(exp_done[a], 1)
                        if live(i, j, TL):
                            m, c = n - TL, (j - TL) % 2
                            act.wait_ge(turned[0], m + 1)
                            wait_count(act, pv_done, m - 1)
                            nc.scalar.activation(pT[:, c, 0].rearrange("p g t k -> p (g t k)"), psum[:, T_BANK, :],
                                                 ACT.Copy).then_inc(pT_kept[0], 1)
                            act.wait_ge(turned_l, m + 1)
                            nc.scalar.activation(plT[:, c, :], psum[0:HG, O_BANK, LEFT_AT:LEFT_AT + PT], ACT.Copy
                                                 ).then_inc(plT_kept, 1)
                steps(act, step)
        clear_counts(nc, sems)


def rope_self_attention(nc, st):
    psum, cst, x = st.psum, st.cst, st.x
    q, rk = st.qT, st.xn_flat
    with ExitStack() as ctx:
        sb = lambda n, shape, dt=F32: ctx.enter_context(nc.sbuf_tensor("e_" + n, shape, dt))
        sems = []

        def sem(n):
            sems.append(ctx.enter_context(nc.semaphore("e_" + n)))
            return sems[-1]

        raw = sb("raw", [PT, 2, TOK])
        womask = sb("womask", [PT, HG, D])
        out_bias = sb("out_bias", [1, D])
        wq, wk, wv, wo = (st.w["L1_attn_" + n] for n in ("wqT", "wkT", "wvT", "woT"))
        layer_norm(nc, st, "n4", products=[([None], [wq], st.col["L1_attn_bq"], DH ** -0.5, raw[:, 0]),
                                           ([None], [wk], st.col["L1_attn_bk"], 1.0, raw[:, 1])])

        by_batch = lambda a: a.rearrange("p (b l) -> p b l", l=L)
        over_b = lambda a, n: a.unsqueeze(1).broadcast_to([PT, n, L])
        rotated, sin_done, cos_done, bias_done = map(sem, ("rotated", "sin_done", "cos_done", "bias_done"))
        sin_part = sb("sin_part", [PT, 2, 512])
        with nc.Block() as block:

            @block.tensor
            def _(pe):
                for k in range(8):
                    wait_count(pe, sin_done, k - 3)
                    nc.tensor.matmul(psum[:, k % 4, :], cst["rotate"], raw[:, k // 4, 512 * (k % 4):512 * (k % 4 + 1)],
                                     start=True, stop=True).then_inc(rotated, 1)
                nc.tensor.matmul(psum[0:1, 4, 0:D], st.col["L1_attn_bv"], wo, start=True, stop=True
                                 ).then_inc(bias_done, 1)

            @block.gpsimd
            def _(pool):
                for k, to in enumerate((q[:], rk)):
                    nc.gpsimd.tensor_tensor(by_batch(to), by_batch(raw[:, k]), over_b(cst["cos"], B), ALU.mult
                                            ).then_inc(cos_done, 1)
                for h in range(HG):
                    nc.gpsimd.tensor_scalar(womask[:, h, :], wo, cst["head4"][:, h:h + 1], None, ALU.mult)

            @block.vector
            def _(dve):
                for k in range(8):
                    to = (q[:], rk)[k // 4][:, 512 * (k % 4):512 * (k % 4 + 1)]
                    dve.wait_ge(rotated, k + 1)
                    nc.vector.tensor_tensor(by_batch(sin_part[:, k % 2]), by_batch(psum[:, k % 4, :]),
                                            over_b(cst["sin"], 16), ALU.mult).then_inc(sin_done, 1)
                    dve.wait_ge(sin_done, k + 1)
                    dve.wait_ge(cos_done, k // 4 + 1)
                    nc.vector.tensor_tensor(to, to, sin_part[:, k % 2], ALU.add)
                dve.wait_ge(bias_done, 1)
                nc.vector.tensor_tensor(out_bias[:], psum[0:1, 4, 0:D], st.row["L1_attn_bo"], ALU.add)

        xs = sb("xs", [PT, 2, PT])
        qs = sb("qs", [PT, 2, PT])
        kbd = sb("kbd", [PT, 2, TPB, NH, L])
        v = sb("v", [PT, 2, D])
        prob = sb("prob", [PT, 2, NH, L])
        pT = sb("pT", [PT, 2, NH * L])
        top = sb("top", [PT, NH])
        total = sb("total", [PT, NH])
        inv = sb("inv", [PT, NH])
        attn = sb("attn", [PT, HG, TPB, L])
        (xs_kept, qs_kept, kbd_done, v_done, v_kept, s_done, top_done, sub_done, exp_done, total_done, inv_done,
         norm_done, pT_done, pv_done, attn_kept, o_done, x_done) = map(sem, (
             "xs_kept", "qs_kept", "kbd_done", "v_done", "v_kept", "s_done", "top_done", "sub_done", "exp_done",
             "total_done", "inv_done", "norm_done", "pT_done", "pv_done", "attn_kept", "o_done", "x_done"))
        pv_open = sem("pv_open")
        V_BANK, A_BANK, O_BANK = 2, 3, 7
        SC, PV, OUT = 1, 2, 3
        is_live = lambda i, j, lag: live(i, j, lag, NT, 2)
        steps = lambda eng, step: tile_steps(eng, step, 2, 2, NT // 2)
        with nc.Block() as block:

            @block.gpsimd
            def _(pool):
                def step(i):
                    for j in range(2):
                        if is_live(i, j, 0):
                            n = 2 * i + j
                            wait_count(pool, s_done, n - 1)
                            for b in range(TPB):
                                ins = nc.gpsimd.tensor_tensor(
                                    kbd[:, j, b], rk[:, bass.ds(n * PT + b * L, L)].unsqueeze(1).broadcast_to(
                                        [PT, NH, L]),
                                    cst["head16"].unsqueeze(2).broadcast_to([PT, NH, L]), ALU.mult)
                            ins.then_inc(kbd_done, 1)
                steps(pool, step)

            @block.tensor
            def _(pe):
                def step(i):
                    for j in range(2):
                        n = 2 * i + j
                        if is_live(i, j, SC):
                            m, c = n - SC, (j - SC) % 2
                            pe.wait_ge(xs_kept, m + 1)
                            wait_count(pe, v_kept, m)
                            nc.tensor.matmul(psum[:, V_BANK, 0:D], xs[:, c], wv, start=True, stop=True
                                             ).then_inc(v_done, 1)
                            pe.wait_ge(kbd_done, m + 1)
                            pe.wait_ge(qs_kept, m + 1)
                            wait_count(pe, sub_done, m - 1)
                            for b in range(TPB):
                                mm = nc.tensor.matmul(psum[32 * b:32 * (b + 1), c, :], qs[:, c, L * b:L * (b + 1)],
                                                      kbd[:, c, b], start=True, stop=True, tile_position=(0, 32 * b))
                            mm.then_inc(s_done, 1)
                        if is_live(i, j, OUT):
                            m = n - OUT
                            pe.wait_ge(attn_kept, m + 1)
                            wait_count(pe, x_done, m)
                            o = psum[:, O_BANK, 0:D]
                            for h in range(HG):
                                nc.tensor.matmul(o, attn[:, h].rearrange("p b l -> p (b l)"), womask[:, h, :],
                                                 start=(h == 0), stop=False)
                            nc.tensor.matmul(o, cst["ones"][0:1, :], out_bias[:], start=False, stop=True
                                             ).then_inc(o_done, 1)
                        if is_live(i, j, PV):
                            m, c = n - PV, (j - PV) % 2
                            pe.wait_ge(pT_done, m + 1)
                            pe.wait_ge(v_kept, m + 1)
                            wait_count(pe, attn_kept, m)
                            pe.sem_inc(pv_open)
                            for g in range(HG):
                                for b in range(TPB):
                                    mm = nc.tensor.matmul(
                                        psum[32 * g:32 * (g + 1), A_BANK + b, 0:PT],
                                        v[32 * b:32 * (b + 1), c, 32 * g:32 * (g + 1)],
                                        pT[32 * b:32 * (b + 1), c, PT * g:PT * (g + 1)],
                                        start=True, stop=True, tile_position=(32 * b, 32 * g))
                            mm.then_inc(pv_done, 1)
                steps(pe, step)

            @block.vector
            def _(dve):
                over_k = lambda a: a.unsqueeze(2).broadcast_to([PT, NH, L])

                def step(i):
                    for j in range(2):
                        n = 2 * i + j
                        if is_live(i, j, SC):
                            m, c = n - SC, (j - SC) % 2
                            sc = psum[:, c, :].rearrange("p (h k) -> p h k", k=L)
                            dve.wait_ge(s_done, m + 1)
                            nc.vector.tensor_reduce(top[:], sc, AX_X, ALU.max).then_inc(top_done, 1)
                            dve.wait_ge(top_done, m + 1)
                            nc.vector.tensor_tensor(prob[:, c], sc, over_k(top[:]), ALU.subtract).then_inc(sub_done, 1)
                            dve.wait_ge(exp_done, m + 1)
                            nc.vector.tensor_reduce(total[:], prob[:, c], AX_X, ALU.add).then_inc(total_done, 1)
                            dve.wait_ge(total_done, m + 1)
                            nc.vector.reciprocal(inv[:], total[:]).then_inc(inv_done, 1)
                            dve.wait_ge(inv_done, m + 1)
                            nc.vector.tensor_tensor(prob[:, c], prob[:, c], over_k(inv[:]), ALU.mult
                                                    ).then_inc(norm_done, 1)
                            dve.wait_ge(norm_done, m + 1)
                            wait_count(dve, pv_done, m - 1)
                            nc.vector.transpose(pT[:, c], prob[:, c].rearrange("p h k -> p (h k)")
                                                ).then_inc(pT_done, 1)
                        if is_live(i, j, OUT):
                            m = n - OUT
                            dve.wait_ge(o_done, m + 1)
                            xt = x[:, bass.ds(m, 1), :].rearrange("p o d -> p (o d)")
                            nc.vector.tensor_tensor(xt, xt, psum[:, O_BANK, 0:D], ALU.add).then_inc(x_done, 1)
                steps(dve, step)

            @block.scalar
            def _(act):
                nc.scalar.preload_act_table(ACT.Exp)

                def step(i):
                    for j in range(2):
                        n = 2 * i + j
                        if is_live(i, j, SC):
                            m, c = n - SC, (j - SC) % 2
                            act.wait_ge(v_done, m + 1)
                            wait_count(act, pv_done, m - 1)
                            nc.scalar.activation(v[:, c], psum[:, V_BANK, 0:D], ACT.Copy).then_inc(v_kept, 1)
                        if is_live(i, j, 0):
                            wait_count(act, v_done, n - 1)
                            nc.scalar.activation(xs[:, j], st.xnT_flat[:, bass.ds(n * PT, PT)], ACT.Copy
                                                 ).then_inc(xs_kept, 1)
                            wait_count(act, s_done, n - 1)
                            nc.scalar.activation(qs[:, j], q[:, bass.ds(n * PT, PT)], ACT.Copy).then_inc(qs_kept, 1)
                        if is_live(i, j, SC):
                            m, c = n - SC, (j - SC) % 2
                            act.wait_ge(sub_done, m + 1)
                            nc.scalar.activation(prob[:, c], prob[:, c], ACT.Exp).then_inc(exp_done, 1)
                        if is_live(i, j, PV):
                            m = n - PV
                            act.wait_ge(pv_done, m + 1)
                            wait_count(act, o_done, m)
                            nc.scalar.activation(attn[:].rearrange("p h b l -> p b h l"),
                                                 psum[:, A_BANK:A_BANK + TPB, 0:PT].rearrange(
                                                     "p b (h l) -> p b h l", h=HG), ACT.Copy).then_inc(attn_kept, 1)
                steps(act, step)
        clear_counts(nc, sems)


def switch_head_ffn(nc, st):
    psum, cst, x = st.psum, st.cst, st.x
    with ExitStack() as ctx:
        sb = lambda n, shape, dt=F32: ctx.enter_context(nc.sbuf_tensor("f_" + n, shape, dt))
        sems = []

        def sem(n):
            sems.append(ctx.enter_context(nc.semaphore("f_" + n)))
            return sems[-1]

        HE = FH * FE
        SCALE = FP ** -0.5
        qw = st.qT[:, 0:FH * FP]
        kw = st.qT[:, FH * FP:2 * FH * FP]
        CHUNKS = 2 * FH
        w_hi = sb("w_hi", [PT, CHUNKS, FE * D], F32R)
        w_lo = sb("w_lo", [PT, CHUNKS, FE * D], F32R)
        whole = [a[:, 0:FE * D] for a in st.spare_weights]
        sel, rs = st.sel, st.rs
        gate = sb("gate", [PT, 2, 2 * HE])
        w_in = sem("w_in")
        chunk_in = [sem(f"chunk_in{k}") for k in range(2)]
        hi_done, lo_done = sem("hi_done"), sem("lo_done")

        def load_chunk(sp, c):
            name = "L1_ffn_v_w" if c < FH else "L1_ffn_o_w"
            of_head = slice(FE * (c % FH), FE * (c % FH + 1))
            sp.dma_start(whole[c % 2].rearrange("p (e q) -> p e q", e=FE),
                         st.dram[name][of_head].rearrange("e p q -> p e q")).then_inc(chunk_in[c % 2], 16)

        logits_done = sem("logits_done")
        routing = st.xn_flat
        LOGIT_BANK = 2

        def load_weights(sp):
            for c in range(2):
                load_chunk(sp, c)
            sp.dma_start(qw, st.dram["L1_ffn_q_wT"]).then_inc(w_in, 16)
            sp.dma_start(kw, st.dram["L1_ffn_k_wT"]).then_inc(w_in, 16)

        def logits(pe, k):
            for t in range(4 * k, 4 * (k + 1)):
                mm = nc.tensor.matmul(psum[:, LOGIT_BANK + k, PT * (t % 4):PT * (t % 4 + 1)],
                                      st.xnT_flat[:, PT * t:PT * (t + 1)], sel[:], start=True, stop=True)
            mm.then_inc(logits_done, 1)

        def probabilities(act):
            nc.scalar.preload_act_table(ACT.Sigmoid)
            for k in range(4):
                act.wait_ge(logits_done, k + 1)
                nc.scalar.activation(routing[:, 512 * k:512 * (k + 1)], psum[:, LOGIT_BANK + k, :], ACT.Sigmoid)

        layer_norm(nc, st, "n5", loads=load_weights, on_group=logits, on_scalar=probabilities)

        xs_hi = sb("xs_hi", [PT, 2, PT], F32R)
        xs_lo = sb("xs_lo", [PT, 2, PT], F32R)
        qk = sb("qk", [PT, 2, 2, PT])
        pT = sb("pT", [PT, FH, L])
        pbd = sb("pbd", [PT, 2, FH, PT])
        top = sb("top", [PT, FH])
        total = sb("total", [PT, FH])
        inv = sb("inv", [PT, FH])
        scaled = sb("scaled", [PT, 2, FE, FP])
        half = st.spare_consts[:, 0:4 * FP].rearrange("p (k d) -> p k d", k=4)
        v = st.spare_consts[:, 4 * FP:8 * FP].rearrange("p (k d) -> p k d", k=4)
        prob = st.spare_consts[:, 8 * FP:8 * FP + FH * L].rearrange("p (h l) -> p h l", l=L)
        cT_hi = sb("cT_hi", [PT, 2, PT], F32R)
        cT_lo = sb("cT_lo", [PT, 2, PT], F32R)
        acc = sb("acc", [PT, 4, D])
        pair = sb("pair", [PT, 2, D])
        choice = sel[:].rearrange("p (a e) -> p a e", e=FE)
        RH = 2 * FH
        prob_of = st.spare_consts[:, 8 * FP + FH * L:8 * FP + FH * L + RH * FE].rearrange("p (a e) -> p a e", e=FE)
        cand = sb("cand", [PT, RH, FE])
        picked = sb("picked", [PT, RH, FE])
        best = sb("best", [PT, 2, RH])
        first = sb("first", [PT, RH])
        weight = sb("weight", [PT, RH])
        GATE_STEPS = 19
        gate_step = sem("gate_step")
        (zeroed, xs_kept, qk_done, qk_kept, s_done, top_done, sub_done, exp_done, total_done,
         inv_done, norm_done, pT_done, pbd_done, v_done, v_scaled, v_half, v_quarter, v_kept, c_done, c_kept, xs_lo_kept, c_lo_kept,
         o_done, o_weighed, pair_done, x_done) = map(sem, (
             "zeroed", "xs_kept", "qk_done", "qk_kept", "s_done", "top_done", "sub_done",
             "exp_done", "total_done", "inv_done", "norm_done", "pT_done", "pbd_done", "v_done", "v_scaled", "v_half",
             "v_quarter", "v_kept", "c_done", "c_kept", "xs_lo_kept", "c_lo_kept", "o_done", "o_weighed", "pair_done", "x_done"))
        V_BANK, O_BANK, QK_BANK, C_BANK = 0, 2, 4, 6
        S_BANK = (5, 7)
        SC, XL, VL, CL, OL = 1, 3, 8, 12, 13

        def multiply_split(out, hi, lo, chunk, f):
            cols = slice(4 * D * f, 4 * D * (f + 1))
            nc.tensor.matmul(out, lo, w_hi[:, chunk, cols], start=True, stop=False)
            nc.tensor.matmul(out, hi, w_lo[:, chunk, cols], start=False, stop=False)
            return nc.tensor.matmul(out, hi, w_hi[:, chunk, cols], start=False, stop=True)
        PER = 2 * FH
        TOTAL = NT * FH
        is_live = lambda i, k, lag: live(i, k, lag, TOTAL, PER)
        steps = lambda eng, step: tile_steps(eng, step, 1, 1, NT // 2)

        with nc.Block() as block:

            @block.sync
            def _(sp):
                for c in range(2, CHUNKS):
                    sp.wait_ge(lo_done, c - 1)
                    load_chunk(sp, c)

            @block.tensor
            def _(pe):
                def step(i):
                    for k in range(PER):
                        s = PER * i + k
                        if is_live(i, k, CL):
                            n, h = s - CL, (k - CL) % FH
                            par = (k - CL) // FH % 2
                            if h == 0:
                                pe.wait_ge(pbd_done, 4 * (2 * i + (k - CL) // FH + 1))
                            pe.wait_ge(v_kept, n + 1)
                            wait_count(pe, c_lo_kept, n)
                            nc.tensor.matmul(psum[:, C_BANK, 0:PT], v[:, (k - CL) % 4], pbd[:, par, h],
                                             start=True, stop=True).then_inc(c_done, 1)
                        if is_live(i, k, VL):
                            n, h = s - VL, (k - VL) % FH
                            if h == 0:
                                pe.wait_ge(xs_lo_kept, 2 * i + (k - VL) // FH + 1)
                            if isinstance(i, int) and i == 0:
                                pe.wait_ge(lo_done, h + 1)
                            par = (k - VL) // FH % 2
                            for f in range(2):
                                wait_count(pe, v_scaled, 2 * n + f - 1)
                                multiply_split(psum[:, V_BANK + f, :], xs_hi[:, par], xs_lo[:, par], h, f
                                               ).then_inc(v_done, 1)
                        if is_live(i, k, 0):
                            h = k % FH
                            wait_count(pe, qk_kept, s)
                            if isinstance(i, int) and i == 0 and k == 0:
                                pe.wait_ge(w_in, 32)
                            xt = st.xnT_flat[:, bass.ds((2 * i + k // FH) * PT, PT)]
                            nc.tensor.matmul(psum[:, QK_BANK, 0:PT], qw[:, FP * h:FP * (h + 1)], xt,
                                             start=True, stop=True)
                            nc.tensor.matmul(psum[:, QK_BANK, PT:2 * PT], kw[:, FP * h:FP * (h + 1)], xt,
                                             start=True, stop=True).then_inc(qk_done, 1)
                        if is_live(i, k, SC):
                            n, h = s - SC, (k - SC) % FH
                            c = (k - SC) % 2
                            par = (k - SC) // FH % 2
                            pe.wait_ge(qk_kept, n + 1)
                            if h == 0:
                                wait_count(pe, sub_done, 2 * i + (k - SC) // FH - 1)
                            for b in range(TPB):
                                mm = nc.tensor.matmul(psum[32 * b:32 * (b + 1), S_BANK[par], L * h:L * (h + 1)],
                                                      qk[:, c, 0, L * b:L * (b + 1)], qk[:, c, 1, L * b:L * (b + 1)],
                                                      start=True, stop=True, tile_position=(0, 32 * b))
                            mm.then_inc(s_done, 1)
                        if is_live(i, k, OL):
                            n, h = s - OL, (k - OL) % FH
                            if isinstance(n, int) and n < FH or not isinstance(n, int) and k < OL:
                                pe.wait_ge(lo_done, FH + h + 1)
                            pe.wait_ge(c_lo_kept, n + 1)
                            c = (k - OL) % 2
                            for f in range(2):
                                wait_count(pe, o_weighed, FE * (n - 1) + 4 * (f + 1))
                                multiply_split(psum[:, O_BANK + f, :], cT_hi[:, c], cT_lo[:, c], FH + h, f
                                               ).then_inc(o_done, 1)
                steps(pe, step)

            @block.scalar
            def _(act):
                nc.scalar.preload_act_table(ACT.Exp)

                def step(i):
                    for k in range(PER):
                        s = PER * i + k
                        if is_live(i, k, CL):
                            n = s - CL
                            act.wait_ge(c_done, n + 1)
                            wait_count(act, o_done, 2 * (n - 1))
                            nc.scalar.activation(cT_hi[:, (k - CL) % 2], psum[:, C_BANK, 0:PT], ACT.Copy
                                                 ).then_inc(c_kept, 1)
                        if is_live(i, k, VL):
                            n, h = s - VL, (k - VL) % FH
                            t = 2 * i + (k - VL) // FH
                            if h == 0:
                                act.wait_ge(gate_step, GATE_STEPS * (t + 1))
                            wait_count(act, v_half, n - 1)
                            for f in range(2):
                                act.wait_ge(v_done, 2 * n + f + 1)
                                for e in range(4 * f, 4 * (f + 1)):
                                    a = nc.scalar.activation(scaled[:, (k - VL) % 2, e, :],
                                                             psum[:, V_BANK + f, FP * (e % 4):FP * (e % 4 + 1)],
                                                             ACT.Copy, scale=gate[:, (k - VL) // FH % 2, FE * h + e:FE * h + e + 1])
                                a.then_inc(v_scaled, 1)
                        if is_live(i, k, 0):
                            act.wait_ge(qk_done, s + 1)
                            wait_count(act, s_done, s - 1)
                            nc.scalar.activation(qk[:, k % 2].rearrange("p a t -> p (a t)"),
                                                 psum[:, QK_BANK, 0:2 * PT], ACT.Copy).then_inc(qk_kept, 1)
                        if k % FH == 1 and is_live(i, k, FH + 1):
                            t = 2 * i + (k - FH - 1) // FH
                            act.wait_ge(sub_done, t + 1)
                            nc.scalar.activation(prob, prob, ACT.Exp, scale=SCALE).then_inc(exp_done, 1)
                        if k % FH == 2 and is_live(i, k, FH + 2):
                            t = 2 * i + (k - FH - 2) // FH
                            par = (k - FH - 2) // FH % 2
                            act.wait_ge(pT_done, t + 1)
                            act.wait_ge(zeroed, 1)
                            wait_count(act, c_done, FH * (t - 1))
                            for b in range(TPB):
                                nc.scalar.activation(pbd[32 * b:32 * (b + 1), par, :, L * b:L * (b + 1)],
                                                     pT[32 * b:32 * (b + 1)], ACT.Copy).then_inc(pbd_done, 1)
                        if k % FH == XL and is_live(i, k, XL):
                            t = 2 * i + k // FH
                            wait_count(act, v_done, 2 * FH * (t - 1))
                            nc.scalar.activation(xs_hi[:, k // FH], st.xnT_flat[:, bass.ds(t * PT, PT)], ACT.Copy
                                                 ).then_inc(xs_kept, 1)
                        if isinstance(i, int) and i == 0:
                            act.wait_ge(chunk_in[k % 2], 16 * (k // 2 + 1))
                            nc.scalar.activation(w_hi[:, k], whole[k % 2], ACT.Copy).then_inc(hi_done, 1)
                steps(act, step)

            @block.gpsimd
            def _(pool):
                nc.gpsimd.memset(pbd[:], 0.0).then_inc(zeroed, 1)

                def step(i):
                    for k in range(PER):
                        s = PER * i + k
                        if is_live(i, k, VL):
                            n = s - VL
                            c = (k - VL) % 2
                            pool.wait_ge(v_scaled, 2 * n + 2)
                            wait_count(pool, v_kept, n)
                            nc.gpsimd.tensor_tensor(half, scaled[:, c, 0:4, :], scaled[:, c, 4:8, :], ALU.add
                                                    ).then_inc(v_half, 1)
                            pool.wait_ge(v_half, n + 1)
                            nc.gpsimd.tensor_tensor(half[:, 0:2, :], half[:, 0:2, :], half[:, 2:4, :], ALU.add
                                                    ).then_inc(v_quarter, 1)
                            pool.wait_ge(v_quarter, n + 1)
                            wait_count(pool, c_done, n - 3)
                            nc.gpsimd.tensor_tensor(v[:, (k - VL) % 4], half[:, 0, :], half[:, 1, :], ALU.add
                                                    ).then_inc(v_kept, 1)
                steps(pool, step)

            @block.vector
            def _(dve):
                over_k = lambda a: a.unsqueeze(2).broadcast_to([PT, FH, L])
                over_e = lambda a: a.unsqueeze(2).broadcast_to([PT, RH, FE])
                rank = cst["rank8"].unsqueeze(1).broadcast_to([PT, RH, FE])

                def make_gates(t, par, part):
                    done = [GATE_STEPS * t + 3 * part + (1 if part else 0)]
                    def stepped(instruction):
                        done[0] += 1
                        instruction.then_inc(gate_step, 1)

                    def ready():
                        dve.wait_ge(gate_step, done[0])

                    if part == 0:
                        stepped(nc.vector.tensor_copy(prob_of.rearrange("p a e -> p (a e)"),
                                                      routing[:, bass.ds(t * 2 * HE, 2 * HE)]))
                        ready()
                        stepped(nc.vector.tensor_reduce(best[:, 0], prob_of, AX_X, ALU.max))
                        ready()
                        stepped(nc.vector.tensor_tensor(cand[:], prob_of, over_e(best[:, 0]), ALU.is_equal))
                        ready()
                        stepped(nc.vector.tensor_tensor(cand[:], cand[:], rank, ALU.mult))
                    elif part == 1:
                        ready()
                        stepped(nc.vector.tensor_reduce(first[:], cand[:], AX_X, ALU.max))
                        ready()
                        stepped(nc.vector.tensor_tensor(picked[:], cand[:], over_e(first[:]), ALU.is_equal))
                        ready()
                        stepped(nc.vector.scalar_tensor_tensor(choice, picked[:], -2.0, prob_of,
                                                               ALU.mult, ALU.add))
                    elif part == 2:
                        ready()
                        stepped(nc.vector.tensor_reduce(best[:, 1], choice, AX_X, ALU.max))
                        ready()
                        stepped(nc.vector.tensor_tensor(cand[:], choice, over_e(best[:, 1]), ALU.is_equal))
                        ready()
                        stepped(nc.vector.tensor_tensor(cand[:], cand[:], rank, ALU.mult))
                    elif part == 3:
                        ready()
                        stepped(nc.vector.tensor_reduce(first[:], cand[:], AX_X, ALU.max))
                        ready()
                        stepped(nc.vector.tensor_tensor(cand[:], cand[:], over_e(first[:]), ALU.is_equal))
                        ready()
                        stepped(nc.vector.tensor_tensor(picked[:], picked[:], cand[:], ALU.add))
                    elif part == 4:
                        ready()
                        stepped(nc.vector.tensor_tensor(weight[:], best[:, 0], best[:, 1], ALU.add))
                        ready()
                        stepped(nc.vector.tensor_scalar(weight[:], weight[:], 1e-9, None, ALU.max))
                        ready()
                        stepped(nc.vector.reciprocal(weight[:], weight[:]))
                    else:
                        ready()
                        stepped(nc.vector.tensor_scalar(weight[:], weight[:], rs[:, 0:1], None, ALU.mult))
                        stepped(nc.vector.tensor_tensor(picked[:], picked[:], prob_of, ALU.mult))
                        ready()
                        wait_count(dve, v_scaled, 2 * FH * (t - 1))
                        wait_count(dve, o_weighed, FE * FH * (t - 1))
                        stepped(nc.vector.tensor_tensor(gate[:, par].rearrange("p (a e) -> p a e", e=FE), picked[:],
                                                        over_e(weight[:]), ALU.mult))

                def step(i):
                    for k in range(PER):
                        s = PER * i + k
                        if is_live(i, k, CL):
                            n, c = s - CL, (k - CL) % 2
                            dve.wait_ge(c_kept, n + 1)
                            wait_count(dve, o_done, 2 * (n - 1))
                            nc.vector.tensor_tensor(cT_lo[:, c], psum[:, C_BANK, 0:PT], cT_hi[:, c], ALU.subtract
                                                    ).then_inc(c_lo_kept, 1)
                        if k % FH == 1 and is_live(i, k, FH + 1):
                            t = 2 * i + (k - FH - 1) // FH
                            par = (k - FH - 1) // FH % 2
                            sc = psum[:, S_BANK[par], 0:FH * L].rearrange("p (h k) -> p h k", k=L)
                            dve.wait_ge(s_done, FH * (t + 1))
                            nc.vector.tensor_reduce(top[:], sc, AX_X, ALU.max).then_inc(top_done, 1)
                            dve.wait_ge(top_done, t + 1)
                            wait_count(dve, pT_done, t)
                            nc.vector.tensor_tensor(prob, sc, over_k(top[:]), ALU.subtract).then_inc(sub_done, 1)
                        if is_live(i, k, OL):
                            n, h = s - OL, (k - OL) % FH
                            t = 2 * i + (k - OL) // FH
                            for f in range(2):
                                dve.wait_ge(o_done, 2 * n + f + 1)
                                for e in range(4 * f, 4 * (f + 1)):
                                    part = psum[:, O_BANK + f, D * (e % 4):D * (e % 4 + 1)]
                                    g = gate[:, (k - OL) // FH % 2, HE + FE * h + e:HE + FE * h + e + 1]
                                    if h == 0 and f == 0:
                                        wait_count(dve, pair_done, 3 * t)
                                        ins = nc.vector.tensor_scalar(acc[:, e], part, g, None, ALU.mult)
                                    else:
                                        dve.wait_ge(o_weighed, FE * n + e - 3)
                                        ins = nc.vector.scalar_tensor_tensor(acc[:, e % 4], part, g, acc[:, e % 4],
                                                                             ALU.mult, ALU.add)
                                    ins.then_inc(o_weighed, 1)
                            if h == FH - 1:
                                dve.wait_ge(o_weighed, FE * (n + 1))
                                wait_count(dve, x_done, t)
                                nc.vector.tensor_tensor(pair[:], acc[:, 0:2], acc[:, 2:4], ALU.add
                                                        ).then_inc(pair_done, 1)
                                dve.wait_ge(pair_done, 3 * t + 1)
                                nc.vector.tensor_tensor(pair[:, 0], pair[:, 0], pair[:, 1], ALU.add
                                                        ).then_inc(pair_done, 2)
                                dve.wait_ge(pair_done, 3 * t + 3)
                                xt = x[:, bass.ds(t, 1), :].rearrange("p o d -> p (o d)")
                                nc.vector.tensor_tensor(xt, xt, pair[:, 0], ALU.add).then_inc(x_done, 1)
                        if k % FH == 1 and is_live(i, k, FH + 1):
                            t = 2 * i + (k - FH - 1) // FH
                            dve.wait_ge(exp_done, t + 1)
                            nc.vector.tensor_reduce(total[:], prob, AX_X, ALU.add).then_inc(total_done, 1)
                            dve.wait_ge(total_done, t + 1)
                            nc.vector.reciprocal(inv[:], total[:]).then_inc(inv_done, 1)
                            dve.wait_ge(inv_done, t + 1)
                            nc.vector.tensor_tensor(prob, prob, over_k(inv[:]), ALU.mult).then_inc(norm_done, 1)
                            dve.wait_ge(norm_done, t + 1)
                            wait_count(dve, pbd_done, 4 * t)
                            nc.vector.transpose(pT[:].rearrange("p h k -> p (h k)"),
                                                prob.rearrange("p h k -> p (h k)")).then_inc(pT_done, 1)
                        if 2 <= k % FH <= 6 and is_live(i, k, 0):
                            make_gates(2 * i + k // FH, k // FH, k % FH - 2)
                            if k % FH == 6:
                                make_gates(2 * i + k // FH, k // FH, 5)
                        if k % FH == XL and is_live(i, k, XL):
                            t = 2 * i + k // FH
                            dve.wait_ge(xs_kept, t + 1)
                            wait_count(dve, v_done, 2 * FH * (t - 1))
                            nc.vector.tensor_tensor(xs_lo[:, k // FH], st.xnT_flat[:, bass.ds(t * PT, PT)],
                                                    xs_hi[:, k // FH], ALU.subtract).then_inc(xs_lo_kept, 1)
                        if isinstance(i, int) and i == 0:
                            dve.wait_ge(hi_done, k + 1)
                            nc.vector.tensor_tensor(w_lo[:, k], whole[k % 2], w_hi[:, k], ALU.subtract
                                                    ).then_inc(lo_done, 1)
                steps(dve, step)
        clear_counts(nc, sems)


WEIGHTS = ["L0_xattn_Wq", "L0_xattn_Wk", "L0_xattn_Wv", "L0_xattn_Wo", "L1_xattn_Wo",
           "L1_attn_wqT", "L1_attn_wkT", "L1_attn_wvT", "L1_attn_woT"]
COLUMNS = ["L0_xattn_bq", "L0_xattn_bk", "L0_xattn_bv", "L1_xattn_bq", "L1_xattn_bk", "L1_xattn_bv",
           "L1_attn_bq", "L1_attn_bk", "L1_attn_bv"]
ROWS = ["L0_xattn_bo", "L1_xattn_bo", "L1_attn_bo"]
CONV_WEIGHTS = ["L1_xattn_Wq", "L1_xattn_Wk", "L1_xattn_Wv"]


def perceiver(nc, ins, out, stop_after=6):
    with ExitStack() as ctx:
        sb = lambda n, shape, dt=F32: ctx.enter_context(nc.sbuf_tensor(n, shape, dt))
        st = State()
        st.dram = ins
        st.ctx = ins["ctx_1024"]
        st.v_dram = nc.dram_tensor("v_dram", (B, PT, SF * D), F32).ap()
        st.x = sb("x", [PT, NT, D])
        st.xn = sb("xn", [PT, NT, D])
        st.xn_flat = st.xn[:].rearrange("p t d -> p (t d)")
        st.xnT_pad = sb("xnT", [PT, B, L + 2])
        st.xnT_flat = st.xnT_pad[:].rearrange("p b l -> p (b l)")[:, 0:TOK]
        st.qT = sb("qT", [PT, TOK])
        st.wg = sb("wg", [PT, NE])
        st.bg = sb("bg", [PT, NE])
        st.b1 = sb("b1", [NE * HC, PT])
        st.sel = sb("sel", [PT, 2 * FH * FE])
        st.rs = sb("rs", [PT, 1])
        st.filt = sb("filt", [PT, L])
        st.past = sb("past", [PT, L])
        st.psum = ctx.enter_context(nc.psum_tensor("psum", [PT, 8, 512], F32))
        consts = sb("consts", [PT, CONST_COLS])
        st.cst = {n: consts[:, a:b] for n, (a, b) in CONST_AT.items()}
        st.ident = st.cst["ident"]
        st.spare_consts = consts[:, CONST_AT["upto"][0]:CONST_AT["own_group"][1]]
        wall = sb("wall", [PT, len(WEIGHTS), D])
        st.w = {n: wall[:, k, :] for k, n in enumerate(WEIGHTS)}
        cols = sb("cols", [PT, len(COLUMNS)])
        st.col = {n: cols[:, k:k + 1] for k, n in enumerate(COLUMNS)}
        rows = sb("rows", [1, len(ROWS), D])
        st.row = {n: rows[:, k, :] for k, n in enumerate(ROWS)}
        st.convw = sb("convw", [PT, 3, 3, D])
        st.spare_weights = [wall[:].rearrange("p k d -> p (k d)"), st.convw[:].rearrange("p a t d -> p (a t d)")]
        st.norm_sem = lambda n: ctx.enter_context(nc.semaphore(n))
        st.scattered, st.gathered = (ctx.enter_context(nc.semaphore(n)) for n in ("scattered", "gathered"))
        st.y_stored = [ctx.enter_context(nc.semaphore(f"y_stored{k}")) for k in range(EB)]
        st.weights_in = ctx.enter_context(nc.semaphore("weights_in"))
        st.x_in = [ctx.enter_context(nc.semaphore(f"x_in{k}")) for k in range(2)]
        stored = ctx.enter_context(nc.semaphore("stored"))
        st.weights_count = 16 * 10

        def load_tokens(eng, half):
            tiles = slice(NT // 2 * half, NT // 2 * (half + 1))
            eng.dma_start(st.x[:, tiles], ins["x"].rearrange("(t b) l d -> (b l) t d", b=TPB)[:, tiles]
                          ).then_inc(st.x_in[half], 16)

        def load_on_sync(sp):
            load_tokens(sp, 0)
            sp.dma_start(consts[:], ins["consts"]).then_inc(st.weights_in, 16)
            sp.dma_start(cols[:], ins["columns"]).then_inc(st.weights_in, 16)
            sp.dma_start(st.convw[:], ins["conv_weights"]).then_inc(st.weights_in, 16)
            sp.dma_start(st.wg[:], ins["L0_ffn_Wg"]).then_inc(st.weights_in, 16)
            sp.dma_start(st.bg[:], ins["L0_ffn_bg"].rearrange("(o e) -> o e", o=1).broadcast_to([PT, NE])
                         ).then_inc(st.weights_in, 16)
            sp.dma_start(st.b1[:], ins["L0_ffn_b1"].rearrange("e (c p) -> (e c) p", p=PT)).then_inc(st.weights_in, 16)
            sp.dma_start(st.sel[:], ins["selectors"]).then_inc(st.weights_in, 16)
            sp.dma_start(st.rs[:], ins["L1_ffn_route_scale"].rearrange("(o n) -> o n", o=1).broadcast_to([PT, 1])
                         ).then_inc(st.weights_in, 16)

        def load_on_scalar(act):
            load_tokens(act, 1)
            act.dma_start(wall[:], ins["weights"]).then_inc(st.weights_in, 16)
            act.dma_start(rows[:], ins["rows"]).then_inc(st.weights_in, 16)

        st.load_on_sync, st.load_on_scalar = load_on_sync, load_on_scalar
        with ExitStack() as inner:
            st.ctx_all = inner.enter_context(nc.sbuf_tensor("ctx_all", [PT, B, S + 2], F32))
            if stop_after >= 1:
                layer_norm(nc, st, "n0", products=[([None], [st.w["L0_xattn_Wq"]], st.col["L0_xattn_bq"],
                                                    DH ** -0.5, st.qT[:])], first=True,
                           loads=st.load_on_sync)
                cross_attention_over_queries(nc, st)
            if stop_after >= 2:
                layer_norm(nc, st, "n1")
                long_convolution(nc, st)
            if stop_after >= 3:
                routed_ffn(nc, st)
            if stop_after >= 4:
                layer_norm(nc, st, "n3", padded=True, products=[
                    ([0, 1, 2], [st.convw[:, 0, t, :] for t in range(3)], st.col["L1_xattn_bq"], DH ** -0.5,
                     st.qT[:])])
                conv_cross_attention(nc, st)
        if stop_after >= 5:
            rope_self_attention(nc, st)
        if stop_after >= 6:
            switch_head_ffn(nc, st)

        with nc.Block() as block:

            @block.sync
            def _(sp):
                sp.dma_start(out.rearrange("(t b) l d -> (b l) t d", b=TPB), st.x[:]).then_inc(stored, 16)
                sp.wait_ge(stored, 16)


_TURNED = {"L1_attn_wqT": "L1_attn_wq", "L1_attn_wkT": "L1_attn_wk", "L1_attn_wvT": "L1_attn_wv",
           "L1_attn_woT": "L1_attn_wo", "L1_ffn_q_wT": "L1_ffn_q_w", "L1_ffn_k_wT": "L1_ffn_k_w",
           "L1_ffn_sel_v_wT": "L1_ffn_sel_v_w", "L1_ffn_sel_o_wT": "L1_ffn_sel_o_w"}


def build(nc, inputs, stop_after=6):
    arrays, aps = {}, {}
    laid = {n: a for n, a in inputs.items() if n not in _TURNED.values()}
    laid.update({new: np.transpose(np.asarray(inputs[old])) for new, old in _TURNED.items()})
    laid["weights"] = np.stack([laid.pop(n) for n in WEIGHTS], axis=1)
    laid["conv_weights"] = np.stack([laid.pop(n) for n in CONV_WEIGHTS], axis=0).transpose(2, 0, 1, 3)
    laid["columns"] = np.stack([laid[n] for n in COLUMNS], axis=1)
    laid["rows"] = np.stack([laid.pop(n) for n in ROWS], axis=0)[None]
    laid["selectors"] = np.concatenate([laid.pop(n) for n in ("L1_ffn_sel_v_wT", "L1_ffn_sel_o_wT")], axis=1)
    laid["consts"] = shape_constants()
    for name, a in laid.items():
        a = np.ascontiguousarray(a)
        arrays[f"in_{name}"] = a
        aps[name] = nc.dram_tensor(f"in_{name}", a.shape, mybir.dt.from_np(a.dtype), kind="ExternalInput").ap()
    out = nc.dram_tensor("out_0", (B, L, D), F32, kind="ExternalOutput").ap()
    perceiver(nc, aps, out, stop_after)
    return arrays


def kernel(**inputs):
    import concourse.bacc as _bacc
    from concourse.bass_utils import run_bass_kernel_spmd as _run

    nc = _bacc.Bacc("TRN2", target_bir_lowering=False, num_devices=1)
    arrays = build(nc, inputs)
    return _run(nc, [arrays], core_ids=[0]).results[0]["out_0"]
```

```python
from contextlib import ExitStack
import math

import numpy as np

import concourse.bass as bass
from concourse import mybir

ALU = mybir.AluOpType
ACT = mybir.ActivationFunctionType
F32 = mybir.dt.float32
BF16 = mybir.dt.bfloat16
F32R = mybir.dt.float32r
U32 = mybir.dt.uint32
AX_X = mybir.AxisListType.X

B = 64
L = 32
D = 128
S = 257
NH = 16
DH = D // NH
PT = 128
TPB = PT // L
NT = B // TPB
TOK = B * L
HG = 4
SF = 2
EPS = 1e-5

CONV_AHEAD = (0, 4)
ROUTE_AHEAD = (4, 6)
EXPERT_AHEAD = (6, 14)
GATHER_AHEAD = (14, 16)

NE = 16
CAP = -(-TOK // NE)
HID = 512
HC = HID // PT
EB = 4

FH = 8
FE = 8
FP = 128

CONST_PARTS = [("ident", 128), ("head16", 16), ("head4", 4), ("upto", 128), ("ones", 128), ("head32", 32), ("spread", 4 * 128),
               ("token_row", NT), ("rotate", 128), ("cos", L), ("sin", L), ("own_head", PT), ("own_group", HG * D),
               ("rank16", NE), ("rank8", FE)]
CONST_AT = {}
_at = 0
for _name, _n in CONST_PARTS:
    CONST_AT[_name] = (_at, _at + _n)
    _at += _n
CONST_COLS = _at


def shape_constants():
    c = {}
    p = np.arange(PT)
    c["ident"] = np.eye(PT)
    c["head16"] = (p[:, None] // DH == np.arange(NH)[None, :])
    c["head4"] = ((p[:, None] // DH) % HG == np.arange(HG)[None, :])
    c["upto"] = (p[:, None] <= p[None, :])
    c["ones"] = np.ones((PT, PT))
    c["head32"] = (p[:, None] // DH == np.arange(32)[None, :])
    c["spread"] = np.zeros((4, 32, 4, PT))
    for k in range(4):
        c["spread"][k, :NH, k] = (np.arange(NH)[:, None] == p[None, :] // DH)
    c["spread"] = c["spread"].reshape(PT, 4 * PT)
    c["token_row"] = NE * CAP + PT * np.arange(NT)[None, :] + p[:, None]
    rot = np.zeros((PT, PT))
    for i in range(PT // 2):
        rot[2 * i + 1, 2 * i] = -1.0
        rot[2 * i, 2 * i + 1] = 1.0
    c["rotate"] = rot
    freqs = np.float32(10000.0) ** (np.arange(0, DH, 2, dtype=np.float32) / np.float32(DH))
    angles = np.arange(L, dtype=np.float32)[:, None] / freqs[None, :]
    of_row = (p % DH) // 2
    c["cos"] = np.cos(angles)[:, of_row].T
    c["sin"] = np.sin(angles)[:, of_row].T
    c["own_head"] = (p[:, None] // L == (p[None, :] // DH) % HG)
    c["own_group"] = np.broadcast_to(
        (np.arange(D)[None, :] // 32 == np.arange(HG)[:, None]).reshape(1, -1), (PT, HG * D))
    c["rank16"] = np.broadcast_to(NE - np.arange(NE)[None, :], (PT, NE))
    c["rank8"] = np.broadcast_to(FE - np.arange(FE)[None, :], (PT, FE))
    return np.concatenate([np.asarray(c[n], np.float32) for n, _ in CONST_PARTS], axis=1)


def wait_count(eng, sem, count):
    if isinstance(count, int) and count <= 0:
        return
    eng.wait_ge(sem, count)


def live(i, j, lag, total=B, per=TPB):
    return not isinstance(i, int) or 0 <= per * i + j - lag < total


def live_tile(i, lag):
    return not isinstance(i, int) or 0 <= i - lag < NT


def tile_steps(eng, step, first=2, tail=2, count=NT):
    for i in range(first):
        step(i)
    with eng.Fori(first, count) as i:
        step(i)
    for i in range(count, count + tail):
        step(i)


def clear_counts(nc, sems):
    nums = sorted(s.num for s in sems)
    runs = []
    for n in nums:
        if runs and runs[-1].stop == n:
            runs[-1] = range(runs[-1].start, n + 1)
        else:
            runs.append(range(n, n + 1))
    with nc.Block() as block:

        @block.gpsimd
        def _(pool):
            for run in runs:
                pool.sem_clear(run)


class State:
    pass


def token_stats(nc, st, dve, x_done, count, x_seen, t):
    dve.wait_ge(x_done, count)
    dve.sem_inc(x_seen)
    one = lambda a: a[:, bass.ds(t, 1), :].rearrange("p o d -> p (o d)")
    nc.vector.bn_stats(one(st.stats), one(st.x))


def layer_norm(nc, st, tag, padded=False, products=(), first=False, loads=None, on_group=None, on_scalar=None,
               stats_made=False):
    st.xnT = st.xnT_pad[:, :, 1:L + 1] if padded else st.xnT_flat.rearrange("p (b l) -> p b l", l=L)
    with ExitStack() as ctx:
        stats = st.stats
        w = ctx.enter_context(nc.sbuf_tensor(f"moments_{tag}", [PT, 8, NT], F32))
        sem = lambda n: st.norm_sem(f"{n}_{tag}")
        stats_done, moment_done, std_done, xn_done, turned, xnT_done, made, kept, pad_done = map(
            sem, ("stats_done", "moment_done", "std_done", "xn_done", "turned", "xnT_done", "made", "kept",
                  "pad_done"))
        G = 4
        mean, var, std, rstd, dif, msum, vsum = (w[:, k, :] for k in range(7))
        x, xn, xnT = st.x, st.xn, st.xnT
        results = [(k, p) for k in range(NT // G) for p in range(len(products))]
        with nc.Block() as block:

            @block.gpsimd
            def _(pool):
                if padded:
                    nc.gpsimd.memset(st.xnT_pad[:, :, 0:1], 0.0).then_inc(pad_done, 1)
                    nc.gpsimd.memset(st.xnT_pad[:, :, L + 1:L + 2], 0.0).then_inc(pad_done, 1)

            @block.sync
            def _(sp):
                if loads:
                    loads(sp)

            @block.vector
            def _(dve):
                if not stats_made:
                    for t in range(NT):
                        if first and t % (NT // 2) == 0:
                            dve.wait_ge(st.x_in[2 * t // NT], 16)
                        ins = nc.vector.bn_stats(stats[:, t, :], x[:, t, :])
                    ins.then_inc(stats_done, 1)
                    dve.wait_ge(stats_done, 1)
                nc.vector.tensor_tensor(msum, stats[:, :, 1], stats[:, :, 4], ALU.add).then_inc(moment_done, 1)
                nc.vector.tensor_tensor(dif, stats[:, :, 1], stats[:, :, 4], ALU.subtract).then_inc(moment_done, 1)
                nc.vector.tensor_tensor(vsum, stats[:, :, 2], stats[:, :, 5], ALU.add).then_inc(moment_done, 1)
                dve.wait_ge(moment_done, 2)
                nc.vector.tensor_scalar(mean, msum, 0.5, None, ALU.mult).then_inc(moment_done, 1)
                nc.vector.scalar_tensor_tensor(var, dif, 0.25, dif, ALU.mult, ALU.mult).then_inc(moment_done, 1)
                dve.wait_ge(moment_done, 3)
                nc.vector.tensor_scalar(vsum, vsum, 1.0 / D, EPS, ALU.mult, ALU.add).then_inc(moment_done, 1)
                dve.wait_ge(moment_done, 6)
                nc.vector.tensor_tensor(var, var, vsum, ALU.add).then_inc(moment_done, 1)
                dve.wait_ge(std_done, 1)
                nc.vector.reciprocal(rstd, std).then_inc(moment_done, 1)
                dve.wait_ge(moment_done, 8)
                for t in range(NT):
                    nc.vector.tensor_scalar(xn[:, t, :], x[:, t, :], mean[:, t:t + 1], rstd[:, t:t + 1],
                                            ALU.subtract, ALU.mult).then_inc(xn_done, 1)
                for n, (k, p) in enumerate(results):
                    _, _, bias, scale, out = products[p]
                    dve.wait_ge(made, n + 1)
                    nc.vector.tensor_scalar(out[:, 512 * k:512 * (k + 1)], st.psum[:, 2 + n % 6, :], bias, scale,
                                            ALU.add, ALU.mult).then_inc(kept, 1)

            @block.scalar
            def _(act):
                if first:
                    st.load_on_scalar(act)
                nc.scalar.preload_act_table(ACT.Sqrt)
                act.wait_ge(moment_done, 7)
                nc.scalar.activation(std, var, ACT.Sqrt).then_inc(std_done, 1)
                for k in range(NT // G):
                    act.wait_ge(turned, k + 1)
                    nc.scalar.activation(xnT[:, 4 * G * k:4 * G * (k + 1), :],
                                         st.psum[:, k % 2, :].rearrange("p (b l) -> p b l", l=L),
                                         ACT.Copy).then_inc(xnT_done, 1)
                if on_scalar:
                    on_scalar(act)

            @block.tensor
            def _(pe):
                def turn(k):
                    pe.wait_ge(xn_done, G * (k + 1))
                    if k >= 2:
                        pe.wait_ge(xnT_done, k - 1)
                    for j in range(G):
                        mm = nc.tensor.transpose(st.psum[:, k % 2, PT * j:PT * (j + 1)], xn[:, G * k + j, :], st.ident)
                    mm.then_inc(turned, 1)

                def multiply(n):
                    k, p = results[n]
                    taps, weights = products[p][0:2]
                    pe.wait_ge(xnT_done, k + 1)
                    wait_count(pe, kept, n - 5)
                    for m, tap in enumerate(taps):
                        src = st.xnT if tap is None else st.xnT_pad[:, :, tap:tap + L]
                        mm = nc.tensor.matmul(st.psum[:, 2 + n % 6, :], weights[m], src[:, 16 * k:16 * (k + 1), :],
                                              start=(m == 0), stop=(m == len(taps) - 1))
                    mm.then_inc(made, 1)

                if padded and products:
                    pe.wait_ge(pad_done, 2)
                if first:
                    pe.wait_ge(st.weights_in, st.weights_count)
                for k in range(NT // G + 1):
                    if k < NT // G:
                        turn(k)
                    if k >= 1:
                        for p in range(len(products)):
                            multiply(len(products) * (k - 1) + p)
                        if on_group:
                            pe.wait_ge(xnT_done, k)
                            on_group(pe, k - 1)


def cross_attention_over_queries(nc, st):
    psum, cst, x = st.psum, st.cst, st.x
    qT = st.qT
    with ExitStack() as ctx:
        sb = lambda n, shape, dt=F32: ctx.enter_context(nc.sbuf_tensor("a_" + n, shape, dt))
        sems = []

        def sem(n):
            sems.append(ctx.enter_context(nc.semaphore("a_" + n)))
            return sems[-1]

        LB = B // 4
        ctx_in = sb("ctx_in", [PT, 4, SF, D])
        ctxT = sb("ctxT", [PT, 4, S + 2])
        kT = sb("kT", [PT, 2, SF * PT])
        v = sb("v", [PT, 4, SF * D])
        vz = sb("vz", [PT, 2, SF * D])
        qbd = sb("qbd", [PT, 2, NH, L])
        prob = sb("prob", [PT, 4, SF * NH, L])
        top = sb("top", [PT, 2, SF * NH])
        total = sb("total", [PT, 2, SF * NH])
        inv = sb("inv", [PT, 2, SF * NH])
        attn = sb("attn", [PT, HG, TPB, L])
        left_in = sb("left_in", [B, D])
        leftT = sb("leftT", [PT, B])
        klT = sb("klT", [PT, B])
        vlT = sb("vlT", [PT, B])
        lprod = sb("lprod", [PT, B, L])
        lprob = sb("lprob", [PT, LB, L])
        ltop = sb("ltop", [PT, LB])
        linv = sb("linv", [PT, LB])
        lattn = sb("lattn", [PT, TOK])
        pairs = sb("pairs", [PT, 2, TPB * L])
        heads = sb("heads", [PT, TPB * L])
        summed = sb("summed", [PT, TPB * L])
        bv_rest = sb("bv_rest", [3, D])
        bv_parts = sb("bv_parts", [3, 3, D], BF16)
        bv_sum = sb("bv_sum", [3, 2, D])
        bv3 = sb("bv3", [3, SF, D], BF16)
        ones3 = sb("ones3", [3, PT], BF16)

        wq, wk, wv, wo = (st.w[n] for n in ("L0_xattn_Wq", "L0_xattn_Wk", "L0_xattn_Wv", "L0_xattn_Wo"))
        bk, bvc = st.col["L0_xattn_bk"], st.col["L0_xattn_bv"]

        ph = sb("ph", [PT, 6])
        w = sb("w", [PT, 8])
        re = sb("re", [PT, L + 1])
        im = sb("im", [PT, L + 1])
        t1 = sb("t1", [PT, L])
        t2 = sb("t2", [PT, L])
        filt, past = st.filt, st.past
        ph_in, mag2_done, act_done, scale_done, power_done = map(sem, (
            "ph_in", "mag2_done", "act_done", "scale_done", "power_done"))

        lload, lturn, lkept, lkv, lkv_kept, lprod_done, ls_done, lsm, lsp, latt, bv_step, bias_in = map(
            sem, ("lload", "lturn", "lkept", "lkv", "lkv_kept", "lprod_done", "ls_done", "lsm", "lsp", "latt",
                  "bv_step", "bias_in"))
        lscore = psum[:, 0, :].rearrange("p (b l) -> p b l", l=L)
        with nc.Block() as block:

            @block.sync
            def _(sp):
                sp.dma_start(left_in[:], st.ctx[:, S - 1, :]).then_inc(lload, 16)
                for k, n in enumerate(("phazor", "phazor_init")):
                    sp.dma_start(ph[:, 2 * k:2 * k + 2], st.dram["L0_attn_" + n]).then_inc(ph_in, 16)
                for k, n in enumerate(("last_conv_re", "last_conv_im")):
                    sp.dma_start(ph[:, 4 + k:5 + k], st.dram["L0_attn_" + n].rearrange("(p o) -> p o", o=1)
                                 ).then_inc(ph_in, 16)
                sp.dma_start(bv_rest[:], st.dram["L0_xattn_bv"].rearrange("(o d) -> o d", o=1).broadcast_to([3, D])
                             ).then_inc(bias_in, 16)

            @block.gpsimd
            def _(pool):
                nc.gpsimd.memset(ones3[:], 1.0)
                for c in (0, S + 1):
                    nc.gpsimd.memset(ctxT[:, :, c:c + 1], 0.0)

            @block.tensor
            def _(pe):
                pe.wait_ge(lload, 16)
                nc.tensor.transpose(psum[:, 4, 0:B], left_in[:], cst["ident"][0:B, 0:B]).then_inc(lturn, 1)
                pe.wait_ge(lkept, 1)
                nc.tensor.matmul(psum[:, 5, 0:B], wk, leftT[:], start=True, stop=True)
                nc.tensor.matmul(psum[:, 5, B:2 * B], wv, leftT[:], start=True, stop=True).then_inc(lkv, 1)
                pe.wait_ge(lprod_done, 1)
                for k in range(4):
                    mm = nc.tensor.matmul(psum[32 * k:32 * (k + 1), 0, :], cst["head32"],
                                          lprod[:, LB * k:LB * (k + 1), :], start=True, stop=True,
                                          tile_position=(0, 32 * k))
                mm.then_inc(ls_done, 1)
                pe.wait_ge(lsp, 1)
                for k in range(4):
                    nc.tensor.matmul(psum[:, k, :], cst["spread"][:, PT * k:PT * (k + 1)], lprob[:],
                                     start=True, stop=True).then_inc(latt, 1)

            @block.vector
            def _(dve):
                dve.wait_ge(lturn, 1)
                nc.vector.tensor_copy(leftT[:], psum[:, 4, 0:B]).then_inc(lkept, 1)
                dve.wait_ge(lkv, 1)
                nc.vector.tensor_scalar(klT[:], psum[:, 5, 0:B], bk, None, ALU.add).then_inc(lkv_kept, 1)
                nc.vector.tensor_scalar(vlT[:], psum[:, 5, B:2 * B], bvc, None, ALU.add).then_inc(lkv_kept, 1)
                dve.wait_ge(lkv_kept, 2)
                nc.vector.tensor_tensor(lprod[:], qT[:].rearrange("p (b l) -> p b l", l=L),
                                        klT[:].unsqueeze(2).broadcast_to([PT, B, L]), ALU.mult).then_inc(lprod_done, 1)
                dve.wait_ge(ph_in, 64)
                nc.vector.tensor_tensor(w[:, 0:2], ph[:, 0:2], ph[:, 0:2], ALU.mult).then_inc(mag2_done, 1)
                nc.vector.memset(re[:, 0:1], 1.0).then_inc(mag2_done, 1)
                nc.vector.memset(im[:, 0:1], 0.0).then_inc(mag2_done, 1)
                dve.wait_ge(mag2_done, 3)
                nc.vector.tensor_tensor(w[:, 2:3], w[:, 0:1], w[:, 1:2], ALU.add).then_inc(mag2_done, 1)
                dve.wait_ge(bias_in, 16)
                for k in range(3):
                    wait_count(dve, bv_step, 2 * k)
                    nc.vector.tensor_copy(bv_parts[:, k], bv_rest[:]).then_inc(bv_step, 1)
                    dve.wait_ge(bv_step, 2 * k + 1)
                    nc.vector.tensor_tensor(bv_rest[:], bv_rest[:], bv_parts[:, k], ALU.subtract).then_inc(bv_step, 1)
                nc.vector.tensor_scalar(bv_sum[:, 0], bv_parts[:, 0], cst["ident"][0:3, 0:1], None, ALU.mult
                                        ).then_inc(bv_step, 1)
                dve.wait_ge(bv_step, 7)
                nc.vector.scalar_tensor_tensor(bv_sum[:, 1], bv_parts[:, 1], cst["ident"][0:3, 1:2], bv_sum[:, 0],
                                               ALU.mult, ALU.add).then_inc(bv_step, 1)
                dve.wait_ge(bv_step, 8)
                nc.vector.scalar_tensor_tensor(bv_sum[:, 0], bv_parts[:, 2], cst["ident"][0:3, 2:3], bv_sum[:, 1],
                                               ALU.mult, ALU.add).then_inc(bv_step, 1)
                dve.wait_ge(bv_step, 9)
                for t in range(SF):
                    nc.vector.tensor_copy(bv3[:, t], bv_sum[:, 0])
                dve.wait_ge(act_done, 1)
                nc.vector.reciprocal(w[:, 5:6], w[:, 3:4]).then_inc(scale_done, 1)
                dve.wait_ge(act_done, 2)
                dve.wait_ge(scale_done, 1)
                nc.vector.tensor_tensor(w[:, 6:7], w[:, 4:5], w[:, 5:6], ALU.mult).then_inc(scale_done, 1)
                dve.wait_ge(scale_done, 2)
                nc.vector.tensor_scalar(re[:, 1:2], ph[:, 0:1], w[:, 6:7], None, ALU.mult).then_inc(power_done, 1)
                nc.vector.tensor_scalar(im[:, 1:2], ph[:, 1:2], w[:, 6:7], None, ALU.mult).then_inc(power_done, 1)
                done = 2
                m = 1
                while m < L:
                    a, b = re[:, m:m + 1], im[:, m:m + 1]
                    dve.wait_ge(power_done, done)
                    nc.vector.tensor_scalar(t1[:, 0:m], im[:, 1:m + 1], b, None, ALU.mult).then_inc(power_done, 1)
                    nc.vector.tensor_scalar(t2[:, 0:m], im[:, 1:m + 1], a, None, ALU.mult).then_inc(power_done, 1)
                    dve.wait_ge(power_done, done + 2)
                    nc.vector.scalar_tensor_tensor(re[:, m + 1:2 * m + 1], re[:, 1:m + 1], a, t1[:, 0:m],
                                                   ALU.mult, ALU.subtract).then_inc(power_done, 1)
                    nc.vector.scalar_tensor_tensor(im[:, m + 1:2 * m + 1], re[:, 1:m + 1], b, t2[:, 0:m],
                                                   ALU.mult, ALU.add).then_inc(power_done, 1)
                    done += 4
                    m *= 2
                dve.wait_ge(power_done, done)
                nc.vector.tensor_scalar(t1[:], im[:, 0:L], ph[:, 3:4], None, ALU.mult).then_inc(power_done, 1)
                nc.vector.tensor_scalar(t2[:], im[:, 1:L + 1], ph[:, 5:6], None, ALU.mult).then_inc(power_done, 1)
                dve.wait_ge(power_done, done + 2)
                nc.vector.scalar_tensor_tensor(filt[:], re[:, 0:L], ph[:, 2:3], t1[:], ALU.mult, ALU.subtract
                                               ).then_inc(power_done, 1)
                nc.vector.scalar_tensor_tensor(past[:], re[:, 1:L + 1], ph[:, 4:5], t2[:], ALU.mult, ALU.subtract
                                               ).then_inc(power_done, 1)
                dve.wait_ge(power_done, done + 4)
                dve.wait_ge(ls_done, 1)
                nc.vector.tensor_reduce(ltop[:], lscore, AX_X, ALU.max).then_inc(lsm, 1)
                dve.wait_ge(lsm, 1)
                nc.vector.tensor_tensor(lprob[:], lscore, ltop[:].unsqueeze(2).broadcast_to([PT, LB, L]),
                                        ALU.subtract).then_inc(lsm, 1)
                dve.wait_ge(lsm, 3)
                nc.vector.tensor_reduce(ltop[:], lprob[:], AX_X, ALU.add).then_inc(lsm, 1)
                dve.wait_ge(lsm, 4)
                nc.vector.reciprocal(linv[:], ltop[:]).then_inc(lsm, 1)
                dve.wait_ge(lsm, 5)
                nc.vector.tensor_tensor(lprob[:], lprob[:], linv[:].unsqueeze(2).broadcast_to([PT, LB, L]),
                                        ALU.mult).then_inc(lsp, 1)
                for k in range(4):
                    dve.wait_ge(latt, k + 1)
                    nc.vector.tensor_tensor(
                        lattn[:, 512 * k:512 * (k + 1)].rearrange("p (b l) -> p b l", l=L),
                        psum[:, k, :].rearrange("p (b l) -> p b l", l=L),
                        vlT[:, 16 * k:16 * (k + 1)].unsqueeze(2).broadcast_to([PT, 16, L]), ALU.mult)

            @block.scalar
            def _(act):
                act.wait_ge(mag2_done, 4)
                nc.scalar.activation(w[:, 3:4], w[:, 2:3], ACT.Sqrt).then_inc(act_done, 1)
                act.wait_ge(act_done, 1)
                nc.scalar.activation(w[:, 4:5], w[:, 3:4], ACT.Exp, scale=-1.0).then_inc(act_done, 1)
                act.wait_ge(lsm, 2)
                nc.scalar.activation(lprob[:], lprob[:], ACT.Exp).then_inc(lsm, 1)

        load_done = [sem(f"load_done{k}") for k in range(4)]
        store_done = [sem(f"store_done{k}") for k in range(4)]
        (turned, left_put, ctxT_kept, kT_kept, v_done, v_kept, qbd_done, s_done, top_done, sub_done, exp_done,
         total_done, inv_done, vz_done, pv_done, attn_kept, pairs_done, heads_done, summed_done, o_done, x_done) = map(sem, (
             "turned", "left_put", "ctxT_kept", "kT_kept", "v_done", "v_kept", "qbd_done", "s_done",
             "top_done", "sub_done", "exp_done", "total_done", "inv_done", "vz_done", "pv_done", "attn_kept",
             "pairs_done", "heads_done", "summed_done", "o_done", "x_done"))
        scores = [psum[:, 0:2, :].rearrange("p t (h l) -> p (t h) l", l=L),
                  psum[:, 2:4, :].rearrange("p t (h l) -> p (t h) l", l=L)]
        T_BANK, KV_BANK, O_BANK, A_BANK = 4, 5, 6, 7
        V_AT = SF * PT
        KV, SC, PV, OUT = 1, 2, 4, 2

        with nc.Block() as block:

            @block.sync
            def _(sp):
                def step(i):
                    for j in range(TPB):
                        n = TPB * i + j
                        if live(i, j, 0):
                            wait_count(sp, turned, n - 3)
                            sp.dma_start(ctx_in[:, j, :, :], st.ctx[n, 0:SF * PT, :].rearrange(
                                "(t p) d -> p t d", p=PT)).then_inc(load_done[j], 16)
                tile_steps(sp, step, 1, 0)

            @block.gpsimd
            def _(pool):
                def step(i):
                    for j in range(TPB):
                        if live(i, j, 0):
                            n = TPB * i + j
                            wait_count(pool, v_done, n - 3)
                            wait_count(pool, store_done[j], 16 * i)
                            nc.gpsimd.tensor_copy(ctxT[:, j, S:S + 1], leftT[:, bass.ds(n, 1)]).then_inc(left_put, 1)
                        if live(i, j, KV):
                            n = TPB * i + j - KV
                            wait_count(pool, s_done, n - 1)
                            nc.gpsimd.tensor_tensor(
                                qbd[:, (j - KV) % 2], qT[:, bass.ds(n * L, L)].unsqueeze(1).broadcast_to([PT, NH, L]),
                                cst["head16"].unsqueeze(2).broadcast_to([PT, NH, L]), ALU.mult).then_inc(qbd_done, 1)
                        if live(i, j, PV):
                            n = TPB * i + j - PV
                            pool.wait_ge(inv_done, n + 1)
                            pool.wait_ge(v_kept, n + 1)
                            wait_count(pool, pv_done, n - 1)
                            nc.gpsimd.tensor_tensor(
                                vz[:, (j - PV) % 2].rearrange("p (h d) -> p h d", d=DH),
                                v[:, (j - PV) % 4].rearrange("p (h d) -> p h d", d=DH),
                                inv[:, (j - PV) % 2].unsqueeze(2).broadcast_to([PT, SF * NH, DH]),
                                ALU.mult).then_inc(vz_done, 1)
                        if j == 0 and live_tile(i, OUT):
                            pool.wait_ge(attn_kept, i - OUT + 1)
                            nc.gpsimd.tensor_tensor(pairs[:], attn[:, 0:2].rearrange("p h b l -> p h (b l)"),
                                                    attn[:, 2:4].rearrange("p h b l -> p h (b l)"), ALU.add
                                                    ).then_inc(pairs_done, 1)
                        if j == 1 and live_tile(i, OUT):
                            pool.wait_ge(pairs_done, i - OUT + 1)
                            nc.gpsimd.tensor_tensor(heads[:], pairs[:, 0], pairs[:, 1], ALU.add
                                                    ).then_inc(heads_done, 1)
                            pool.wait_ge(heads_done, i - OUT + 1)
                            wait_count(pool, o_done, i - OUT)
                            nc.gpsimd.tensor_tensor(summed[:], heads[:], lattn[:, bass.ds((i - OUT) * PT, PT)],
                                                    ALU.add).then_inc(summed_done, 1)
                tile_steps(pool, step)

            @block.tensor
            def _(pe):
                def step(i):
                    for j in range(TPB):
                        n = TPB * i + j
                        if live(i, j, 0):
                            pe.wait_ge(load_done[j], 16 * (i + 1))
                            wait_count(pe, ctxT_kept, n)
                            for t in range(SF):
                                mm = nc.tensor.transpose(psum[:, T_BANK, PT * t:PT * (t + 1)], ctx_in[:, j, t, :],
                                                         st.ident)
                            mm.then_inc(turned, 1)
                        if live(i, j, SC):
                            m = n - SC
                            pe.wait_ge(kT_kept, m + 1)
                            pe.wait_ge(qbd_done, m + 1)
                            wait_count(pe, sub_done, m - 1)
                            for t in range(SF):
                                mm = nc.tensor.matmul(psum[:, 2 * ((j - SC) % 2) + t, :],
                                                      kT[:, (j - SC) % 2, PT * t:PT * (t + 1)],
                                                      qbd[:, (j - SC) % 2], start=True, stop=True)
                            mm.then_inc(s_done, 1)
                        if live(i, j, KV):
                            m = n - KV
                            c = (j - KV) % 4
                            pe.wait_ge(ctxT_kept, m + 1)
                            wait_count(pe, v_kept, m)
                            nc.tensor.matmul(psum[:, KV_BANK, 0:SF * PT], wk, ctxT[:, c, 1:SF * PT + 1],
                                             start=True, stop=True)
                            nc.tensor.matmul(psum[:, KV_BANK, V_AT:V_AT + SF * D], ones3[:],
                                             bv3[:].rearrange("p t d -> p (t d)"), start=True, stop=False)
                            for t in range(SF):
                                mm = nc.tensor.matmul(psum[:, KV_BANK, V_AT + D * t:V_AT + D * (t + 1)],
                                                      ctxT[:, c, 1 + PT * t:1 + PT * (t + 1)], wv,
                                                      start=False, stop=(t == SF - 1))
                            mm.then_inc(v_done, 1)
                        if live(i, j, PV):
                            m = n - PV
                            c = (j - PV) % 4
                            pe.wait_ge(vz_done, m + 1)
                            if c == 0:
                                wait_count(pe, attn_kept, i - 1)
                            for t in range(SF):
                                for g in range(HG):
                                    mm = nc.tensor.matmul(
                                        psum[32 * g:32 * (g + 1), A_BANK, PT * c:PT * (c + 1)],
                                        vz[:, (j - PV) % 2, D * t + 32 * g:D * t + 32 * (g + 1)],
                                        prob[:, c, NH * t + HG * g:NH * t + HG * (g + 1), :],
                                        start=(t == 0), stop=(t == SF - 1), tile_position=(0, 32 * g))
                            mm.then_inc(pv_done, 1)
                        if j == 2 and live_tile(i, OUT):
                            t = i - OUT
                            pe.wait_ge(summed_done, t + 1)
                            wait_count(pe, x_done, t)
                            o = psum[:, O_BANK, 0:D]
                            nc.tensor.matmul(o, summed[:], wo, start=True, stop=False)
                            nc.tensor.matmul(o, cst["ones"][0:1, :], st.row["L0_xattn_bo"], start=False, stop=True
                                             ).then_inc(o_done, 1)
                tile_steps(pe, step)

            @block.vector
            def _(dve):
                def step(i):
                    for j in range(TPB):
                        n = TPB * i + j
                        if j == 3 and live_tile(i, OUT):
                            dve.wait_ge(o_done, i - OUT + 1)
                            xt = x[:, bass.ds(i - OUT, 1), :].rearrange("p o d -> p (o d)")
                            nc.vector.tensor_tensor(xt, xt, psum[:, O_BANK, 0:D], ALU.add).then_inc(x_done, 1)
                        if live(i, j, SC):
                            m = n - SC
                            sc = scores[(j - SC) % 2]
                            dve.wait_ge(s_done, m + 1)
                            nc.vector.tensor_reduce(top[:, (j - SC) % 2], sc, AX_X, ALU.max).then_inc(top_done, 1)
                        if live(i, j, SC + 1):
                            m = n - SC - 1
                            c = (j - SC - 1) % 4
                            dve.wait_ge(exp_done, m + 1)
                            nc.vector.tensor_reduce(total[:, c % 2], prob[:, c], AX_X, ALU.add).then_inc(total_done, 1)
                        if live(i, j, SC):
                            m = n - SC
                            c = (j - SC) % 4
                            dve.wait_ge(top_done, m + 1)
                            wait_count(dve, pv_done, m - 3)
                            nc.vector.tensor_tensor(prob[:, c], scores[c % 2],
                                                    top[:, c % 2].unsqueeze(2).broadcast_to([PT, SF * NH, L]),
                                                    ALU.subtract).then_inc(sub_done, 1)
                        if live(i, j, SC + 1):
                            m = n - SC - 1
                            c = (j - SC - 1) % 2
                            dve.wait_ge(total_done, m + 1)
                            wait_count(dve, vz_done, m - 1)
                            nc.vector.reciprocal(inv[:, c], total[:, c]).then_inc(inv_done, 1)
                tile_steps(dve, step)

            @block.scalar
            def _(act):
                nc.scalar.preload_act_table(ACT.Exp)

                def step(i):
                    for j in range(TPB):
                        n = TPB * i + j
                        if live(i, j, 0):
                            act.wait_ge(turned, n + 1)
                            wait_count(act, v_done, n - 3)
                            wait_count(act, store_done[j], 16 * i)
                            nc.scalar.activation(ctxT[:, j, 1:SF * PT + 1], psum[:, T_BANK, 0:SF * PT], ACT.Copy
                                                 ).then_inc(ctxT_kept, 1)
                        if live(i, j, KV):
                            m = n - KV
                            act.wait_ge(left_put, m + 1)
                            act.wait_ge(ctxT_kept, m + 1)
                            act.dma_start(st.ctx_all[:, bass.ds(m, 1), :].rearrange("p o s -> p (o s)"),
                                          ctxT[:, (j - KV) % 4, :]).then_inc(store_done[(j - KV) % 4], 16)
                            act.wait_ge(v_done, m + 1)
                            wait_count(act, s_done, m - 1)
                            nc.scalar.activation(kT[:, (j - KV) % 2], psum[:, KV_BANK, 0:SF * PT], ACT.Identity,
                                                 bias=bk).then_inc(kT_kept, 1)
                            wait_count(act, vz_done, m - 3)
                            nc.scalar.activation(v[:, (j - KV) % 4], psum[:, KV_BANK, V_AT:V_AT + SF * D], ACT.Copy
                                                 ).then_inc(v_kept, 1)
                        if j == 3 and live_tile(i, 1):
                            t = i - 1
                            act.wait_ge(pv_done, TPB * (t + 1))
                            wait_count(act, pairs_done, t)
                            for h in range(HG):
                                ins = nc.scalar.activation(attn[:, h], psum[:, A_BANK, :].rearrange(
                                    "p (b h l) -> p b h l", b=TPB, h=HG)[:, :, h, :], ACT.Copy,
                                    scale=cst["head4"][:, h:h + 1])
                            ins.then_inc(attn_kept, 1)
                        if live(i, j, SC):
                            m = n - SC
                            act.wait_ge(sub_done, m + 1)
                            nc.scalar.activation(prob[:, (j - SC) % 4], prob[:, (j - SC) % 4], ACT.Exp
                                                 ).then_inc(exp_done, 1)
                tile_steps(act, step)
                for k in range(4):
                    act.wait_ge(store_done[k], 16 * NT)
        clear_counts(nc, sems)


class ContextProjection:
    BANKS = 4
    GROUPS = B // 4

    def __init__(self, nc, st, ctx):
        self.nc, self.st = nc, st
        sb = lambda n, shape: ctx.enter_context(nc.sbuf_tensor("p_" + n, shape, F32))
        self.sems = []

        def sem(n):
            self.sems.append(ctx.enter_context(nc.semaphore("p_" + n)))
            return self.sems[-1]

        self.ctxT = sb("ctxT", [PT, 4, S + 2])
        self.v = sb("v", [PT, 4, SF * D])
        self.load_done = [sem(f"load_done{k}") for k in range(4)]
        self.store_done = [sem(f"store_done{k}") for k in range(4)]
        self.v_done, self.k_done, self.v_kept, self.k_kept = map(sem, ("v_done", "k_done", "v_kept", "k_kept"))

    def load(self, sp, g, j):
        n = 4 * g + j
        wait_count(sp, self.k_done, n - 3)
        sp.dma_start(self.ctxT[:, j, :], self.st.ctx_all[:, bass.ds(n, 1), :].rearrange("p o s -> p (o s)")
                     ).then_inc(self.load_done[j], 16)

    def project(self, pe, g, j):
        nc, st, n = self.nc, self.st, 4 * g + j
        bank = self.BANKS + 2 * (j % 2)
        pe.wait_ge(self.load_done[j], 16 * (g + 1))
        wait_count(pe, self.v_kept, n - 1)
        for t in range(SF):
            for tap in range(3):
                mm = nc.tensor.matmul(st.psum[:, bank, D * t:D * (t + 1)],
                                      self.ctxT[:, j, tap + PT * t:tap + PT * (t + 1)], st.convw[:, 2, tap, :],
                                      start=(tap == 0), stop=(tap == 2))
        mm.then_inc(self.v_done, 1)
        wait_count(pe, self.k_kept, n - 1)
        for tap in range(3):
            mm = nc.tensor.matmul(st.psum[:, bank + 1, 0:S], st.convw[:, 1, tap, :], self.ctxT[:, j, tap:tap + S],
                                  start=(tap == 0), stop=(tap == 2))
        mm.then_inc(self.k_done, 1)

    def keep(self, act, g, j):
        nc, st, n = self.nc, self.st, 4 * g + j
        bank = self.BANKS + 2 * (j % 2)
        act.wait_ge(self.v_done, n + 1)
        wait_count(act, self.store_done[j], 16 * g)
        nc.scalar.activation(self.v[:, j, :], st.psum[:, bank, 0:SF * D], ACT.Copy).then_inc(self.v_kept, 1)
        act.wait_ge(self.k_done, n + 1)
        nc.scalar.activation(st.ctx_all[:, bass.ds(n, 1), 0:S].rearrange("p o s -> p (o s)"),
                             st.psum[:, bank + 1, 0:S], ACT.Identity, bias=st.col["L1_xattn_bk"]
                             ).then_inc(self.k_kept, 1)
        act.wait_ge(self.v_kept, n + 1)
        act.dma_start(st.v_dram[bass.ds(n, 1)].rearrange("o p d -> p (o d)"), self.v[:, j, :]
                      ).then_inc(self.store_done[j], 16)

    def run(self, eng, work, groups):
        first, end = groups
        if first == 0:
            for j in range(4):
                work(eng, 0, j)
        if max(first, 1) < end:
            with eng.Fori(max(first, 1), end) as g:
                for j in range(4):
                    work(eng, g, j)

    def load_ahead(self, sp, groups):
        self.run(sp, self.load, (groups[0] + 1, min(groups[1] + 1, self.GROUPS)))

    def finish(self, sp):
        for k in range(4):
            sp.wait_ge(self.store_done[k], 16 * self.GROUPS)


def long_convolution(nc, st, ahead):
    x, psum = st.x, st.psum
    with ExitStack() as ctx:
        sb = lambda n, shape, dt=F32: ctx.enter_context(nc.sbuf_tensor("b_" + n, shape, dt))
        sems = []

        def sem(n):
            sems.append(ctx.enter_context(nc.semaphore("b_" + n)))
            return sems[-1]

        filt, past = st.filt, st.past
        y = sb("y", [PT, B, L])
        tap_done, turned, x_done = map(sem, ("tap_done", "turned", "x_done"))
        with nc.Block() as block:

            @block.sync
            def _(sp):
                ahead.load_ahead(sp, CONV_AHEAD)

            @block.scalar
            def _(act):
                ahead.run(act, ahead.keep, CONV_AHEAD)

            @block.vector
            def _(dve):
                nc.vector.scalar_tensor_tensor(y[:], st.xnT, filt[:, 0:1],
                                               past[:].unsqueeze(1).broadcast_to([PT, B, L]),
                                               ALU.mult, ALU.add).then_inc(tap_done, 1)
                for j in range(1, L):
                    dve.wait_ge(tap_done, j)
                    nc.vector.scalar_tensor_tensor(y[:, :, j:L], st.xnT[:, :, 0:L - j], filt[:, j:j + 1], y[:, :, j:L],
                                                   ALU.mult, ALU.add).then_inc(tap_done, 1)
                for k in range(4):
                    dve.wait_ge(turned, k + 1)
                    xk = x[:, 4 * k:4 * (k + 1), :].rearrange("p t d -> p (t d)")
                    nc.vector.tensor_tensor(xk, xk, psum[:, k, :], ALU.add).then_inc(x_done, 1)
                    dve.wait_ge(x_done, k + 1)
                    for t in range(4 * k, 4 * (k + 1)):
                        nc.vector.bn_stats(st.stats[:, t, :], x[:, t, :])

            @block.tensor
            def _(pe):
                ahead.run(pe, ahead.project, CONV_AHEAD)
                pe.wait_ge(tap_done, L)
                for k in range(4):
                    for j in range(4):
                        t = 4 * k + j
                        mm = nc.tensor.transpose(psum[:, k, PT * j:PT * (j + 1)],
                                                 y[:, TPB * t:TPB * (t + 1), :].rearrange("p b l -> p (b l)"), st.ident)
                    mm.then_inc(turned, 1)
        clear_counts(nc, sems)


def routed_ffn(nc, st, ahead, once):
    x, xn, psum, cst = st.x, st.xn, st.psum, st.cst
    with ExitStack() as ctx:
        sb = lambda n, shape, dt=F32: ctx.enter_context(nc.sbuf_tensor("c_" + n, shape, dt))
        sems = []

        def sem(n):
            sems.append(ctx.enter_context(nc.semaphore("c_" + n)))
            return sems[-1]

        scattered, gathered, y_stored = st.scattered, st.gathered, st.y_stored
        slots = nc.dram_tensor("slots_dram", (NE * CAP + TOK, D), F32).ap()
        answers = nc.dram_tensor("answers_dram", (NE * CAP, D), F32).ap()
        wg, bg, b1 = st.wg, st.bg, st.b1
        b1T = sb("b1T", [PT, NE * HC])
        logit = sb("logit", [PT, NT, NE])
        cand = sb("cand", [PT, NT, NE])
        onehot = sb("onehot", [PT, NT, NE])
        before = sb("before", [PT, 2, NT, NE])
        r = sb("r", [PT, 10, NT])
        dst = sb("dst", [PT, NT], U32)
        src = sb("src", [PT, NT], U32)
        back = sb("back", [PT, NT, D])
        w1 = sb("w1", [PT, EB, HID])
        w2 = sb("w2", [PT, EB, HC, D])
        b2 = sb("b2", [1, EB, D])
        rows = sb("rows", [PT, EB, D])
        rowsT = sb("rowsT", [PT, EB, CAP])
        hT = sb("hT", [PT, EB, HC, CAP])
        y = sb("y", [PT, EB, D])
        top, total, gate, first, count, keep, slot, gk, dstf, srcf = (r[:, k, :] for k in range(10))
        over_e = lambda a: a.unsqueeze(2).broadcast_to([PT, NT, NE])

        LOGIT_BANK = 3

        def logits(pe, k):
            for t in range(4 * k, 4 * (k + 1)):
                nc.tensor.matmul(psum[:, LOGIT_BANK, NE * t:NE * (t + 1)], st.xnT_flat[:, PT * t:PT * (t + 1)], wg[:],
                                 start=True, stop=True)

        layer_norm(nc, st, "n2", stats_made=True, on_group=logits)
        (zeroed, zero_stored, b1_turned, route, exp_done, count_done, dst_done,
         prefix_done) = map(sem, ("zeroed", "zero_stored", "b1_turned", "route", "exp_done",
                       "count_done", "dst_done", "prefix_done"))
        with nc.Block() as block:

            @block.sync
            def _(sp):
                sp.wait_ge(zeroed, 1)
                sp.dma_start(slots[0:NE * CAP, :].rearrange("(p r) d -> p r d", p=PT), back[:]
                             ).then_inc(zero_stored, 16)
                ahead.load_ahead(sp, ROUTE_AHEAD)
                sp.wait_ge(zero_stored, 16)

            @block.tensor
            def _(pe):
                nc.tensor.transpose(psum[:, 2, 0:NE * HC], b1[:], cst["ident"][0:NE * HC, 0:NE * HC]
                                    ).then_inc(b1_turned, 1)
                first, end = ROUTE_AHEAD
                for j in range(3):
                    ahead.project(pe, first, j)
                pe.wait_ge(route, 10)
                nc.tensor.matmul(psum[:, 1, 0:NT * NE], cst["upto"], onehot[:], start=True, stop=False)
                nc.tensor.matmul(psum[:, 1, 0:NT * NE], cst["ones"], before[:, 0], start=False, stop=True
                                 ).then_inc(count_done, 1)
                ahead.project(pe, first, 3)
                ahead.run(pe, ahead.project, (first + 1, end))

            @block.scalar
            def _(act):
                act.wait_ge(route, 4)
                nc.scalar.activation(logit[:], logit[:], ACT.Exp).then_inc(exp_done, 1)
                act.wait_ge(b1_turned, 1)
                nc.scalar.activation(b1T[:], psum[:, 2, 0:NE * HC], ACT.Copy)
                ahead.run(act, ahead.keep, ROUTE_AHEAD)

            @block.vector
            def _(dve):
                n = [0]

                def counted(instruction):
                    n[0] += 1
                    instruction.then_inc(route, 1)

                flat = lambda a: a.rearrange("p t e -> p (t e)")
                ps = psum[:, LOGIT_BANK, 0:NT * NE].rearrange("p (t e) -> p t e", e=NE)
                counted(nc.vector.tensor_tensor(logit[:], ps, bg[:].unsqueeze(1).broadcast_to([PT, NT, NE]), ALU.add))
                nc.vector.memset(back[:], 0.0).then_inc(zeroed, 1)
                dve.wait_ge(route, 1)
                counted(nc.vector.tensor_reduce(top, logit[:], AX_X, ALU.max))
                dve.wait_ge(route, 2)
                counted(nc.vector.tensor_tensor(logit[:], logit[:], over_e(top), ALU.subtract))
                dve.wait_ge(route, 3)
                counted(nc.vector.scalar_tensor_tensor(cand[:], logit[:], 0.0,
                                                       cst["rank16"].unsqueeze(1).broadcast_to([PT, NT, NE]),
                                                       ALU.is_ge, ALU.mult))
                dve.wait_ge(exp_done, 1)
                counted(nc.vector.tensor_reduce(total, logit[:], AX_X, ALU.add))
                dve.wait_ge(route, 5)
                counted(nc.vector.tensor_reduce(first, cand[:], AX_X, ALU.max))
                dve.wait_ge(route, 6)
                counted(nc.vector.tensor_tensor(onehot[:], cand[:], over_e(first), ALU.is_equal))
                dve.wait_ge(route, 7)
                counted(nc.vector.memset(before[:, 0, 0:1, :], 0.0))
                counted(nc.vector.tensor_copy(before[:, 0, 1:NT, :], onehot[:, 0:NT - 1, :]))
                a = 0
                for k in range(4):
                    m = 1 << k
                    dve.wait_ge(prefix_done, 2 * k) if k else dve.wait_ge(route, 9)
                    nc.vector.tensor_copy(before[:, 1 - a, 0:m, :], before[:, a, 0:m, :]).then_inc(prefix_done, 1)
                    nc.vector.tensor_tensor(before[:, 1 - a, m:NT, :], before[:, a, m:NT, :],
                                            before[:, a, 0:NT - m, :], ALU.add).then_inc(prefix_done, 1)
                    a = 1 - a
                dve.wait_ge(prefix_done, 8)
                counted(nc.vector.reciprocal(gate, total))
                dve.wait_ge(count_done, 1)
                ps = psum[:, 1, 0:NT * NE].rearrange("p (t e) -> p t e", e=NE)
                counted(nc.vector.tensor_tensor(cand[:], ps, onehot[:], ALU.mult))
                dve.wait_ge(route, 11)
                counted(nc.vector.tensor_reduce(count, cand[:], AX_X, ALU.add))
                dve.wait_ge(route, 12)
                counted(nc.vector.tensor_scalar(keep, count, float(CAP), None, ALU.is_le))
                counted(nc.vector.tensor_scalar(slot, first, -float(CAP), float(NE * CAP - 1), ALU.mult, ALU.add))
                dve.wait_ge(route, 14)
                counted(nc.vector.tensor_tensor(slot, slot, count, ALU.add))
                counted(nc.vector.tensor_tensor(gk, gate, keep, ALU.mult))
                dve.wait_ge(route, 16)
                counted(nc.vector.tensor_tensor(dstf, slot, cst["token_row"], ALU.subtract))
                counted(nc.vector.tensor_tensor(srcf, slot, keep, ALU.mult))
                dve.wait_ge(route, 18)
                counted(nc.vector.tensor_tensor(dstf, dstf, keep, ALU.mult))
                nc.vector.tensor_copy(src[:], srcf)
                dve.wait_ge(route, 19)
                counted(nc.vector.tensor_tensor(dstf, dstf, cst["token_row"], ALU.add))
                dve.wait_ge(route, 20)
                nc.vector.tensor_copy(dst[:], dstf).then_inc(dst_done, 1)

            @block.gpsimd
            def _(pool):
                pool.wait_ge(dst_done, 1)
                pool.wait_ge(zero_stored, 16)
                for t in range(NT):
                    nc.gpsimd.indirect_dma_start(
                        out=slots, out_offset=bass.IndirectOffsetOnAxis(ap=dst[:, t:t + 1], axis=0),
                        in_=xn[:, t, :], in_offset=None).then_inc(scattered, 16)
                pool.wait_ge(scattered, 16 * NT)

        row_in = [sem(f"row_in{k}") for k in range(EB)]
        w_in = [sem(f"w_in{k}") for k in range(EB)]
        turned, rowsT_kept, h_done, hT_kept, y_done, y_kept, updated = map(sem, (
            "turned", "rowsT_kept", "h_done", "hT_kept", "y_done", "y_kept", "updated"))
        HL, YL = 1, 2
        is_live = lambda i, j, lag: live(i, j, lag, NE, EB)
        steps = lambda eng, step: tile_steps(eng, step, 1, 1, NE // EB)

        def batch_ahead(i, k):
            return EXPERT_AHEAD[0] + 2 * EB // 4 * i + k // 4, k % 4

        with nc.Block() as block:

            @block.sync
            def _(sp):
                def step(i):
                    for j in range(EB):
                        e = EB * i + j
                        if is_live(i, j, 0):
                            wait_count(sp, turned, e - EB + 1)
                            sp.dma_start(rows[:, j, :], slots[bass.ds(e * CAP, CAP), :]).then_inc(row_in[j], 16)
                            wait_count(sp, y_done, e - EB + 1)
                            sp.dma_start(w1[:, j, :], st.dram["L0_ffn_W1"][e]).then_inc(w_in[j], 16)
                            sp.dma_start(w2[:, j], st.dram["L0_ffn_W2"][e].rearrange("(c p) d -> p c d", p=PT)
                                         ).then_inc(w_in[j], 16)
                            sp.dma_start(b2[:, j, :], st.dram["L0_ffn_b2"][bass.ds(e, 1), :]).then_inc(w_in[j], 16)
                        if is_live(i, j, 1):
                            for k in (2 * j - 2, 2 * j - 1):
                                ahead.load(sp, *batch_ahead(i, k + 4))
                steps(sp, step)

            @block.scalar
            def _(act):
                def step(i):
                    for j in range(EB):
                        e = EB * i + j
                        if is_live(i, j, HL):
                            m, c = e - HL, (j - HL) % EB
                            act.wait_ge(h_done, m + 1)
                            wait_count(act, y_done, m - EB + 1)
                            for k in range(HC):
                                a = nc.scalar.activation(hT[:, c, k, :], psum[:, 1 + c % 2, CAP * k:CAP * (k + 1)],
                                                         ACT.Relu, bias=b1T[:, bass.ds(m * HC + k, 1)])
                            a.then_inc(hT_kept, 1)
                        for k in (2 * j - 1, 2 * j):
                            if live(i, k, 0, 2 * NE, 2 * EB):
                                ahead.keep(act, *batch_ahead(i, k))
                steps(act, step)

            @block.tensor
            def _(pe):
                def step(i):
                    for j in range(EB):
                        e = EB * i + j
                        if is_live(i, j, 0):
                            pe.wait_ge(row_in[j], 16 * (i + 1))
                            wait_count(pe, rowsT_kept, e)
                            nc.tensor.transpose(psum[:, 0, 0:CAP], rows[:, j, :], st.ident).then_inc(turned, 1)
                        if is_live(i, j, HL):
                            m, c = e - HL, (j - HL) % EB
                            pe.wait_ge(rowsT_kept, m + 1)
                            pe.wait_ge(w_in[c], 48 * (i + (0 if j >= HL else -1) + 1))
                            wait_count(pe, hT_kept, m - 1)
                            for k in range(HC):
                                mm = nc.tensor.matmul(psum[:, 1 + c % 2, CAP * k:CAP * (k + 1)],
                                                      w1[:, c, PT * k:PT * (k + 1)], rowsT[:, c, :],
                                                      start=True, stop=True)
                            mm.then_inc(h_done, 1)
                        if is_live(i, j, YL):
                            m, c = e - YL, (j - YL) % EB
                            pe.wait_ge(hT_kept, m + 1)
                            wait_count(pe, y_kept, m)
                            for k in range(HC):
                                nc.tensor.matmul(psum[:, 3, 0:D], hT[:, c, k, :], w2[:, c, k, :],
                                                 start=(k == 0), stop=False)
                            nc.tensor.matmul(psum[:, 3, 0:D], cst["ones"][0:1, :], b2[:, c, :],
                                             start=False, stop=True).then_inc(y_done, 1)
                        if is_live(i, j, 0):
                            for k in (2 * j, 2 * j + 1):
                                ahead.project(pe, *batch_ahead(i, k))
                steps(pe, step)

            @block.vector
            def _(dve):
                def step(i):
                    for j in range(EB):
                        e = EB * i + j
                        if is_live(i, j, 0):
                            dve.wait_ge(turned, e + 1)
                            wait_count(dve, h_done, e - EB + 1)
                            nc.vector.tensor_copy(rowsT[:, j, :], psum[:, 0, 0:CAP]).then_inc(rowsT_kept, 1)
                        if is_live(i, j, YL):
                            m, c = e - YL, (j - YL) % EB
                            dve.wait_ge(y_done, m + 1)
                            wait_count(dve, y_stored[c], 16 * (i + (0 if j >= YL else -1)))
                            nc.vector.tensor_copy(y[:, c, :], psum[:, 3, 0:D]).then_inc(y_kept, 1)
                steps(dve, step)

            @block.gpsimd
            def _(pool):
                def step(i):
                    for j in range(EB):
                        if is_live(i, j, YL):
                            m, c = EB * i + j - YL, (j - YL) % EB
                            pool.wait_ge(y_kept, m + 1)
                            pool.dma_start(answers[bass.ds(m * CAP, CAP), :], y[:, c, :]).then_inc(y_stored[c], 16)
                steps(pool, step)
                for c in range(2):
                    pool.wait_ge(y_stored[c], 16 * NE // EB)

        with nc.Block() as block:

            @block.sync
            def _(sp):
                once.load(sp)
                ahead.load_ahead(sp, GATHER_AHEAD)
                once.store(sp)

            @block.scalar
            def _(act):
                ahead.run(act, ahead.keep, GATHER_AHEAD)

            @block.tensor
            def _(pe):
                ahead.run(pe, ahead.project, (GATHER_AHEAD[0], GATHER_AHEAD[0] + 1))
                once.products(pe)
                ahead.run(pe, ahead.project, (GATHER_AHEAD[0] + 1, GATHER_AHEAD[1]))

            @block.gpsimd
            def _(pool):
                for t in range(NT):
                    nc.gpsimd.indirect_dma_start(
                        out=back[:, t, :], out_offset=None, in_=answers,
                        in_offset=bass.IndirectOffsetOnAxis(ap=src[:, t:t + 1], axis=0)
                        ).then_inc(gathered[2 * t // NT], 16)
                for half in range(2):
                    pool.wait_ge(gathered[half], 16 * NT // 2)

            @block.vector
            def _(dve):
                once.vector(dve)
                for half in range(2):
                    dve.wait_ge(gathered[half], 16 * NT // 2)
                    tiles = range(NT // 2 * half, NT // 2 * (half + 1))
                    for t in tiles:
                        nc.vector.scalar_tensor_tensor(x[:, t, :], back[:, t, :], r[:, 7, t:t + 1], x[:, t, :],
                                                       ALU.mult, ALU.add).then_inc(updated, 1)
                    for t in tiles:
                        dve.wait_ge(updated, t + 1)
                        nc.vector.bn_stats(st.stats[:, t, :], x[:, t, :])
        clear_counts(nc, sems)


class ConvAttentionOnce:

    def __init__(self, nc, st, ctx):
        self.nc, self.st = nc, st
        self.mask_dram = nc.dram_tensor("mask_dram", (B, S), F32).ap()
        self.vleft_dram = nc.dram_tensor("vleft_dram", (B, HG, D), F32).ap()
        kept = lambda n, shape, dt=F32: ctx.enter_context(nc.sbuf_tensor("d_" + n, shape, dt))
        self.out_bias = kept("out_bias", [1, D])

    def take_room(self, ctx):
        nc = self.nc
        sb = lambda n, shape, dt=F32: ctx.enter_context(nc.sbuf_tensor("d_" + n, shape, dt))
        self.last_in, self.lastT = sb("last_in", [B, 2, D]), sb("lastT", [PT, 2, B])
        self.vleft = sb("vleft", [B, HG, D])
        self.mask = sb("mask", [B, S])
        self.sems = [ctx.enter_context(nc.semaphore("d_once_" + n)) for n in (
            "pre_in", "mask_scaled", "mask_stored", "last_turned", "last_kept", "vleft_done", "vleft_kept",
            "vleft_stored")]
        (self.pre_in, self.mask_scaled, self.mask_stored, self.last_turned, self.last_kept, self.vleft_done,
         self.vleft_kept, self.vleft_stored) = self.sems

    def load(self, sp):
        sp.dma_start(self.last_in[:], self.st.ctx[:, S - 2:S, :]).then_inc(self.pre_in, 16)
        sp.dma_start(self.mask[:], self.st.dram["mask_Bx1x1xS2_ff0"].rearrange("b o u s -> (b o u) s")
                     ).then_inc(self.pre_in, 16)

    def store(self, sp):
        sp.wait_ge(self.mask_scaled, 1)
        sp.dma_start(self.mask_dram, self.mask[:]).then_inc(self.mask_stored, 16)
        sp.wait_ge(self.vleft_kept, 1)
        sp.dma_start(self.vleft_dram, self.vleft[:]).then_inc(self.vleft_stored, 16)

    def finish(self, sp):
        sp.wait_ge(self.mask_stored, 16)
        sp.wait_ge(self.vleft_stored, 16)

    def products(self, pe):
        nc, st, psum = self.nc, self.st, self.st.psum
        pe.wait_ge(self.pre_in, 32)
        for r in range(2):
            mm = nc.tensor.transpose(psum[:, 0, B * r:B * (r + 1)], self.last_in[:, r, :], st.cst["ident"][0:B, 0:B])
        mm.then_inc(self.last_turned, 1)
        nc.tensor.matmul(psum[0:1, 2, 0:D], st.col["L1_xattn_bv"], st.w["L1_xattn_Wo"], start=True, stop=True)
        pe.wait_ge(self.last_kept, 1)
        for r in range(2):
            mm = nc.tensor.matmul(psum[0:B, 1, 0:D], self.lastT[:, r, :], st.convw[:, 2, r, :],
                                  start=(r == 0), stop=(r == 1))
        mm.then_inc(self.vleft_done, 1)

    def vector(self, dve):
        nc, st, psum, cst = self.nc, self.st, self.st.psum, self.st.cst
        dve.wait_ge(self.pre_in, 32)
        nc.vector.tensor_scalar(self.mask[:], self.mask[:], -1e9, None, ALU.mult).then_inc(self.mask_scaled, 1)
        dve.wait_ge(self.last_turned, 1)
        nc.vector.tensor_copy(self.lastT[:], psum[:, 0, 0:2 * B].rearrange("p (r b) -> p r b", r=2)
                              ).then_inc(self.last_kept, 1)
        dve.wait_ge(self.vleft_done, 1)
        nc.vector.tensor_tensor(self.vleft[:], psum[0:B, 1, 0:D].unsqueeze(1).broadcast_to([B, HG, D]),
                                cst["own_group"][0:B, :].rearrange("p (g d) -> p g d", g=HG), ALU.mult
                                ).then_inc(self.vleft_kept, 1)
        nc.vector.tensor_tensor(self.out_bias[:], psum[0:1, 2, 0:D], st.row["L1_xattn_bo"], ALU.add)


def conv_cross_attention(nc, st, once):
    psum, cst, x, qT = st.psum, st.cst, st.x, st.qT
    with ExitStack() as ctx:
        sb = lambda n, shape, dt=F32: ctx.enter_context(nc.sbuf_tensor("d_" + n, shape, dt))
        sems = []

        def sem(n):
            sems.append(ctx.enter_context(nc.semaphore("d_" + n)))
            return sems[-1]

        out_bias, wo = once.out_bias, st.w["L1_xattn_Wo"]

        HALF = HG // 2
        vl = sb("vl", [HG, 4, D])
        mask = sb("mask_rows", [PT, 4, S])
        v = sb("v", [PT, 4, SF * D])
        qbd = sb("qbd", [PT, 2, NH, L])
        prob = sb("prob", [PT, 2, HG, S])
        ntop = sb("ntop", [PT, 2, HG])
        total = sb("total", [PT, 2, HG])
        inv = sb("inv", [PT, 2, HG])
        invrep = sb("invrep", [PT, 2, HG, 32])
        pT = sb("pT", [PT, 2, 2, HALF, SF, PT])
        plT = sb("plT", [HG, 2, PT])
        scale = sb("scale", [PT, 2, PT])
        attn = sb("attn", [PT, HG, TPB, L])
        pairs = sb("pairs", [PT, 2, TPB * L])
        heads = sb("heads", [PT, TPB * L])
        load_done = [sem(f"load_done{k}") for k in range(4)]
        (qbd_done, inv_done, invrep_done, turned_l, plT_kept, pv_done, scale_kept, attn_done, pairs_done, heads_done,
         o_done, x_done, x_seen) = map(sem, ("qbd_done", "inv_done", "invrep_done", "turned_l", "plT_kept", "pv_done", "scale_kept",
                       "attn_done", "pairs_done", "heads_done", "o_done", "x_done", "x_seen"))
        s_done, masked_done, ntop_done, exp_done, turned, pT_kept = (
            [sem(f"{n}{a}") for a in range(2)] for n in ("s_done", "masked_done", "ntop_done", "exp_done", "turned", "pT_kept"))
        T_BANK, A_BANK, O_BANK = 4, 6, 7
        LEFT_AT = PT
        TL, PV, NORM = 1, 2, 3
        steps = lambda eng, step: tile_steps(eng, step, 2, 1)

        with nc.Block() as block:

            @block.sync
            def _(sp):
                def step(i):
                    for j in range(TPB):
                        n = TPB * i + j
                        if live(i, j, 0):
                            wait_count(sp, pv_done, n - 3)
                            sp.dma_start(v[:, j, :], st.v_dram[n]).then_inc(load_done[j], 16)
                            sp.dma_start(vl[:, j, :], once.vleft_dram[n]).then_inc(load_done[j], 16)
                            sp.dma_start(mask[:, j, :], once.mask_dram[bass.ds(n, 1), :].broadcast_to([PT, S])).then_inc(load_done[j], 16)
                steps(sp, step)

            @block.gpsimd
            def _(pool):
                def step(i):
                    for j in range(TPB):
                        n = TPB * i + j
                        if live(i, j, 0):
                            wait_count(pool, s_done[1], n - 1)
                            nc.gpsimd.tensor_tensor(
                                qbd[:, j % 2], qT[:, bass.ds(n * L, L)].unsqueeze(1).broadcast_to([PT, NH, L]),
                                cst["head16"].unsqueeze(2).broadcast_to([PT, NH, L]), ALU.mult).then_inc(qbd_done, 1)
                        if live(i, j, PV):
                            m, c = n - PV, (j - PV) % 2
                            pool.wait_ge(inv_done, m + 1)
                            wait_count(pool, pv_done, m - 1)
                            nc.gpsimd.tensor_tensor(invrep[:, c], inv[:, c].unsqueeze(2).broadcast_to([PT, HG, 32]),
                                                    cst["own_head"].rearrange("p (g r) -> p g r", g=HG), ALU.mult
                                                    ).then_inc(invrep_done, 1)
                steps(pool, step)

            @block.tensor
            def _(pe):
                def step(i):
                    for j in range(TPB):
                        n = TPB * i + j
                        if live(i, j, 0):
                            pe.wait_ge(load_done[j], 48 * (i + 1))
                            pe.wait_ge(qbd_done, n + 1)
                            keys = st.ctx_all[:, bass.ds(n, 1), 0:S].rearrange("p o s -> p (o s)")
                            for a in range(2):
                                wait_count(pe, masked_done[a], n)
                                for g in range(HALF * a, HALF * (a + 1)):
                                    mm = nc.tensor.matmul(
                                        psum[:, g, 0:S], qbd[:, j % 2, HG * g:HG * (g + 1), :].rearrange(
                                            "p h l -> p (h l)"), keys, start=True, stop=True)
                                mm.then_inc(s_done[a], 1)
                        if j == 3 and live_tile(i, 1):
                            t = i - 1
                            pe.wait_ge(heads_done, t + 1)
                            wait_count(pe, plT_kept, n - TL if live(i, j, TL) else B)
                            o = psum[:, O_BANK, 0:D]
                            nc.tensor.matmul(o, heads[:], wo, start=True, stop=False)
                            nc.tensor.matmul(o, cst["ones"][0:1, :], out_bias[:], start=False, stop=True
                                             ).then_inc(o_done, 1)
                        if live(i, j, TL):
                            m, c = n - TL, (j - TL) % 2
                            for a in range(2):
                                pe.wait_ge(exp_done[a], m + 1)
                                wait_count(pe, pT_kept[a], m)
                                for g in range(HALF):
                                    for t in range(SF):
                                        at = PT * (SF * g + t)
                                        mm = nc.tensor.transpose(psum[:, T_BANK + a, at:at + PT],
                                                                 prob[:, c, HALF * a + g, PT * t:PT * (t + 1)],
                                                                 st.ident)
                                mm.then_inc(turned[a], 1)
                        if live(i, j, PV):
                            m, c = n - PV, (j - PV) % 2
                            at = psum[:, A_BANK, 256 * c:256 * c + PT]
                            for a in range(2):
                                pe.wait_ge(pT_kept[a], m + 1)
                            pe.wait_ge(plT_kept, m + 1)
                            if c == 0:
                                wait_count(pe, attn_done, (TPB * i + j - PV) // 2 if isinstance(i, int)
                                           else 2 * i + (j - PV) // 2)
                            nc.tensor.matmul(at, vl[:, (j - PV) % 4, :], plT[:, c, :], start=True, stop=False)
                            for t in range(SF):
                                for g in range(HG):
                                    nc.tensor.matmul(
                                        at[32 * g:32 * (g + 1), :],
                                        v[:, (j - PV) % 4, D * t + 32 * g:D * t + 32 * (g + 1)],
                                        pT[:, c, g // HALF, g % HALF, t, :],
                                        start=False, stop=(t == SF - 1), tile_position=(0, 32 * g))
                            pe.wait_ge(invrep_done, m + 1)
                            nc.tensor.matmul(psum[:, A_BANK, 256 * c + PT:256 * (c + 1)],
                                             invrep[:, c].rearrange("p g r -> p (g r)"), st.ident,
                                             start=True, stop=True).then_inc(pv_done, 1)
                        if live(i, j, TL):
                            m, c = n - TL, (j - TL) % 2
                            wait_count(pe, plT_kept, m)
                            if j == 3:
                                wait_count(pe, x_done, i)
                            nc.tensor.transpose(psum[0:HG, O_BANK, LEFT_AT:LEFT_AT + PT], prob[:, c, :, S - 1],
                                                st.ident).then_inc(turned_l, 1)
                steps(pe, step)

            @block.vector
            def _(dve):
                def step(i):
                    for j in range(TPB):
                        n = TPB * i + j
                        for a in range(2):
                            if live(i, j, 0):
                                if a == 0:
                                    dve.wait_ge(load_done[j], 48 * (i + 1))
                                    wait_count(dve, turned_l, n - 1)
                                half = slice(HALF * a, HALF * (a + 1))
                                dve.wait_ge(s_done[a], n + 1)
                                nc.vector.tensor_tensor(prob[:, j % 2, half], psum[:, half, 0:S], mask[
                                    :, j, :].unsqueeze(1).broadcast_to([PT, HALF, S]), ALU.add
                                    ).then_inc(masked_done[a], 1)
                                dve.wait_ge(masked_done[a], n + 1)
                                wait_count(dve, exp_done[a], n - 1)
                                nc.vector.tensor_reduce(ntop[:, j % 2, half], prob[:, j % 2, half], AX_X, ALU.max,
                                                        negate=True).then_inc(ntop_done[a], 1)
                            if a == 0 and j == 3 and live_tile(i, 1):
                                dve.wait_ge(o_done, i)
                                xt = x[:, bass.ds(i - 1, 1), :].rearrange("p o d -> p (o d)")
                                nc.vector.tensor_tensor(xt, xt, psum[:, O_BANK, 0:D], ALU.add).then_inc(x_done, 1)
                            if a == 0 and j % 2 == 0 and live(i, j, NORM):
                                m = n - NORM
                                pair = (j - NORM) // 2 % 2
                                count = m // 2 if isinstance(m, int) else 2 * i + (j - NORM) // 2
                                dve.wait_ge(scale_kept, count + 1)
                                if pair == 0:
                                    wait_count(dve, pairs_done, i - 1 if j == 0 else i)
                                both = psum[:, A_BANK, :].rearrange("p (c w) -> p c w", c=2)[:, :, 0:PT]
                                nc.vector.tensor_tensor(
                                    attn[:, :, 2 * pair:2 * pair + 2, :].rearrange("p h b l -> p b h l"),
                                    both.rearrange("p b (h l) -> p b h l", h=HG),
                                    scale[:].rearrange("p b (h l) -> p b h l", h=HG), ALU.mult).then_inc(attn_done, 1)
                        if j == 2 and live_tile(i, 1):
                            dve.wait_ge(attn_done, 2 * i)
                            nc.vector.tensor_tensor(pairs[:], attn[:, 0:2].rearrange("p h b l -> p h (b l)"),
                                                    attn[:, 2:4].rearrange("p h b l -> p h (b l)"), ALU.add
                                                    ).then_inc(pairs_done, 1)
                            dve.wait_ge(pairs_done, i)
                            wait_count(dve, o_done, i - 1)
                            nc.vector.tensor_tensor(heads[:], pairs[:, 0], pairs[:, 1], ALU.add
                                                    ).then_inc(heads_done, 1)
                        if j == 3 and live_tile(i, 1):
                            token_stats(nc, st, dve, x_done, i, x_seen, i - 1)
                        if live(i, j, TL):
                            m, c = n - TL, (j - TL) % 2
                            for a in range(2):
                                dve.wait_ge(exp_done[a], m + 1)
                            wait_count(dve, invrep_done, m - 1)
                            nc.vector.reciprocal(inv[:, c], total[:, c]).then_inc(inv_done, 1)
                            dve.wait_ge(turned[1], m + 1)
                            wait_count(dve, pv_done, m - 1)
                            nc.vector.tensor_copy(pT[:, c, 1].rearrange("p g t k -> p (g t k)"),
                                                  psum[:, T_BANK + 1, :]).then_inc(pT_kept[1], 1)
                steps(dve, step)

            @block.scalar
            def _(act):
                nc.scalar.preload_act_table(ACT.Exp)

                def step(i):
                    for j in range(TPB):
                        n = TPB * i + j
                        if j % 2 == 0 and live(i, j, NORM):
                            m = n - NORM
                            count = m // 2 if isinstance(m, int) else 2 * i + (j - NORM) // 2
                            act.wait_ge(pv_done, m + 1)
                            wait_count(act, attn_done, count)
                            both = psum[:, A_BANK, :].rearrange("p (c w) -> p c w", c=2)[:, :, PT:2 * PT]
                            nc.scalar.activation(scale[:], both, ACT.Copy).then_inc(scale_kept, 1)
                        for a in range(2):
                            if live(i, j, 0):
                                if a == 0:
                                    wait_count(act, inv_done, n - 1)
                                act.wait_ge(ntop_done[a], n + 1)
                                for g in range(HALF * a, HALF * (a + 1)):
                                    ins = nc.scalar.activation(prob[:, j % 2, g, :], prob[:, j % 2, g, :], ACT.Exp,
                                                               bias=ntop[:, j % 2, g:g + 1],
                                                               accum_out=total[:, j % 2, g:g + 1])
                                ins.then_inc(exp_done[a], 1)
                            if a == 0 and live(i, j, TL):
                                m, c = n - TL, (j - TL) % 2
                                act.wait_ge(turned[0], m + 1)
                                wait_count(act, pv_done, m - 1)
                                nc.scalar.activation(pT[:, c, 0].rearrange("p g t k -> p (g t k)"),
                                                     psum[:, T_BANK, :], ACT.Copy).then_inc(pT_kept[0], 1)
                        if live(i, j, TL):
                            m, c = n - TL, (j - TL) % 2
                            act.wait_ge(turned_l, m + 1)
                            nc.scalar.activation(plT[:, c, :], psum[0:HG, O_BANK, LEFT_AT:LEFT_AT + PT], ACT.Copy
                                                 ).then_inc(plT_kept, 1)
                steps(act, step)
        clear_counts(nc, sems)


def rope_self_attention(nc, st):
    psum, cst, x = st.psum, st.cst, st.x
    q, rk = st.qT, st.xn_flat
    with ExitStack() as ctx:
        sb = lambda n, shape, dt=F32: ctx.enter_context(nc.sbuf_tensor("e_" + n, shape, dt))
        sems = []

        def sem(n):
            sems.append(ctx.enter_context(nc.semaphore("e_" + n)))
            return sems[-1]

        raw = sb("raw", [PT, 2, TOK])
        out_bias = sb("out_bias", [1, D])
        wq, wk, wv, wo = (st.w["L1_attn_" + n] for n in ("wqT", "wkT", "wvT", "woT"))
        layer_norm(nc, st, "n4", stats_made=True, products=[([None], [wq], st.col["L1_attn_bq"], DH ** -0.5, raw[:, 0]),
                                           ([None], [wk], st.col["L1_attn_bk"], 1.0, raw[:, 1])])

        by_batch = lambda a: a.rearrange("p (b l) -> p b l", l=L)
        over_b = lambda a, n: a.unsqueeze(1).broadcast_to([PT, n, L])
        rotated, sin_done, cos_done, bias_done = map(sem, ("rotated", "sin_done", "cos_done", "bias_done"))
        sin_part = sb("sin_part", [PT, 2, 512])
        with nc.Block() as block:

            @block.tensor
            def _(pe):
                for k in range(8):
                    wait_count(pe, sin_done, k - 3)
                    nc.tensor.matmul(psum[:, k % 4, :], cst["rotate"], raw[:, k // 4, 512 * (k % 4):512 * (k % 4 + 1)],
                                     start=True, stop=True).then_inc(rotated, 1)
                nc.tensor.matmul(psum[0:1, 4, 0:D], st.col["L1_attn_bv"], wo, start=True, stop=True
                                 ).then_inc(bias_done, 1)

            @block.gpsimd
            def _(pool):
                for k, to in enumerate((q[:], rk)):
                    nc.gpsimd.tensor_tensor(by_batch(to), by_batch(raw[:, k]), over_b(cst["cos"], B), ALU.mult
                                            ).then_inc(cos_done, 1)

            @block.vector
            def _(dve):
                for k in range(8):
                    to = (q[:], rk)[k // 4][:, 512 * (k % 4):512 * (k % 4 + 1)]
                    dve.wait_ge(rotated, k + 1)
                    nc.vector.tensor_tensor(by_batch(sin_part[:, k % 2]), by_batch(psum[:, k % 4, :]),
                                            over_b(cst["sin"], 16), ALU.mult).then_inc(sin_done, 1)
                    dve.wait_ge(sin_done, k + 1)
                    dve.wait_ge(cos_done, k // 4 + 1)
                    nc.vector.tensor_tensor(to, to, sin_part[:, k % 2], ALU.add)
                dve.wait_ge(bias_done, 1)
                nc.vector.tensor_tensor(out_bias[:], psum[0:1, 4, 0:D], st.row["L1_attn_bo"], ALU.add)

        xs = sb("xs", [PT, 2, PT])
        qs = sb("qs", [PT, 2, PT])
        kbd = sb("kbd", [PT, 2, TPB, NH, L])
        v = sb("v", [PT, 2, D])
        prob = sb("prob", [PT, 2, NH, L])
        pT = sb("pT", [PT, 2, NH * L])
        top = sb("top", [PT, NH])
        total = sb("total", [PT, NH])
        inv = sb("inv", [PT, NH])
        attn = sb("attn", [PT, HG, TPB, L])
        pairs = sb("pairs", [PT, 2, TPB * L])
        heads = sb("heads", [PT, TPB * L])
        (xs_kept, qs_kept, kbd_done, v_done, v_kept, s_done, top_done, sub_done, exp_done, total_done, inv_done,
         norm_done, pT_done, pv_done, attn_kept, o_done, x_done) = map(sem, (
             "xs_kept", "qs_kept", "kbd_done", "v_done", "v_kept", "s_done", "top_done", "sub_done", "exp_done",
             "total_done", "inv_done", "norm_done", "pT_done", "pv_done", "attn_kept", "o_done", "x_done"))
        pv_open, x_seen, pairs_done, heads_done = map(sem, ("pv_open", "x_seen", "pairs_done", "heads_done"))
        V_BANK, A_BANK, O_BANK = 2, 3, 7
        SC, NORM, PV, OUT = 1, 2, 3, 4
        is_live = lambda i, j, lag: live(i, j, lag, NT, 2)
        steps = lambda eng, step: tile_steps(eng, step, 2, 2, NT // 2)
        with nc.Block() as block:

            @block.gpsimd
            def _(pool):
                def step(i):
                    for j in range(2):
                        if is_live(i, j, 0):
                            n = 2 * i + j
                            wait_count(pool, s_done, n - 1)
                            for b in range(TPB):
                                ins = nc.gpsimd.tensor_tensor(
                                    kbd[:, j, b], rk[:, bass.ds(n * PT + b * L, L)].unsqueeze(1).broadcast_to(
                                        [PT, NH, L]),
                                    cst["head16"].unsqueeze(2).broadcast_to([PT, NH, L]), ALU.mult)
                            ins.then_inc(kbd_done, 1)
                steps(pool, step)

            @block.tensor
            def _(pe):
                def step(i):
                    for j in range(2):
                        n = 2 * i + j
                        if is_live(i, j, SC):
                            m, c = n - SC, (j - SC) % 2
                            pe.wait_ge(xs_kept, m + 1)
                            wait_count(pe, v_kept, m)
                            nc.tensor.matmul(psum[:, V_BANK, 0:D], xs[:, c], wv, start=True, stop=True
                                             ).then_inc(v_done, 1)
                            pe.wait_ge(kbd_done, m + 1)
                            pe.wait_ge(qs_kept, m + 1)
                            wait_count(pe, sub_done, m - 1)
                            for b in range(TPB):
                                mm = nc.tensor.matmul(psum[32 * b:32 * (b + 1), c, :], qs[:, c, L * b:L * (b + 1)],
                                                      kbd[:, c, b], start=True, stop=True, tile_position=(0, 32 * b))
                            mm.then_inc(s_done, 1)
                        if is_live(i, j, PV):
                            m, c = n - PV, (j - PV) % 2
                            pe.wait_ge(pT_done, m + 1)
                            pe.wait_ge(v_kept, m + 1)
                            wait_count(pe, attn_kept, m)
                            pe.sem_inc(pv_open)
                            for g in range(HG):
                                for b in range(TPB):
                                    mm = nc.tensor.matmul(
                                        psum[32 * g:32 * (g + 1), A_BANK + b, 0:PT],
                                        v[32 * b:32 * (b + 1), c, 32 * g:32 * (g + 1)],
                                        pT[32 * b:32 * (b + 1), c, PT * g:PT * (g + 1)],
                                        start=True, stop=True, tile_position=(32 * b, 32 * g))
                            mm.then_inc(pv_done, 1)
                        if is_live(i, j, OUT):
                            m = n - OUT
                            pe.wait_ge(heads_done, m + 1)
                            wait_count(pe, x_done, m)
                            o = psum[:, O_BANK, 0:D]
                            nc.tensor.matmul(o, heads[:], wo, start=True, stop=False)
                            nc.tensor.matmul(o, cst["ones"][0:1, :], out_bias[:], start=False, stop=True
                                             ).then_inc(o_done, 1)
                steps(pe, step)

            @block.vector
            def _(dve):
                over_k = lambda a: a.unsqueeze(2).broadcast_to([PT, NH, L])

                def step(i):
                    for j in range(2):
                        n = 2 * i + j
                        if is_live(i, j, SC):
                            m, c = n - SC, (j - SC) % 2
                            sc = psum[:, c, :].rearrange("p (h k) -> p h k", k=L)
                            dve.wait_ge(s_done, m + 1)
                            nc.vector.tensor_reduce(top[:], sc, AX_X, ALU.max).then_inc(top_done, 1)
                            dve.wait_ge(top_done, m + 1)
                            nc.vector.tensor_tensor(prob[:, c], sc, over_k(top[:]), ALU.subtract).then_inc(sub_done, 1)
                        if is_live(i, j, OUT):
                            m = n - OUT
                            dve.wait_ge(attn_kept, m + 1)
                            nc.vector.tensor_tensor(pairs[:], attn[:, 0:2].rearrange("p h b l -> p h (b l)"),
                                                    attn[:, 2:4].rearrange("p h b l -> p h (b l)"), ALU.add
                                                    ).then_inc(pairs_done, 1)
                            dve.wait_ge(pairs_done, m + 1)
                            wait_count(dve, o_done, m)
                            nc.vector.tensor_tensor(heads[:], pairs[:, 0], pairs[:, 1], ALU.add
                                                    ).then_inc(heads_done, 1)
                        if is_live(i, j, NORM):
                            m, c = n - NORM, (j - NORM) % 2
                            dve.wait_ge(exp_done, m + 1)
                            nc.vector.tensor_reduce(total[:], prob[:, c], AX_X, ALU.add).then_inc(total_done, 1)
                            dve.wait_ge(total_done, m + 1)
                            nc.vector.reciprocal(inv[:], total[:]).then_inc(inv_done, 1)
                            dve.wait_ge(inv_done, m + 1)
                            nc.vector.tensor_tensor(prob[:, c], prob[:, c], over_k(inv[:]), ALU.mult
                                                    ).then_inc(norm_done, 1)
                            dve.wait_ge(norm_done, m + 1)
                            wait_count(dve, pv_done, m - 1)
                            nc.vector.transpose(pT[:, c], prob[:, c].rearrange("p h k -> p (h k)")
                                                ).then_inc(pT_done, 1)
                        if is_live(i, j, OUT):
                            m = n - OUT
                            dve.wait_ge(o_done, m + 1)
                            xt = x[:, bass.ds(m, 1), :].rearrange("p o d -> p (o d)")
                            nc.vector.tensor_tensor(xt, xt, psum[:, O_BANK, 0:D], ALU.add).then_inc(x_done, 1)
                            token_stats(nc, st, dve, x_done, m + 1, x_seen, m)
                steps(dve, step)

            @block.scalar
            def _(act):
                nc.scalar.preload_act_table(ACT.Exp)

                def step(i):
                    for j in range(2):
                        n = 2 * i + j
                        if is_live(i, j, 0):
                            wait_count(act, v_done, n - 1)
                            nc.scalar.activation(xs[:, j], st.xnT_flat[:, bass.ds(n * PT, PT)], ACT.Copy
                                                 ).then_inc(xs_kept, 1)
                            wait_count(act, s_done, n - 1)
                            nc.scalar.activation(qs[:, j], q[:, bass.ds(n * PT, PT)], ACT.Copy).then_inc(qs_kept, 1)
                        if is_live(i, j, SC):
                            m, c = n - SC, (j - SC) % 2
                            act.wait_ge(sub_done, m + 1)
                            nc.scalar.activation(prob[:, c], prob[:, c], ACT.Exp).then_inc(exp_done, 1)
                            act.wait_ge(v_done, m + 1)
                            wait_count(act, pv_done, m - 1)
                            nc.scalar.activation(v[:, c], psum[:, V_BANK, 0:D], ACT.Copy).then_inc(v_kept, 1)
                        if is_live(i, j, PV):
                            m = n - PV
                            act.wait_ge(pv_done, m + 1)
                            wait_count(act, pairs_done, m)
                            for h in range(HG):
                                ins = nc.scalar.activation(attn[:, h], psum[:, A_BANK:A_BANK + TPB, L * h:L * (h + 1)],
                                                           ACT.Copy, scale=cst["head4"][:, h:h + 1])
                            ins.then_inc(attn_kept, 1)
                steps(act, step)
        clear_counts(nc, sems)


def switch_head_ffn(nc, st):
    psum, cst, x = st.psum, st.cst, st.x
    with ExitStack() as ctx:
        sb = lambda n, shape, dt=F32: ctx.enter_context(nc.sbuf_tensor("f_" + n, shape, dt))
        sems = []

        def sem(n):
            sems.append(ctx.enter_context(nc.semaphore("f_" + n)))
            return sems[-1]

        HE = FH * FE
        SCALE = FP ** -0.5
        qw = st.qT[:, 0:FH * FP]
        kw = st.qT[:, FH * FP:2 * FH * FP]
        CHUNKS = 2 * FH
        w_hi = sb("w_hi", [PT, CHUNKS, FE * D], F32R)
        w_lo = sb("w_lo", [PT, CHUNKS, FE * D], F32R)
        whole = [a[:, 0:FE * D] for a in st.spare_weights]
        sel, rs = st.sel, st.rs
        gate = sb("gate", [PT, 2, 2 * HE])
        w_in = sem("w_in")
        chunk_in = [sem(f"chunk_in{k}") for k in range(2)]
        hi_done, lo_done = sem("hi_done"), sem("lo_done")

        def load_chunk(sp, c):
            name = "L1_ffn_v_w" if c < FH else "L1_ffn_o_w"
            of_head = slice(FE * (c % FH), FE * (c % FH + 1))
            sp.dma_start(whole[c % 2].rearrange("p (e q) -> p e q", e=FE),
                         st.dram[name][of_head].rearrange("e p q -> p e q")).then_inc(chunk_in[c % 2], 16)

        logits_done = sem("logits_done")
        routing = st.xn_flat
        LOGIT_BANK = 2

        def load_weights(sp):
            for c in range(2):
                load_chunk(sp, c)
            sp.dma_start(qw, st.dram["L1_ffn_q_wT"]).then_inc(w_in, 16)
            sp.dma_start(kw, st.dram["L1_ffn_k_wT"]).then_inc(w_in, 16)

        def logits(pe, k):
            for t in range(4 * k, 4 * (k + 1)):
                mm = nc.tensor.matmul(psum[:, LOGIT_BANK + k, PT * (t % 4):PT * (t % 4 + 1)],
                                      st.xnT_flat[:, PT * t:PT * (t + 1)], sel[:], start=True, stop=True)
            mm.then_inc(logits_done, 1)

        def probabilities(act):
            nc.scalar.preload_act_table(ACT.Sigmoid)
            for k in range(4):
                act.wait_ge(logits_done, k + 1)
                nc.scalar.activation(routing[:, 512 * k:512 * (k + 1)], psum[:, LOGIT_BANK + k, :], ACT.Sigmoid)

        layer_norm(nc, st, "n5", stats_made=True, loads=load_weights, on_group=logits, on_scalar=probabilities)

        xs_hi = sb("xs_hi", [PT, 2, PT], F32R)
        xs_lo = sb("xs_lo", [PT, 2, PT], F32R)
        qk = sb("qk", [PT, 2, 2, PT])
        pT = sb("pT", [PT, FH, L])
        pbd = sb("pbd", [PT, 2, FH, PT])
        top = sb("top", [PT, FH])
        total = sb("total", [PT, FH])
        inv = sb("inv", [PT, FH])
        scaled = sb("scaled", [PT, 2, FE, FP])
        half = st.spare_consts[:, 0:4 * FP].rearrange("p (k d) -> p k d", k=4)
        v = st.spare_consts[:, 4 * FP:8 * FP].rearrange("p (k d) -> p k d", k=4)
        prob = st.spare_consts[:, 8 * FP:8 * FP + FH * L].rearrange("p (h l) -> p h l", l=L)
        cT_hi = sb("cT_hi", [PT, 2, PT], F32R)
        cT_lo = sb("cT_lo", [PT, 2, PT], F32R)
        acc = sb("acc", [PT, 4, D])
        pair = sb("pair", [PT, 2, D])
        choice = sel[:].rearrange("p (a e) -> p a e", e=FE)
        RH = 2 * FH
        prob_of, picked = (st.spare_consts[:, 8 * FP + FH * L + RH * FE * k:8 * FP + FH * L + RH * FE * (k + 1)].rearrange(
            "p (a e) -> p a e", e=FE) for k in range(2))
        cand = sb("cand", [PT, RH, FE])
        best = sb("best", [PT, 2, RH])
        first = sb("first", [PT, RH])
        weight = sb("weight", [PT, RH])
        GATE_STEPS = 19
        GATE_PARTS = {0: (0,), 2: (1,), 3: (2,), 5: (3,), 6: (4,), 7: (5,)}
        gate_step = sem("gate_step")
        (zeroed, xs_kept, qk_done, qk_kept, s_done, top_done, sub_done, exp_done, total_done,
         inv_done, norm_done, pT_done, pbd_done, v_done, v_scaled, v_half, v_quarter, v_kept, c_done, c_kept, xs_lo_kept, c_lo_kept,
         o_done, o_weighed, pair_done, x_done) = map(sem, (
             "zeroed", "xs_kept", "qk_done", "qk_kept", "s_done", "top_done", "sub_done",
             "exp_done", "total_done", "inv_done", "norm_done", "pT_done", "pbd_done", "v_done", "v_scaled", "v_half",
             "v_quarter", "v_kept", "c_done", "c_kept", "xs_lo_kept", "c_lo_kept", "o_done", "o_weighed", "pair_done", "x_done"))
        V_BANK, O_BANK, QK_BANK, C_BANK = 0, 2, 4, 6
        S_BANK = (5, 7)
        SC, XL, VL, CL, OL = 1, 3, 8, 12, 13

        def multiply_split(out, hi, lo, chunk, f):
            cols = slice(4 * D * f, 4 * D * (f + 1))
            nc.tensor.matmul(out, lo, w_hi[:, chunk, cols], start=True, stop=False)
            nc.tensor.matmul(out, hi, w_lo[:, chunk, cols], start=False, stop=False)
            return nc.tensor.matmul(out, hi, w_hi[:, chunk, cols], start=False, stop=True)
        PER = 2 * FH
        TOTAL = NT * FH
        is_live = lambda i, k, lag: live(i, k, lag, TOTAL, PER)
        steps = lambda eng, step: tile_steps(eng, step, 1, 1, NT // 2)

        with nc.Block() as block:

            @block.sync
            def _(sp):
                for c in range(2, CHUNKS):
                    sp.wait_ge(lo_done, c - 1)
                    load_chunk(sp, c)

            @block.tensor
            def _(pe):
                def step(i):
                    for k in range(PER):
                        s = PER * i + k
                        if is_live(i, k, CL):
                            n, h = s - CL, (k - CL) % FH
                            par = (k - CL) // FH % 2
                            if h == 0:
                                pe.wait_ge(pbd_done, 4 * (2 * i + (k - CL) // FH + 1))
                            pe.wait_ge(v_kept, n + 1)
                            wait_count(pe, c_lo_kept, n)
                            nc.tensor.matmul(psum[:, C_BANK, 0:PT], v[:, (k - CL) % 4], pbd[:, par, h],
                                             start=True, stop=True).then_inc(c_done, 1)
                        if is_live(i, k, VL):
                            n, h = s - VL, (k - VL) % FH
                            if h == 0:
                                pe.wait_ge(xs_lo_kept, 2 * i + (k - VL) // FH + 1)
                            if isinstance(i, int) and i == 0:
                                pe.wait_ge(lo_done, h + 1)
                            par = (k - VL) // FH % 2
                            for f in range(2):
                                wait_count(pe, v_scaled, 2 * n + f - 1)
                                multiply_split(psum[:, V_BANK + f, :], xs_hi[:, par], xs_lo[:, par], h, f
                                               ).then_inc(v_done, 1)
                        if is_live(i, k, 0):
                            h = k % FH
                            wait_count(pe, qk_kept, s)
                            if isinstance(i, int) and i == 0 and k == 0:
                                pe.wait_ge(w_in, 32)
                            xt = st.xnT_flat[:, bass.ds((2 * i + k // FH) * PT, PT)]
                            nc.tensor.matmul(psum[:, QK_BANK, 0:PT], qw[:, FP * h:FP * (h + 1)], xt,
                                             start=True, stop=True)
                            nc.tensor.matmul(psum[:, QK_BANK, PT:2 * PT], kw[:, FP * h:FP * (h + 1)], xt,
                                             start=True, stop=True).then_inc(qk_done, 1)
                        if is_live(i, k, SC):
                            n, h = s - SC, (k - SC) % FH
                            c = (k - SC) % 2
                            par = (k - SC) // FH % 2
                            pe.wait_ge(qk_kept, n + 1)
                            if h == 0:
                                wait_count(pe, sub_done, 2 * i + (k - SC) // FH - 1)
                            for b in range(TPB):
                                mm = nc.tensor.matmul(psum[32 * b:32 * (b + 1), S_BANK[par], L * h:L * (h + 1)],
                                                      qk[:, c, 0, L * b:L * (b + 1)], qk[:, c, 1, L * b:L * (b + 1)],
                                                      start=True, stop=True, tile_position=(0, 32 * b))
                            mm.then_inc(s_done, 1)
                        if is_live(i, k, OL):
                            n, h = s - OL, (k - OL) % FH
                            if isinstance(n, int) and n < FH or not isinstance(n, int) and k < OL:
                                pe.wait_ge(lo_done, FH + h + 1)
                            pe.wait_ge(c_lo_kept, n + 1)
                            c = (k - OL) % 2
                            for f in range(2):
                                wait_count(pe, o_weighed, FE * (n - 1) + 4 * (f + 1))
                                multiply_split(psum[:, O_BANK + f, :], cT_hi[:, c], cT_lo[:, c], FH + h, f
                                               ).then_inc(o_done, 1)
                steps(pe, step)

            @block.scalar
            def _(act):
                nc.scalar.preload_act_table(ACT.Exp)

                def step(i):
                    for k in range(PER):
                        s = PER * i + k
                        if is_live(i, k, CL):
                            n = s - CL
                            act.wait_ge(c_done, n + 1)
                            wait_count(act, o_done, 2 * (n - 1))
                            nc.scalar.activation(cT_hi[:, (k - CL) % 2], psum[:, C_BANK, 0:PT], ACT.Copy
                                                 ).then_inc(c_kept, 1)
                        if is_live(i, k, VL):
                            n, h = s - VL, (k - VL) % FH
                            t = 2 * i + (k - VL) // FH
                            if h == 0:
                                act.wait_ge(gate_step, GATE_STEPS * (t + 1))
                            wait_count(act, v_half, n - 1)
                            for f in range(2):
                                act.wait_ge(v_done, 2 * n + f + 1)
                                for e in range(4 * f, 4 * (f + 1)):
                                    a = nc.scalar.activation(scaled[:, (k - VL) % 2, e, :],
                                                             psum[:, V_BANK + f, FP * (e % 4):FP * (e % 4 + 1)],
                                                             ACT.Copy, scale=gate[:, (k - VL) // FH % 2, FE * h + e:FE * h + e + 1])
                                a.then_inc(v_scaled, 1)
                        if is_live(i, k, 0):
                            act.wait_ge(qk_done, s + 1)
                            wait_count(act, s_done, s - 1)
                            nc.scalar.activation(qk[:, k % 2].rearrange("p a t -> p (a t)"),
                                                 psum[:, QK_BANK, 0:2 * PT], ACT.Copy).then_inc(qk_kept, 1)
                        if k % FH == 1 and is_live(i, k, FH + 1):
                            t = 2 * i + (k - FH - 1) // FH
                            act.wait_ge(sub_done, t + 1)
                            nc.scalar.activation(prob, prob, ACT.Exp, scale=SCALE).then_inc(exp_done, 1)
                        if k % FH == 2 and is_live(i, k, FH + 2):
                            t = 2 * i + (k - FH - 2) // FH
                            par = (k - FH - 2) // FH % 2
                            act.wait_ge(pT_done, t + 1)
                            act.wait_ge(zeroed, 1)
                            wait_count(act, c_done, FH * (t - 1))
                            for b in range(TPB):
                                nc.scalar.activation(pbd[32 * b:32 * (b + 1), par, :, L * b:L * (b + 1)],
                                                     pT[32 * b:32 * (b + 1)], ACT.Copy).then_inc(pbd_done, 1)
                        if k % FH == XL and is_live(i, k, XL):
                            t = 2 * i + k // FH
                            wait_count(act, v_done, 2 * FH * (t - 1))
                            nc.scalar.activation(xs_hi[:, k // FH], st.xnT_flat[:, bass.ds(t * PT, PT)], ACT.Copy
                                                 ).then_inc(xs_kept, 1)
                        if isinstance(i, int) and i == 0:
                            act.wait_ge(chunk_in[k % 2], 16 * (k // 2 + 1))
                            nc.scalar.activation(w_hi[:, k], whole[k % 2], ACT.Copy).then_inc(hi_done, 1)
                steps(act, step)

            @block.gpsimd
            def _(pool):
                nc.gpsimd.memset(pbd[:], 0.0).then_inc(zeroed, 1)

                def step(i):
                    for k in range(PER):
                        s = PER * i + k
                        if is_live(i, k, VL):
                            n = s - VL
                            c = (k - VL) % 2
                            pool.wait_ge(v_scaled, 2 * n + 2)
                            wait_count(pool, v_kept, n)
                            nc.gpsimd.tensor_tensor(half, scaled[:, c, 0:4, :], scaled[:, c, 4:8, :], ALU.add
                                                    ).then_inc(v_half, 1)
                            pool.wait_ge(v_half, n + 1)
                            nc.gpsimd.tensor_tensor(half[:, 0:2, :], half[:, 0:2, :], half[:, 2:4, :], ALU.add
                                                    ).then_inc(v_quarter, 1)
                            pool.wait_ge(v_quarter, n + 1)
                            wait_count(pool, c_done, n - 3)
                            nc.gpsimd.tensor_tensor(v[:, (k - VL) % 4], half[:, 0, :], half[:, 1, :], ALU.add
                                                    ).then_inc(v_kept, 1)
                steps(pool, step)

            @block.vector
            def _(dve):
                over_k = lambda a: a.unsqueeze(2).broadcast_to([PT, FH, L])
                over_e = lambda a: a.unsqueeze(2).broadcast_to([PT, RH, FE])
                rank = cst["rank8"].unsqueeze(1).broadcast_to([PT, RH, FE])

                def make_gates(t, par, part):
                    done = [GATE_STEPS * t + 3 * part + (1 if part else 0)]
                    def stepped(instruction):
                        done[0] += 1
                        instruction.then_inc(gate_step, 1)

                    def ready():
                        dve.wait_ge(gate_step, done[0])

                    if part == 0:
                        stepped(nc.vector.tensor_copy(prob_of.rearrange("p a e -> p (a e)"),
                                                      routing[:, bass.ds(t * 2 * HE, 2 * HE)]))
                        ready()
                        stepped(nc.vector.tensor_reduce(best[:, 0], prob_of, AX_X, ALU.max))
                        ready()
                        stepped(nc.vector.tensor_tensor(cand[:], prob_of, over_e(best[:, 0]), ALU.is_equal))
                        ready()
                        stepped(nc.vector.tensor_tensor(cand[:], cand[:], rank, ALU.mult))
                    elif part == 1:
                        ready()
                        stepped(nc.vector.tensor_reduce(first[:], cand[:], AX_X, ALU.max))
                        ready()
                        stepped(nc.vector.tensor_tensor(picked, cand[:], over_e(first[:]), ALU.is_equal))
                        ready()
                        stepped(nc.vector.scalar_tensor_tensor(choice, picked, -2.0, prob_of,
                                                               ALU.mult, ALU.add))
                    elif part == 2:
                        ready()
                        stepped(nc.vector.tensor_reduce(best[:, 1], choice, AX_X, ALU.max))
                        ready()
                        stepped(nc.vector.tensor_tensor(cand[:], choice, over_e(best[:, 1]), ALU.is_equal))
                        ready()
                        stepped(nc.vector.tensor_tensor(cand[:], cand[:], rank, ALU.mult))
                    elif part == 3:
                        ready()
                        stepped(nc.vector.tensor_reduce(first[:], cand[:], AX_X, ALU.max))
                        ready()
                        stepped(nc.vector.tensor_tensor(cand[:], cand[:], over_e(first[:]), ALU.is_equal))
                        ready()
                        stepped(nc.vector.tensor_tensor(picked, picked, cand[:], ALU.add))
                    elif part == 4:
                        ready()
                        stepped(nc.vector.tensor_tensor(weight[:], best[:, 0], best[:, 1], ALU.add))
                        ready()
                        stepped(nc.vector.tensor_scalar(weight[:], weight[:], 1e-9, None, ALU.max))
                        ready()
                        stepped(nc.vector.reciprocal(weight[:], weight[:]))
                    else:
                        ready()
                        stepped(nc.vector.tensor_scalar(weight[:], weight[:], rs[:, 0:1], None, ALU.mult))
                        stepped(nc.vector.tensor_tensor(picked, picked, prob_of, ALU.mult))
                        ready()
                        wait_count(dve, v_scaled, 2 * FH * (t - 1))
                        wait_count(dve, o_weighed, FE * FH * (t - 1))
                        stepped(nc.vector.tensor_tensor(gate[:, par].rearrange("p (a e) -> p a e", e=FE), picked,
                                                        over_e(weight[:]), ALU.mult))

                def step(i):
                    for k in range(PER):
                        s = PER * i + k
                        if is_live(i, k, CL):
                            n, c = s - CL, (k - CL) % 2
                            dve.wait_ge(c_kept, n + 1)
                            wait_count(dve, o_done, 2 * (n - 1))
                            nc.vector.tensor_tensor(cT_lo[:, c], psum[:, C_BANK, 0:PT], cT_hi[:, c], ALU.subtract
                                                    ).then_inc(c_lo_kept, 1)
                        if k % FH == 1 and is_live(i, k, FH + 1):
                            t = 2 * i + (k - FH - 1) // FH
                            par = (k - FH - 1) // FH % 2
                            sc = psum[:, S_BANK[par], 0:FH * L].rearrange("p (h k) -> p h k", k=L)
                            dve.wait_ge(s_done, FH * (t + 1))
                            nc.vector.tensor_reduce(top[:], sc, AX_X, ALU.max).then_inc(top_done, 1)
                            dve.wait_ge(top_done, t + 1)
                            wait_count(dve, pT_done, t)
                            nc.vector.tensor_tensor(prob, sc, over_k(top[:]), ALU.subtract).then_inc(sub_done, 1)
                        if is_live(i, k, OL):
                            n, h = s - OL, (k - OL) % FH
                            t = 2 * i + (k - OL) // FH
                            for f in range(2):
                                dve.wait_ge(o_done, 2 * n + f + 1)
                                for e in range(4 * f, 4 * (f + 1)):
                                    part = psum[:, O_BANK + f, D * (e % 4):D * (e % 4 + 1)]
                                    g = gate[:, (k - OL) // FH % 2, HE + FE * h + e:HE + FE * h + e + 1]
                                    if h == 0 and f == 0:
                                        wait_count(dve, pair_done, 3 * t)
                                        ins = nc.vector.tensor_scalar(acc[:, e], part, g, None, ALU.mult)
                                    else:
                                        dve.wait_ge(o_weighed, FE * n + e - 3)
                                        ins = nc.vector.scalar_tensor_tensor(acc[:, e % 4], part, g, acc[:, e % 4],
                                                                             ALU.mult, ALU.add)
                                    ins.then_inc(o_weighed, 1)
                            if h == FH - 1:
                                dve.wait_ge(o_weighed, FE * (n + 1))
                                wait_count(dve, x_done, t)
                                nc.vector.tensor_tensor(pair[:], acc[:, 0:2], acc[:, 2:4], ALU.add
                                                        ).then_inc(pair_done, 1)
                                dve.wait_ge(pair_done, 3 * t + 1)
                                nc.vector.tensor_tensor(pair[:, 0], pair[:, 0], pair[:, 1], ALU.add
                                                        ).then_inc(pair_done, 2)
                                dve.wait_ge(pair_done, 3 * t + 3)
                                xt = x[:, bass.ds(t, 1), :].rearrange("p o d -> p (o d)")
                                nc.vector.tensor_tensor(xt, xt, pair[:, 0], ALU.add).then_inc(x_done, 1)
                        if k % FH == 1 and is_live(i, k, FH + 1):
                            t = 2 * i + (k - FH - 1) // FH
                            dve.wait_ge(exp_done, t + 1)
                            nc.vector.tensor_reduce(total[:], prob, AX_X, ALU.add).then_inc(total_done, 1)
                            dve.wait_ge(total_done, t + 1)
                            nc.vector.reciprocal(inv[:], total[:]).then_inc(inv_done, 1)
                            dve.wait_ge(inv_done, t + 1)
                            nc.vector.tensor_tensor(prob, prob, over_k(inv[:]), ALU.mult).then_inc(norm_done, 1)
                            dve.wait_ge(norm_done, t + 1)
                            wait_count(dve, pbd_done, 4 * t)
                            nc.vector.transpose(pT[:].rearrange("p h k -> p (h k)"),
                                                prob.rearrange("p h k -> p (h k)")).then_inc(pT_done, 1)
                        if is_live(i, k, 0):
                            for part in GATE_PARTS.get(k % FH, ()):
                                make_gates(2 * i + k // FH, k // FH, part)
                        if k % FH == XL and is_live(i, k, XL):
                            t = 2 * i + k // FH
                            dve.wait_ge(xs_kept, t + 1)
                            wait_count(dve, v_done, 2 * FH * (t - 1))
                            nc.vector.tensor_tensor(xs_lo[:, k // FH], st.xnT_flat[:, bass.ds(t * PT, PT)],
                                                    xs_hi[:, k // FH], ALU.subtract).then_inc(xs_lo_kept, 1)
                        if isinstance(i, int) and i == 0:
                            dve.wait_ge(hi_done, k + 1)
                            nc.vector.tensor_tensor(w_lo[:, k], whole[k % 2], w_hi[:, k], ALU.subtract
                                                    ).then_inc(lo_done, 1)
                steps(dve, step)
        clear_counts(nc, sems)


WEIGHTS = ["L0_xattn_Wq", "L0_xattn_Wk", "L0_xattn_Wv", "L0_xattn_Wo", "L1_xattn_Wo",
           "L1_attn_wqT", "L1_attn_wkT", "L1_attn_wvT", "L1_attn_woT"]
COLUMNS = ["L0_xattn_bq", "L0_xattn_bk", "L0_xattn_bv", "L1_xattn_bq", "L1_xattn_bk", "L1_xattn_bv",
           "L1_attn_bq", "L1_attn_bk", "L1_attn_bv"]
ROWS = ["L0_xattn_bo", "L1_xattn_bo", "L1_attn_bo"]
CONV_WEIGHTS = ["L1_xattn_Wq", "L1_xattn_Wk", "L1_xattn_Wv"]


def perceiver(nc, ins, out, stop_after=6):
    with ExitStack() as ctx:
        sb = lambda n, shape, dt=F32: ctx.enter_context(nc.sbuf_tensor(n, shape, dt))
        st = State()
        st.dram = ins
        st.ctx = ins["ctx_1024"]
        st.v_dram = nc.dram_tensor("v_dram", (B, PT, SF * D), F32).ap()
        st.x = sb("x", [PT, NT, D])
        st.xn = sb("xn", [PT, NT, D])
        st.xn_flat = st.xn[:].rearrange("p t d -> p (t d)")
        st.xnT_pad = sb("xnT", [PT, B, L + 2])
        st.xnT_flat = st.xnT_pad[:].rearrange("p b l -> p (b l)")[:, 0:TOK]
        st.qT = sb("qT", [PT, TOK])
        st.wg = sb("wg", [PT, NE])
        st.bg = sb("bg", [PT, NE])
        st.b1 = sb("b1", [NE * HC, PT])
        st.sel = sb("sel", [PT, 2 * FH * FE])
        st.rs = sb("rs", [PT, 1])
        st.stats = sb("stats", [PT, NT, 6])
        st.filt = sb("filt", [PT, L])
        st.past = sb("past", [PT, L])
        st.psum = ctx.enter_context(nc.psum_tensor("psum", [PT, 8, 512], F32))
        consts = sb("consts", [PT, CONST_COLS])
        st.cst = {n: consts[:, a:b] for n, (a, b) in CONST_AT.items()}
        st.ident = st.cst["ident"]
        st.spare_consts = consts[:, CONST_AT["upto"][0]:CONST_AT["own_group"][1]]
        wall = sb("wall", [PT, len(WEIGHTS), D])
        st.w = {n: wall[:, k, :] for k, n in enumerate(WEIGHTS)}
        cols = sb("cols", [PT, len(COLUMNS)])
        st.col = {n: cols[:, k:k + 1] for k, n in enumerate(COLUMNS)}
        rows = sb("rows", [1, len(ROWS), D])
        st.row = {n: rows[:, k, :] for k, n in enumerate(ROWS)}
        st.convw = sb("convw", [PT, 3, 3, D])
        st.spare_weights = [wall[:].rearrange("p k d -> p (k d)"), st.convw[:].rearrange("p a t d -> p (a t d)")]
        st.norm_sem = lambda n: ctx.enter_context(nc.semaphore(n))
        st.scattered = ctx.enter_context(nc.semaphore("scattered"))
        st.gathered = [ctx.enter_context(nc.semaphore(f"gathered{k}")) for k in range(2)]
        st.y_stored = [ctx.enter_context(nc.semaphore(f"y_stored{k}")) for k in range(EB)]
        st.weights_in = ctx.enter_context(nc.semaphore("weights_in"))
        st.x_in = [ctx.enter_context(nc.semaphore(f"x_in{k}")) for k in range(2)]
        stored = ctx.enter_context(nc.semaphore("stored"))
        st.weights_count = 16 * 10

        def load_tokens(eng, half):
            tiles = slice(NT // 2 * half, NT // 2 * (half + 1))
            eng.dma_start(st.x[:, tiles], ins["x"].rearrange("(t b) l d -> (b l) t d", b=TPB)[:, tiles]
                          ).then_inc(st.x_in[half], 16)

        def load_on_sync(sp):
            load_tokens(sp, 0)
            sp.dma_start(consts[:], ins["consts"]).then_inc(st.weights_in, 16)
            sp.dma_start(cols[:], ins["columns"]).then_inc(st.weights_in, 16)
            sp.dma_start(st.convw[:], ins["conv_weights"]).then_inc(st.weights_in, 16)
            sp.dma_start(st.wg[:], ins["L0_ffn_Wg"]).then_inc(st.weights_in, 16)
            sp.dma_start(st.bg[:], ins["L0_ffn_bg"].rearrange("(o e) -> o e", o=1).broadcast_to([PT, NE])
                         ).then_inc(st.weights_in, 16)
            sp.dma_start(st.b1[:], ins["L0_ffn_b1"].rearrange("e (c p) -> (e c) p", p=PT)).then_inc(st.weights_in, 16)
            sp.dma_start(st.sel[:], ins["selectors"]).then_inc(st.weights_in, 16)
            sp.dma_start(st.rs[:], ins["L1_ffn_route_scale"].rearrange("(o n) -> o n", o=1).broadcast_to([PT, 1])
                         ).then_inc(st.weights_in, 16)

        def load_on_scalar(act):
            load_tokens(act, 1)
            act.dma_start(wall[:], ins["weights"]).then_inc(st.weights_in, 16)
            act.dma_start(rows[:], ins["rows"]).then_inc(st.weights_in, 16)

        st.load_on_sync, st.load_on_scalar = load_on_sync, load_on_scalar
        with ExitStack() as inner:
            st.ctx_all = inner.enter_context(nc.sbuf_tensor("ctx_all", [PT, B, S + 2], F32))
            if stop_after >= 1:
                layer_norm(nc, st, "n0", products=[([None], [st.w["L0_xattn_Wq"]], st.col["L0_xattn_bq"],
                                                    DH ** -0.5, st.qT[:])], first=True,
                           loads=st.load_on_sync)
                cross_attention_over_queries(nc, st)
            once = ConvAttentionOnce(nc, st, inner)
            with ExitStack() as slots:
                ahead = ContextProjection(nc, st, slots)
                once.take_room(slots)

                def load_first(sp):
                    for j in range(4):
                        ahead.load(sp, 0, j)

                if stop_after >= 2:
                    layer_norm(nc, st, "n1", loads=load_first)
                    long_convolution(nc, st, ahead)
                if stop_after >= 3:
                    routed_ffn(nc, st, ahead, once)
                if stop_after >= 4:
                    def wait_for_stores(sp):
                        ahead.finish(sp)
                        once.finish(sp)

                    layer_norm(nc, st, "n3", padded=True, stats_made=True, loads=wait_for_stores, products=[
                        ([0, 1, 2], [st.convw[:, 0, t, :] for t in range(3)], st.col["L1_xattn_bq"], DH ** -0.5,
                         st.qT[:])])
                    clear_counts(nc, ahead.sems + once.sems)
            if stop_after >= 4:
                conv_cross_attention(nc, st, once)
        if stop_after >= 5:
            rope_self_attention(nc, st)
        if stop_after >= 6:
            switch_head_ffn(nc, st)

        with nc.Block() as block:

            @block.sync
            def _(sp):
                sp.dma_start(out.rearrange("(t b) l d -> (b l) t d", b=TPB), st.x[:]).then_inc(stored, 16)
                sp.wait_ge(stored, 16)


_TURNED = {"L1_attn_wqT": "L1_attn_wq", "L1_attn_wkT": "L1_attn_wk", "L1_attn_wvT": "L1_attn_wv",
           "L1_attn_woT": "L1_attn_wo", "L1_ffn_q_wT": "L1_ffn_q_w", "L1_ffn_k_wT": "L1_ffn_k_w",
           "L1_ffn_sel_v_wT": "L1_ffn_sel_v_w", "L1_ffn_sel_o_wT": "L1_ffn_sel_o_w"}


def build(nc, inputs, stop_after=6):
    arrays, aps = {}, {}
    laid = {n: a for n, a in inputs.items() if n not in _TURNED.values()}
    laid.update({new: np.transpose(np.asarray(inputs[old])) for new, old in _TURNED.items()})
    laid["weights"] = np.stack([laid.pop(n) for n in WEIGHTS], axis=1)
    laid["conv_weights"] = np.stack([laid.pop(n) for n in CONV_WEIGHTS], axis=0).transpose(2, 0, 1, 3)
    laid["columns"] = np.stack([laid[n] for n in COLUMNS], axis=1)
    laid["rows"] = np.stack([laid.pop(n) for n in ROWS], axis=0)[None]
    laid["selectors"] = np.concatenate([laid.pop(n) for n in ("L1_ffn_sel_v_wT", "L1_ffn_sel_o_wT")], axis=1)
    laid["consts"] = shape_constants()
    for name, a in laid.items():
        a = np.ascontiguousarray(a)
        arrays[f"in_{name}"] = a
        aps[name] = nc.dram_tensor(f"in_{name}", a.shape, mybir.dt.from_np(a.dtype), kind="ExternalInput").ap()
    out = nc.dram_tensor("out_0", (B, L, D), F32, kind="ExternalOutput").ap()
    perceiver(nc, aps, out, stop_after)
    return arrays


def kernel(**inputs):
    import concourse.bacc as _bacc
    from concourse.bass_utils import run_bass_kernel_spmd as _run

    nc = _bacc.Bacc("TRN2", target_bir_lowering=False, num_devices=1)
    arrays = build(nc, inputs)
    return _run(nc, [arrays], core_ids=[0]).results[0]["out_0"]
```
